# Optimizing a Trainium2 kernel written in Bass

```python
import numpy as np
import jax
import jax.numpy as jnp

def _softmax(x, axis=-1):
    return jax.nn.softmax(x, axis=axis)

def _gelu(x):
    return jax.nn.gelu(x, approximate=True)

def _silu(x):
    return jax.nn.silu(x)

def _sigmoid(x):
    return jax.nn.sigmoid(x)

def _layernorm(x, axis=-1, eps=1e-05):
    m = jnp.mean(x, axis=axis, keepdims=True)
    v = jnp.var(x, axis=axis, keepdims=True)
    return (x - m) / jnp.sqrt(v + eps)

def _scatter_add(tgt, idx, src, axis=0):
    return tgt.at[idx].add(src)

def _segment_sum(src, seg, n):
    return jax.ops.segment_sum(src, seg, n)
kernel_name = 'mk_hybrid_d1_jaxref_r4_600c7b'

def setup_inputs(seed: int=0):
    np.random.seed(seed)
    _w = jnp.asarray

    def _L0_attn_a_setup():
        import jax, jax.numpy as jnp
        import numpy as np
        DIM = 256
        N_HEADS = 16
        HEAD_DIM = DIM // N_HEADS
        HIDDEN = 704
        WINDOW_PER_SIDE = 128
        EPS = 1e-05
        THETA = 10000.0

        def rope_cos_sin(seqlen, head_dim):
            freqs = 1.0 / THETA ** (jnp.arange(0, head_dim, 2, dtype=jnp.float32) / head_dim)
            t = jnp.arange(seqlen, dtype=jnp.float32)
            ang = jnp.outer(t, freqs)
            return (jnp.cos(ang), jnp.sin(ang))

        def apply_rope(x, cos, sin):
            xr = x[..., 0::2]
            xi = x[..., 1::2]
            c = cos[None, :, None, :]
            s = sin[None, :, None, :]
            or_ = xr * c - xi * s
            oi_ = xr * s + xi * c
            return jnp.stack([or_, oi_], axis=-1).reshape(x.shape)

        def layernorm(x, g, b):
            mu = jnp.mean(x, axis=-1, keepdims=True)
            var = jnp.mean(jnp.square(x - mu), axis=-1, keepdims=True)
            return (x - mu) * jax.lax.rsqrt(var + EPS) * g + b

        def attention(x, wq, wk, wv, wo):
            b, s, _ = x.shape
            scale = HEAD_DIM ** (-0.5)
            q = (x @ wq).reshape(b, s, N_HEADS, HEAD_DIM)
            k = (x @ wk).reshape(b, s, N_HEADS, HEAD_DIM)
            v = (x @ wv).reshape(b, s, N_HEADS, HEAD_DIM)
            cos, sin = rope_cos_sin(s, HEAD_DIM)
            q = apply_rope(q, cos, sin)
            k = apply_rope(k, cos, sin)
            i = jnp.arange(s)[:, None]
            j = jnp.arange(s)[None, :]
            mask = (j <= i) & (i - j <= WINDOW_PER_SIDE)
            scores = jnp.einsum('bqhd,bkhd->bhqk', q, k) * scale
            scores = jnp.where(mask[None, None], scores, jnp.finfo(scores.dtype).min)
            probs = jax.nn.softmax(scores, axis=-1)
            out = jnp.einsum('bhqk,bkhd->bqhd', probs, v).reshape(b, s, -1)
            return out @ wo

        def ffn(x, w1, w2, w3):
            return jax.nn.silu(x @ w1) * (x @ w3) @ w2
        key = jax.random.key(seed)
        ks = jax.random.split(key, 9)
        sd = 0.02
        x = jax.random.normal(ks[0], (4, 512, DIM), dtype=jnp.float32)
        wq = jax.random.normal(ks[1], (DIM, DIM), dtype=jnp.float32) * sd
        wk = jax.random.normal(ks[2], (DIM, DIM), dtype=jnp.float32) * sd
        wv = jax.random.normal(ks[3], (DIM, DIM), dtype=jnp.float32) * sd
        wo = jax.random.normal(ks[4], (DIM, DIM), dtype=jnp.float32) * sd
        w1 = jax.random.normal(ks[5], (DIM, HIDDEN), dtype=jnp.float32) * sd
        w2 = jax.random.normal(ks[6], (HIDDEN, DIM), dtype=jnp.float32) * sd
        w3 = jax.random.normal(ks[7], (DIM, HIDDEN), dtype=jnp.float32) * sd
        ln1_g = jnp.ones((DIM,), jnp.float32)
        ln1_b = jnp.zeros((DIM,), jnp.float32)
        ln2_g = jnp.ones((DIM,), jnp.float32)
        ln2_b = jnp.zeros((DIM,), jnp.float32)
        return dict(x=x, wq=wq, wk=wk, wv=wv, wo=wo, w1=w1, w2=w2, w3=w3, ln1_g=ln1_g, ln1_b=ln1_b, ln2_g=ln2_g, ln2_b=ln2_b)
    _L0_attn_a_in = _L0_attn_a_setup()

    def _L0_attn_b_setup():
        import jax, jax.numpy as jnp
        import numpy as np
        D_MODEL = 256
        NUM_HEADS = 16
        HEAD_DIM = D_MODEL // NUM_HEADS
        key = jax.random.key(seed)
        ks = jax.random.split(key, 5)
        B, S = (1, 1024)
        scale = 0.02
        return {'x': jax.random.normal(ks[0], (B, S, D_MODEL), dtype=jnp.float32), 'w_q': jax.random.normal(ks[1], (D_MODEL, D_MODEL), dtype=jnp.float32) * scale, 'w_k': jax.random.normal(ks[2], (D_MODEL, D_MODEL), dtype=jnp.float32) * scale, 'w_v': jax.random.normal(ks[3], (D_MODEL, D_MODEL), dtype=jnp.float32) * scale, 'w_o': jax.random.normal(ks[4], (D_MODEL, D_MODEL), dtype=jnp.float32) * scale}
    _L0_attn_b_in = _L0_attn_b_setup()

    def _L0_ffn_setup():
        import jax, jax.numpy as jnp
        import numpy as np
        E = 8
        K = 2
        D = 256
        H = 1024
        CAP_FACTOR = 1.0
        key = jax.random.key(seed)
        ks = jax.random.split(key, 5)
        x = jax.random.normal(ks[0], (4, 512, D), jnp.float32)
        gate_w = jax.random.normal(ks[1], (E, D), jnp.float32) * 0.02
        fc1_w = jax.random.normal(ks[2], (E, H, D), jnp.float32) * 0.02
        fc1_b = jnp.zeros((E, 1, H), jnp.float32)
        fc2_w = jax.random.normal(ks[3], (E, H, D), jnp.float32) * 0.02
        fc2_b = jnp.zeros((E, 1, D), jnp.float32)
        return {'x': x, 'gate_w': gate_w, 'fc1_w': fc1_w, 'fc1_b': fc1_b, 'fc2_w': fc2_w, 'fc2_b': fc2_b}
    _L0_ffn_in = _L0_ffn_setup()
    _d = {'L0_attn_a_x': _L0_attn_a_in['x'], 'L0_attn_a_wq': _L0_attn_a_in['wq'], 'L0_attn_a_wk': _L0_attn_a_in['wk'], 'L0_attn_a_wv': _L0_attn_a_in['wv'], 'L0_attn_a_wo': _L0_attn_a_in['wo'], 'L0_attn_a_w1': _L0_attn_a_in['w1'], 'L0_attn_a_w2': _L0_attn_a_in['w2'], 'L0_attn_a_w3': _L0_attn_a_in['w3'], 'L0_attn_a_ln1_g': _L0_attn_a_in['ln1_g'], 'L0_attn_a_ln1_b': _L0_attn_a_in['ln1_b'], 'L0_attn_a_ln2_g': _L0_attn_a_in['ln2_g'], 'L0_attn_a_ln2_b': _L0_attn_a_in['ln2_b'], 'L0_attn_b_w_q': _L0_attn_b_in['w_q'], 'L0_attn_b_w_k': _L0_attn_b_in['w_k'], 'L0_attn_b_w_v': _L0_attn_b_in['w_v'], 'L0_attn_b_w_o': _L0_attn_b_in['w_o'], 'L0_ffn_gate_w': _L0_ffn_in['gate_w'], 'L0_ffn_fc1_w': _L0_ffn_in['fc1_w'], 'L0_ffn_fc1_b': _L0_ffn_in['fc1_b'], 'L0_ffn_fc2_w': _L0_ffn_in['fc2_w'], 'L0_ffn_fc2_b': _L0_ffn_in['fc2_b']}
    _x0 = _d['L0_attn_a_x']
    _d['L0_attn_a_x'] = jax.random.normal(jax.random.fold_in(jax.random.key(seed), 1), (8, 512, 256), dtype=_x0.dtype)
    del _x0
    return _d

def reference(L0_attn_a_x, L0_attn_a_wq, L0_attn_a_wk, L0_attn_a_wv, L0_attn_a_wo, L0_attn_a_w1, L0_attn_a_w2, L0_attn_a_w3, L0_attn_a_ln1_g, L0_attn_a_ln1_b, L0_attn_a_ln2_g, L0_attn_a_ln2_b, L0_attn_b_w_q, L0_attn_b_w_k, L0_attn_b_w_v, L0_attn_b_w_o, L0_ffn_gate_w, L0_ffn_fc1_w, L0_ffn_fc1_b, L0_ffn_fc2_w, L0_ffn_fc2_b):

    def _L0_attn_a_ref(x, wq, wk, wv, wo, w1, w2, w3, ln1_g, ln1_b, ln2_g, ln2_b):
        import jax, jax.numpy as jnp
        import numpy as np
        DIM = 256
        N_HEADS = 16
        HEAD_DIM = DIM // N_HEADS
        HIDDEN = 704
        WINDOW_PER_SIDE = 128
        EPS = 1e-05
        THETA = 10000.0

        def rope_cos_sin(seqlen, head_dim):
            freqs = 1.0 / THETA ** (jnp.arange(0, head_dim, 2, dtype=jnp.float32) / head_dim)
            t = jnp.arange(seqlen, dtype=jnp.float32)
            ang = jnp.outer(t, freqs)
            return (jnp.cos(ang), jnp.sin(ang))

        def apply_rope(x, cos, sin):
            xr = x[..., 0::2]
            xi = x[..., 1::2]
            c = cos[None, :, None, :]
            s = sin[None, :, None, :]
            or_ = xr * c - xi * s
            oi_ = xr * s + xi * c
            return jnp.stack([or_, oi_], axis=-1).reshape(x.shape)

        def layernorm(x, g, b):
            mu = jnp.mean(x, axis=-1, keepdims=True)
            var = jnp.mean(jnp.square(x - mu), axis=-1, keepdims=True)
            return (x - mu) * jax.lax.rsqrt(var + EPS) * g + b

        def attention(x, wq, wk, wv, wo):
            b, s, _ = x.shape
            scale = HEAD_DIM ** (-0.5)
            q = (x @ wq).reshape(b, s, N_HEADS, HEAD_DIM)
            k = (x @ wk).reshape(b, s, N_HEADS, HEAD_DIM)
            v = (x @ wv).reshape(b, s, N_HEADS, HEAD_DIM)
            cos, sin = rope_cos_sin(s, HEAD_DIM)
            q = apply_rope(q, cos, sin)
            k = apply_rope(k, cos, sin)
            i = jnp.arange(s)[:, None]
            j = jnp.arange(s)[None, :]
            mask = (j <= i) & (i - j <= WINDOW_PER_SIDE)
            scores = jnp.einsum('bqhd,bkhd->bhqk', q, k) * scale
            scores = jnp.where(mask[None, None], scores, jnp.finfo(scores.dtype).min)
            probs = jax.nn.softmax(scores, axis=-1)
            out = jnp.einsum('bhqk,bkhd->bqhd', probs, v).reshape(b, s, -1)
            return out @ wo

        def ffn(x, w1, w2, w3):
            return jax.nn.silu(x @ w1) * (x @ w3) @ w2
        h = x + attention(layernorm(x, ln1_g, ln1_b), wq, wk, wv, wo)
        out = h + ffn(layernorm(h, ln2_g, ln2_b), w1, w2, w3)
        return out

    def _L0_attn_b_ref(x, w_q, w_k, w_v, w_o):
        import jax, jax.numpy as jnp
        import numpy as np
        D_MODEL = 256
        NUM_HEADS = 16
        HEAD_DIM = D_MODEL // NUM_HEADS
        B, S, _ = x.shape
        q = x @ w_q.T
        k = x @ w_k.T
        v = x @ w_v.T
        q = q.reshape(B, S, NUM_HEADS, HEAD_DIM)
        k = k.reshape(B, S, NUM_HEADS, HEAD_DIM)
        v = v.reshape(B, S, NUM_HEADS, HEAD_DIM)
        scale = HEAD_DIM ** (-0.5)
        scores = jnp.einsum('bqhd,bkhd->bhqk', q, k) * scale
        weights = jax.nn.softmax(scores, axis=-1)
        out = jnp.einsum('bhqk,bkhd->bqhd', weights, v)
        concat = out.reshape(B, S, D_MODEL)
        return concat @ w_o.T

    def _L0_ffn_ref(x, gate_w, fc1_w, fc1_b, fc2_w, fc2_b):
        import jax, jax.numpy as jnp
        import numpy as np
        E = 8
        K = 2
        D = 256
        H = 1024
        CAP_FACTOR = 1.0
        B, S, Dm = x.shape
        xf = x.reshape(-1, Dm)
        N = xf.shape[0]
        cap = int(K * CAP_FACTOR * ((N + E - 1) // E))
        logits = xf @ gate_w.T
        scores = jax.nn.softmax(logits, axis=-1)
        topv, topi = jax.lax.top_k(scores, K)
        gates = topv / jnp.sum(topv, axis=-1, keepdims=True)
        offset = jnp.zeros((E,), jnp.int32)
        locs = []
        for j in range(K):
            mask = jax.nn.one_hot(topi[:, j], E, dtype=jnp.int32)
            loc_in = jnp.cumsum(mask, axis=0) - 1 + offset[None, :]
            locs.append(jnp.take_along_axis(loc_in, topi[:, j:j + 1], axis=1)[:, 0])
            offset = offset + mask.sum(axis=0)
        loc = jnp.stack(locs, axis=1)
        valid = loc < cap
        flat_idx = jnp.where(valid, topi * cap + loc, 0)
        w = valid.astype(xf.dtype)
        disp = jnp.zeros((E * cap, Dm), xf.dtype)
        disp = disp.at[flat_idx.reshape(-1)].add((xf[:, None, :] * w[:, :, None]).reshape(-1, Dm))
        de = disp.reshape(E, cap, Dm)
        h = jax.nn.relu(jnp.einsum('ecd,ehd->ech', de, fc1_w) + fc1_b)
        eo = jnp.einsum('ech,ehd->ecd', h, fc2_w) + fc2_b
        gathered = eo.reshape(E * cap, Dm)[flat_idx]
        out = jnp.sum(gathered * (gates * w)[:, :, None], axis=1)
        return out.reshape(B, S, Dm)
    x = L0_attn_a_x
    x = x + _L0_attn_a_ref(_layernorm(x, axis=-1), L0_attn_a_wq, L0_attn_a_wk, L0_attn_a_wv, L0_attn_a_wo, L0_attn_a_w1, L0_attn_a_w2, L0_attn_a_w3, L0_attn_a_ln1_g, L0_attn_a_ln1_b, L0_attn_a_ln2_g, L0_attn_a_ln2_b)
    x = x + _L0_ffn_ref(_layernorm(x, axis=-1), L0_ffn_gate_w, L0_ffn_fc1_w, L0_ffn_fc1_b, L0_ffn_fc2_w, L0_ffn_fc2_b)
    x = x + _L0_attn_b_ref(_layernorm(x, axis=-1), L0_attn_b_w_q, L0_attn_b_w_k, L0_attn_b_w_v, L0_attn_b_w_o)
    x = x + _L0_ffn_ref(_layernorm(x, axis=-1), L0_ffn_gate_w, L0_ffn_fc1_w, L0_ffn_fc1_b, L0_ffn_fc2_w, L0_ffn_fc2_b)
    return x

_drawn_inputs = setup_inputs


def setup_inputs(seed=0):
    import zlib

    import numpy as np

    out = dict(_drawn_inputs(seed))
    spreads = {'L0_attn_a_ln1_g': (1.0, 0.6),
     'L0_attn_a_ln1_b': (0.0, 0.8),
     'L0_attn_a_ln2_g': (1.0, 0.6),
     'L0_attn_a_ln2_b': (0.0, 0.8),
     'L0_ffn_fc1_b': (0.0, 0.587),
     'L0_ffn_fc2_b': (0.0, 0.278)}
    factors = {'L0_attn_a_wq': 8.0,
     'L0_attn_a_wk': 8.0,
     'L0_attn_a_wv': 4.883,
     'L0_attn_a_wo': 4.824,
     'L0_attn_a_w1': 3.067,
     'L0_attn_a_w2': 3.05,
     'L0_attn_a_w3': 3.047,
     'L0_attn_b_w_q': 8.0,
     'L0_attn_b_w_k': 8.0,
     'L0_attn_b_w_v': 8.0,
     'L0_attn_b_w_o': 8.0}
    for name, (base, spread) in spreads.items():
        noise = np.random.default_rng([zlib.crc32(name.encode()), seed]).standard_normal(out[name].shape)
        drawn = base * np.exp(spread * noise) if base else spread * noise
        out[name] = jnp.asarray(drawn.astype(out[name].dtype))
    for name, factor in factors.items():
        out[name] = (out[name] * factor).astype(out[name].dtype)
    return out
```

```python
from contextlib import ExitStack

import numpy as np

import concourse.bass as bass
from concourse import mybir

ALU = mybir.AluOpType
ACT = mybir.ActivationFunctionType
AX = mybir.AxisListType
F32 = mybir.dt.float32
BF16 = mybir.dt.bfloat16
U32 = mybir.dt.uint32

P = 128
NSEQ, SEQ, D = 8, 512, 256
NTOK = NSEQ * SEQ
NT = NTOK // P
TPS = SEQ // P
KD = D // P
NH, HD = 16, 16
SCALE = HD ** -0.5
WINDOW = 128
EPS = 1e-5
HID, HIDP = 704, 768
KH = HIDP // P
NE, TOPK, EH = 8, 2, 1024
CAP = TOPK * ((NTOK + NE - 1) // NE)
KE = EH // P
MASKED = -(2.0 ** 127)
Q_PARTS = (0, 0, 1, 1, 0, 2)
K_PARTS = (0, 1, 0, 1, 2, 0)
NPROD = len(Q_PARTS)
SROWS = NPROD * HD


class Program:

    def __init__(self, nc, ctx):
        self.nc, self.ctx, self.prefix, self.sems = nc, ctx, "", []

    def sem(self, name):
        self.sems.append(self.nc.alloc_semaphore(name=self.prefix + name))
        return self.sems[-1]

    def end_layer(self):
        self.nc.clear_and_free_semaphores(self.sems)
        self.nc.all_engine_barrier()
        self.sems = []

    def sb(self, name, shape, dt=F32, ctx=None):
        return (ctx or self.ctx).enter_context(self.nc.sbuf_tensor(self.prefix + name, shape, dt))


class Chain:

    def __init__(self, eng, sem, per=0, it=None, start=0):
        self.eng, self.sem, self.base, self.k, self.per = eng, sem, start, 0, per
        self.it = it

    def value(self):
        n = self.base + self.k
        return n if self.it is None else self.it * self.per + n

    def __call__(self, ins):
        ins.then_inc(self.sem, 1)
        self.k += 1
        self.eng.wait_ge(self.sem, self.value())


def rstd_steps(link, dve, act_sqrt, stat, mean, rstd, tmp, sq_done):
    me, mo = stat[:, :, 1], stat[:, :, 4]
    link(dve.tensor_tensor(mean[:, :], me, mo, ALU.add))
    link(dve.tensor_scalar(mean[:, :], mean[:, :], 0.5, None, ALU.mult))
    link(dve.tensor_tensor(tmp[:, 0, :], me, mo, ALU.subtract))
    link(dve.tensor_tensor(tmp[:, 0, :], tmp[:, 0, :], tmp[:, 0, :], ALU.mult))
    link(dve.tensor_tensor(tmp[:, 1, :], stat[:, :, 2], stat[:, :, 5], ALU.add))
    link(dve.tensor_scalar(tmp[:, 1, :], tmp[:, 1, :], 1.0 / D, EPS, ALU.mult, ALU.add))
    act_sqrt(dve.scalar_tensor_tensor(out=tmp[:, 1, :], in0=tmp[:, 0, :], scalar=0.25, in1=tmp[:, 1, :],
                                      op0=ALU.mult, op1=ALU.add))
    sq_done()
    link(dve.reciprocal(rstd[:, :], tmp[:, 2, :]))
    link(dve.tensor_tensor(tmp[:, 0, :], rstd[:, :], rstd[:, :], ALU.mult))
    link(dve.tensor_tensor(tmp[:, 0, :], tmp[:, 0, :], tmp[:, 1, :], ALU.mult))
    link(dve.tensor_scalar(tmp[:, 0, :], tmp[:, 0, :], -0.5, 1.5, ALU.mult, ALU.add))
    link(dve.tensor_tensor(rstd[:, :], rstd[:, :], tmp[:, 0, :], ALU.mult))


def statistics(pr, name, src, stats, normalised=None, stat_of_normalised=None):
    nc = pr.nc
    pr.prefix = name
    chain, var_ready, sqrt_ready = pr.sem("chain"), pr.sem("var_ready"), pr.sem("sqrt_ready")
    rows_ready = pr.sem("rows_ready")
    rounds = [(src, stats)] + ([(normalised, stat_of_normalised)] if normalised is not None else [])
    with nc.Block() as block:

        @block.scalar
        def _(act):
            for n, (_, st) in enumerate(rounds):
                act.wait_ge(var_ready, n + 1)
                act.activation(st["tmp"][:, 2, :], st["tmp"][:, 1, :], ACT.Sqrt).then_inc(sqrt_ready, 1)

        @block.vector
        def _(dve):
            link = Chain(dve, chain)
            for n, (rows, st) in enumerate(rounds):
                with dve.Fori(0, NSEQ) as b:
                    for i in range(TPS):
                        last = dve.bn_stats(st["stat"][:, bass.ds(b * TPS + i, 1), :].rearrange("p o c -> p (o c)"),
                                            rows[:, bass.ds(b * TPS + i, 1), :].rearrange("p o c -> p (o c)"))
                    last.then_inc(rows_ready, 1)
                dve.wait_ge(rows_ready, NSEQ * (2 * n + 1))

                def to_sqrt(ins, n=n):
                    ins.then_inc(var_ready, 1)

                def sqrt_back(n=n):
                    dve.wait_ge(sqrt_ready, n + 1)

                rstd_steps(link, dve, to_sqrt, st["stat"], st["mean"], st["rstd"], st["tmp"], sqrt_back)
                if n + 1 < len(rounds):
                    with dve.Fori(0, NSEQ) as b:
                        for i in range(TPS):
                            t = b * TPS + i
                            last = dve.tensor_scalar(normalised[:, bass.ds(t, 1), :], rows[:, bass.ds(t, 1), :],
                                                     st["mean"][:, bass.ds(t, 1)], st["rstd"][:, bass.ds(t, 1)],
                                                     ALU.subtract, ALU.mult)
                        last.then_inc(rows_ready, 1)
                    dve.wait_ge(rows_ready, NSEQ * (2 * n + 2))


def attention(pr, name, windowed, src, stats, w, cst, psum, qk_parts):
    nc = pr.nc
    pr.prefix = name
    NPJ = 2 * KD
    MU = 32 if windowed else 64
    UPT = MU // TPS
    RND = 4 if windowed else 8
    RPG = RND // 4
    SU = 4 * RND
    LINKS = 5 if windowed else 2
    with ExitStack() as ctx:
        sb = lambda n, s, d=F32: pr.sb(n, s, d, ctx)
        wqk = sb("wqk", [P, KD, w["qk"].shape[-1]])
        wv = sb("wv", [P, KD, D])
        wo = sb("wo", [P, NH // 4, D])
        z = sb("z", [P, TPS, D])
        zT = sb("zT", [P, KD, SEQ])
        rows = sb("rows", [P, 3, SEQ])
        parts = sb("parts", [P, NPJ, 3, SEQ], BF16)
        q_stack = sb("q_stack", [P, NH, SEQ], BF16)
        k_stack = sb("k_stack", [P, NH, SEQ], BF16)
        v_ones = sb("v_ones", [P, TPS, NH, 2 * HD])
        probs = sb("probs", [P, 2, 4, 2 * SEQ])
        row_max = sb("row_max", [P, TPS, NH])
        neg_max = sb("neg_max", [P, 2, NH])
        neg_parts = sb("neg_parts", [P, TPS, 3, NH], BF16)
        maxT = sb("maxT", [3 * NH, SEQ], BF16)
        denom = sb("denom", [P, 2, SEQ])
        headsT = sb("headsT", [P, NH // 4, SEQ])
        if windowed:
            rope = sb("rope", [P, 2, SEQ])
            gain = sb("gain", [P, 2, D])
            window = sb("window", [P, 2, SEQ])
            window_bf = sb("window_bf", [P, 2, SEQ], BF16)

        weights_in = pr.sem("weights_in")
        setup_done, window_ready = pr.sem("setup_done"), pr.sem("window_ready")
        passed = pr.sem("passed")
        z_normed, z_scaled, z_ready = pr.sem("z_normed"), pr.sem("z_scaled"), pr.sem("z_ready")
        z_turned, zT_ready = pr.sem("z_turned"), pr.sem("zT_ready")
        proj_done, proj_read = pr.sem("proj_done"), pr.sem("proj_read")
        parts_ready = pr.sem("parts_ready")
        parts_out = [pr.sem(f"parts_out{g}") for g in range(NPJ)]
        stack_in = [pr.sem("q_stack_in"), pr.sem("k_stack_in")]
        v_done, v_ready = pr.sem("v_done"), pr.sem("v_ready")
        scores_done, max_done = pr.sem("scores_done"), pr.sem("max_done")
        neg_ready, max_turned, maxT_ready, max_in = (pr.sem("neg_ready"), pr.sem("max_turned"), pr.sem("maxT_ready"),
                                                     pr.sem("max_in"))
        scoresT_done, probs_ready, values_done = pr.sem("scoresT_done"), pr.sem("probs_ready"), pr.sem("values_done")
        heads_ready, out_done, out_added = pr.sem("heads_ready"), pr.sem("out_done"), pr.sem("out_added")
        chain = pr.sem("chain")
        NW = 6 if windowed else 3

        with nc.Block() as block:

            @block.sync
            def _(sp):
                sp.dma_start(wqk[:], w["qk"]).then_inc(weights_in, 16)
                sp.dma_start(wv[:], w["v"]).then_inc(weights_in, 16)
                sp.dma_start(wo[:], w["o"]).then_inc(weights_in, 16)
                if windowed:
                    sp.dma_start(rope[:], w["rope"]).then_inc(weights_in, 16)
                    sp.dma_start(gain[:], w["gain"]).then_inc(weights_in, 16)
                    sp.dma_start(window[:], w["window"]).then_inc(weights_in, 16)
                with sp.Fori(0, NSEQ) as b:
                    for g in range(NPJ):
                        qk, half = g // KD, g % KD
                        sp.wait_ge(parts_ready, b * NPJ + g + 1)
                        sp.dma_start(qk_parts[qk, :, half * P:(half + 1) * P, :].rearrange("c p t -> p c t"),
                                     parts[:, g]).then_inc(parts_out[g], 16)
                        if half == KD - 1:
                            for h in range(KD):
                                sp.wait_ge(parts_out[qk * KD + h], b * 16 + 16)
                            for n in range(NPROD):
                                c = (Q_PARTS, K_PARTS)[qk][n]
                                stack = (q_stack, k_stack)[qk]
                                sp.dma_start(stack[n * HD:(n + 1) * HD, :, :],
                                             qk_parts[qk, c].rearrange("(h d) t -> d h t", d=HD)
                                             ).then_inc(stack_in[qk], 16)
                    sp.wait_ge(maxT_ready, b + 1)
                    for c in range(3):
                        sp.dma_start(q_stack[SROWS + c:SROWS + c + 1, :, :],
                                     maxT[c * NH:(c + 1) * NH, :]).then_inc(max_in, 16)

            @block.gpsimd
            def _(pool):
                pool.memset(v_ones[:, :, :, HD:], 1.0).then_inc(setup_done, 1)
                pool.wait_ge(setup_done, 1)
                pool.memset(k_stack[SROWS:SROWS + 32, :, :], 1.0).then_inc(setup_done, 1)
                pool.wait_ge(setup_done, 2)
                if windowed:
                    pool.wait_ge(weights_in, 16 * NW)
                    with pool.Fori(0, NSEQ) as b:
                        pool.wait_ge(z_normed, b + 1)
                        for i in range(TPS):
                            ins = pool.tensor_tensor(z[:, i, :], z[:, i, :], gain[:, 0, :], ALU.mult)
                        ins.then_inc(z_scaled, 1)
                        pool.wait_ge(z_scaled, b + 1)
                        for i in range(TPS):
                            ins = pool.tensor_tensor(z[:, i, :], z[:, i, :], gain[:, 1, :], ALU.add)
                        ins.then_inc(z_ready, 1)

            @block.scalar
            def _(act):
                with act.Fori(0, NSEQ) as b:
                    for k in range(KD):
                        act.wait_ge(z_turned, b * KD + k + 1)
                        act.activation(zT[:, k, :], psum[:, 2 + k, :], ACT.Copy).then_inc(zT_ready, 1)
                    for v in range(2):
                        act.wait_ge(v_done, b * 2 + v + 1)
                        act.activation(v_ones[:, 2 * v:2 * v + 2, :, 0:HD],
                                       psum[:, 6 + v, :].rearrange("p (i h d) -> p i h d", i=2, h=NH),
                                       ACT.Copy).then_inc(v_ready, 1)
                    for u in range(SU):
                        r, s = u // 4, u % 4
                        act.wait_ge(scoresT_done, b * SU + u + 1)
                        if r >= 2:
                            act.wait_ge(values_done, b * RND + r - 1)
                        act.activation(probs[:, r % 2, s, :],
                                       psum[:, 2 + 2 * (u % 2):4 + 2 * (u % 2), :].rearrange("p a c -> p (a c)"),
                                       ACT.Exp, scale=SCALE).then_inc(probs_ready, 1)

            @block.vector
            def _(dve):
                if windowed:
                    dve.wait_ge(weights_in, 16 * NW)
                    dve.tensor_copy(window_bf[:], window[:]).then_inc(window_ready, 1)
                per = NPJ * LINKS + TPS * 4 + 4 * 2
                with dve.Fori(0, NSEQ) as b:
                    link = Chain(dve, chain, per, b)
                    for i in range(TPS):
                        t = b * TPS + i
                        ins = dve.tensor_scalar(z[:, i:i + 1, :], src[:, bass.ds(t, 1), :],
                                                stats["mean"][:, bass.ds(t, 1)], stats["rstd"][:, bass.ds(t, 1)],
                                                ALU.subtract, ALU.mult)
                    ins.then_inc(z_normed, 1)
                    for g in range(NPJ):
                        dve.wait_ge(proj_done, b * NPJ + g + 1)
                        if windowed:
                            bank = 2 * (g % 3)
                            link(dve.tensor_tensor(rows[:, 0, :], psum[:, bank, :], rope[:, 0, :], ALU.mult))
                            dve.tensor_tensor(rows[:, 1, :], psum[:, bank + 1, :], rope[:, 1, :],
                                              ALU.mult).then_inc(proj_read, 1)
                            dve.wait_ge(proj_read, b * NPJ + g + 1)
                            link(dve.tensor_tensor(rows[:, 2, :], rows[:, 0, :], rows[:, 1, :], ALU.add))
                            whole = rows[:, 2, :]
                        else:
                            whole = psum[:, (0, 1, 4, 5)[g], :]
                        link(dve.tensor_copy(parts[:, g, 0, :], whole))
                        rest = dve.tensor_tensor(rows[:, 0, :], whole, parts[:, g, 0, :], ALU.subtract)
                        if windowed:
                            link(rest)
                        else:
                            rest.then_inc(proj_read, 1)
                            dve.wait_ge(proj_read, b * NPJ + g + 1)
                        link(dve.tensor_copy(parts[:, g, 1, :], rows[:, 0, :]))
                        dve.tensor_tensor(parts[:, g, 2, :], rows[:, 0, :], parts[:, g, 1, :],
                                          ALU.subtract).then_inc(parts_ready, 1)
                        dve.wait_ge(parts_ready, b * NPJ + g + 1)
                    for m in range(MU):
                        i = m // UPT
                        dve.wait_ge(scores_done, b * MU + m + 1)
                        if windowed:
                            h = 2 * (m % UPT)
                            lo = WINDOW if i == 0 else 0
                            block_ = psum[:, m % 2, :].rearrange("p (h c) -> p h c", h=2)[:, :, lo:]
                            ins = dve.tensor_reduce(row_max[:, i, h:h + 2], block_, AX.X, ALU.max)
                        else:
                            h = m % UPT
                            ins = dve.tensor_reduce(row_max[:, i, h:h + 1], psum[:, m % 2, :], AX.X, ALU.max)
                        ins.then_inc(max_done, 1)
                        if m % UPT == UPT - 1:
                            dve.wait_ge(max_done, b * MU + m + 1)
                            link(dve.tensor_scalar(neg_max[:, 0, :], row_max[:, i, :], -1.0, None, ALU.mult))
                            link(dve.tensor_copy(neg_parts[:, i, 0, :], neg_max[:, 0, :]))
                            link(dve.tensor_tensor(neg_max[:, 1, :], neg_max[:, 0, :], neg_parts[:, i, 0, :],
                                                   ALU.subtract))
                            link(dve.tensor_copy(neg_parts[:, i, 1, :], neg_max[:, 1, :]))
                            dve.tensor_tensor(neg_parts[:, i, 2, :], neg_max[:, 1, :], neg_parts[:, i, 1, :],
                                              ALU.subtract).then_inc(neg_ready, 1)
                            dve.wait_ge(neg_ready, b * TPS + i + 1)
                    dve.wait_ge(max_turned, b * TPS + TPS)
                    dve.tensor_copy(maxT[:, :], psum[:, 6, :].bitcast(BF16)[0:3 * NH, 0:SEQ]).then_inc(maxT_ready, 1)
                    for g in range(4):
                        dve.wait_ge(values_done, b * RND + (g + 1) * RPG)
                        dve.sem_inc(passed, 1)
                        heads = psum[:, 6 + g % 2, :]
                        link(dve.stream_shuffle(denom[:, 0, :], heads, [HD + j % HD for j in range(32)]))
                        link(dve.reciprocal(denom[:, 1, :], denom[:, 0, :]))
                        dve.tensor_tensor(headsT[:, g, :], heads, denom[:, 1, :], ALU.mult).then_inc(heads_ready, 1)
                        dve.wait_ge(heads_ready, b * 4 + g + 1)
                    for o in range(2):
                        dve.wait_ge(out_done, b * 2 + o + 1)
                        res = src[:, bass.ds(b * TPS + 2 * o, 2), :]
                        dve.tensor_tensor(res, psum[:, o, :].rearrange("p (i c) -> p i c", i=2), res,
                                          ALU.add).then_inc(out_added, 1)
                    assert link.k == per, (link.k, per)
                dve.wait_ge(out_added, 2 * NSEQ)

            @block.tensor
            def _(pe):
                pe.wait_ge(weights_in, 16 * NW)
                pe.wait_ge(setup_done, 2)
                if windowed:
                    pe.wait_ge(window_ready, 1)
                with pe.Fori(0, NSEQ) as b:
                    pe.wait_ge(z_ready if windowed else z_normed, b + 1)
                    for k in range(KD):
                        for i in range(TPS):
                            ins = pe.transpose(psum[:, 2 + k, i * P:(i + 1) * P], z[:, i, k * P:(k + 1) * P],
                                               cst["ident"][:])
                        ins.then_inc(z_turned, 1)
                    pe.wait_ge(zT_ready, b * KD + KD)
                    for g in range(NPJ):
                        if windowed:
                            if g == 3:
                                pe.wait_ge(proj_read, b * NPJ + 1)
                            banks = (2 * (g % 3), 2 * (g % 3) + 1)
                        else:
                            banks = ((0, 1, 4, 5)[g],)
                        for n, bank in enumerate(banks):
                            col = (g // KD * len(banks) + n) * D + (g % KD) * P
                            for k in range(KD):
                                ins = pe.matmul(psum[:, bank, :], wqk[:, k, col:col + P], zT[:, k, :],
                                                start=(k == 0), stop=(k == KD - 1))
                        ins.then_inc(proj_done, 1)
                    for i in range(TPS):
                        for k in range(KD):
                            ins = pe.matmul(psum[:, 6 + i // 2, (i % 2) * D:(i % 2 + 1) * D],
                                            zT[:, k, i * P:(i + 1) * P], wv[:, k, :],
                                            start=(k == 0), stop=(k == KD - 1))
                        if i % 2:
                            ins.then_inc(v_done, 1)
                    for qk in range(2):
                        pe.wait_ge(stack_in[qk], b * (16 * NPROD) + 16 * NPROD)
                    pe.wait_ge(proj_read, b * NPJ + NPJ)

                    def turn_max(i):
                        pe.wait_ge(neg_ready, b * TPS + i + 1)
                        if i == 0:
                            pe.wait_ge(v_ready, b * 2 + 2)
                        pe.sem_inc(passed, 1)
                        pe.transpose(psum[:, 6, :].bitcast(BF16)[0:3 * NH, i * P:(i + 1) * P],
                                     neg_parts[:, i].rearrange("p c h -> p (c h)"),
                                     cst["ident_bf"][:]).then_inc(max_turned, 1)

                    for m in range(MU):
                        i = m // UPT
                        if m >= 2:
                            pe.wait_ge(max_done, b * MU + m - 1)
                        bank = psum[:, m % 2, :]
                        if windowed:
                            pe.matmul(bank, cst["ident_bf"][:], window_bf[:, 0, :], start=True, stop=False)
                            for n in range(2):
                                h = 2 * (m % UPT) + n
                                lo = 0 if i else WINDOW
                                ins = pe.matmul(bank[:, 2 * n * P + lo:2 * (n + 1) * P],
                                                q_stack[0:SROWS, h, i * P:(i + 1) * P],
                                                k_stack[0:SROWS, h, (i - 1) * P + lo:(i + 1) * P],
                                                start=False, stop=(n == 1))
                        else:
                            ins = pe.matmul(bank, q_stack[0:SROWS, m % UPT, i * P:(i + 1) * P],
                                            k_stack[0:SROWS, m % UPT, :], start=True, stop=True)
                        ins.then_inc(scores_done, 1)
                        if m % UPT == UPT // 2 and i:
                            turn_max(i - 1)
                    turn_max(TPS - 1)
                    pe.wait_ge(max_in, b * 48 + 48)
                    pe.wait_ge(zT_ready, b * KD + KD)

                    def scoresT(r):
                        for s in range(4):
                            u = 4 * r + s
                            h = (r // RPG) * 4 + s
                            if u >= 2:
                                pe.wait_ge(probs_ready, b * SU + u - 1)
                            for a in range(2):
                                bank = psum[:, 2 + 2 * (u % 2) + a, :]
                                if windowed:
                                    pe.matmul(bank, cst["ident_bf"][:], window_bf[:, 1, :], start=True, stop=False)
                                    for n in range(2):
                                        j = 2 * a + n
                                        w_ = min(2 * P, SEQ - j * P)
                                        ins = pe.matmul(bank[:, 2 * n * P:2 * n * P + w_],
                                                        k_stack[0:SROWS + 3, h, j * P:(j + 1) * P],
                                                        q_stack[0:SROWS + 3, h, j * P:j * P + w_],
                                                        start=False, stop=(n == 1))
                                else:
                                    j = 2 * (r % 2) + a
                                    ins = pe.matmul(bank, k_stack[0:SROWS + 3, h, j * P:(j + 1) * P],
                                                    q_stack[0:SROWS + 3, h, :], start=True, stop=True)
                            ins.then_inc(scoresT_done, 1)

                    def values(r):
                        g = r // RPG
                        pe.wait_ge(probs_ready, b * SU + 4 * r + 4)
                        if r == 0:
                            pe.wait_ge(maxT_ready, b + 1)
                        if g >= 2 and r % RPG == 0:
                            pe.wait_ge(heads_ready, b * 4 + g - 1)
                        if windowed:
                            for i in range(TPS):
                                for j in range(max(i - 1, 0), i + 1):
                                    for s in range(4):
                                        c = 2 * P * j + P * (i - j)
                                        ins = pe.matmul(psum[32 * s:32 * s + 32, 6 + g % 2, i * P:(i + 1) * P],
                                                        v_ones[:, j, 4 * g + s, :], probs[:, r % 2, s, c:c + P],
                                                        start=(j == max(i - 1, 0)), stop=(j == i))
                        else:
                            for a in range(2):
                                j = 2 * (r % 2) + a
                                for s in range(4):
                                    ins = pe.matmul(psum[32 * s:32 * s + 32, 6 + g % 2, :],
                                                    v_ones[:, j, 4 * g + s, :],
                                                    probs[:, r % 2, s, a * SEQ:(a + 1) * SEQ],
                                                    start=(j == 0), stop=(j == TPS - 1))
                        ins.then_inc(values_done, 1)

                    scoresT(0)
                    for r in range(1, RND):
                        scoresT(r)
                        values(r - 1)
                    values(RND - 1)
                    pe.wait_ge(heads_ready, b * 4 + 4)
                    for i in range(TPS):
                        for g in range(4):
                            ins = pe.matmul(psum[:, i // 2, (i % 2) * D:(i % 2 + 1) * D],
                                            headsT[:, g, i * P:(i + 1) * P], wo[:, g, :],
                                            start=(g == 0), stop=(g == 3))
                        if i % 2:
                            ins.then_inc(out_done, 1)


def swiglu(pr, name, x_res, h_res, stats, w, cst, psum):
    nc = pr.nc
    pr.prefix = name
    with ExitStack() as ctx:
        sb = lambda n, s, d=F32: pr.sb(n, s, d, ctx)
        w1, w3, w2 = sb("w1", [P, KD, HIDP]), sb("w3", [P, KD, HIDP]), sb("w2", [P, KH, D])
        gain = sb("gain", [P, 2, D])
        z = sb("z", [P, TPS, D])
        zT = sb("zT", [P, KD, SEQ])
        th = sb("th", [P, 2, SEQ])
        act_gate = sb("act_gate", [P, 2, SEQ])
        hidT = sb("hidT", [P, KH, SEQ])
        block_out = sb("block_out", [P, 2, 2 * D])
        weights_in = pr.sem("weights_in")
        z_normed, z_scaled, z_ready = pr.sem("z_normed"), pr.sem("z_scaled"), pr.sem("z_ready")
        z_turned, zT_ready = pr.sem("z_turned"), pr.sem("zT_ready")
        up_done, tanh_ready, gate_ready, hid_ready = (pr.sem("up_done"), pr.sem("tanh_ready"), pr.sem("gate_ready"),
                                                      pr.sem("hid_ready"))
        down_done, down_read, added = pr.sem("down_done"), pr.sem("down_read"), pr.sem("added")
        with nc.Block() as block:

            @block.sync
            def _(sp):
                for dst, s in ((w1, w["w1"]), (w3, w["w3"]), (w2, w["w2"]), (gain, w["gain"])):
                    sp.dma_start(dst[:], s).then_inc(weights_in, 16)

            @block.gpsimd
            def _(pool):
                pool.wait_ge(weights_in, 64)
                with pool.Fori(0, NSEQ) as b:
                    pool.wait_ge(z_normed, b + 1)
                    for i in range(TPS):
                        ins = pool.tensor_tensor(z[:, i, :], z[:, i, :], gain[:, 0, :], ALU.mult)
                    ins.then_inc(z_scaled, 1)
                    pool.wait_ge(z_scaled, b + 1)
                    for i in range(TPS):
                        ins = pool.tensor_tensor(z[:, i, :], z[:, i, :], gain[:, 1, :], ALU.add)
                    ins.then_inc(z_ready, 1)
                    for o in range(2):
                        pool.wait_ge(down_read, b * 2 + o + 1)
                        res = x_res[:, bass.ds(b * TPS + 2 * o, 2), :]
                        pool.tensor_tensor(res, block_out[:, o, :].rearrange("p (i c) -> p i c", i=2), res,
                                           ALU.add).then_inc(added, 1)
                pool.wait_ge(added, 2 * NSEQ)

            @block.scalar
            def _(act):
                with act.Fori(0, NSEQ) as b:
                    for k in range(KD):
                        act.wait_ge(z_turned, b * KD + k + 1)
                        act.activation(zT[:, k, :], psum[:, k, :], ACT.Copy).then_inc(zT_ready, 1)
                    for m in range(KH):
                        act.wait_ge(up_done, b * KH + m + 1)
                        if m >= 2:
                            act.wait_ge(gate_ready, b * KH + m - 1)
                        act.activation(th[:, m % 2, :], psum[:, 2 + 2 * (m % 2), :], ACT.Tanh,
                                       scale=0.5).then_inc(tanh_ready, 1)

            @block.vector
            def _(dve):
                with dve.Fori(0, NSEQ) as b:
                    for i in range(TPS):
                        t = b * TPS + i
                        ins = dve.tensor_scalar(z[:, i:i + 1, :], h_res[:, bass.ds(t, 1), :],
                                                stats["mean"][:, bass.ds(t, 1)], stats["rstd"][:, bass.ds(t, 1)],
                                                ALU.subtract, ALU.mult)
                    ins.then_inc(z_normed, 1)
                    for m in range(KH):
                        dve.wait_ge(tanh_ready, b * KH + m + 1)
                        if m >= 2:
                            dve.wait_ge(hid_ready, b * KH + m - 1)
                        dve.scalar_tensor_tensor(out=act_gate[:, m % 2, :], in0=th[:, m % 2, :], scalar=1.0,
                                                 in1=psum[:, 2 + 2 * (m % 2), :], op0=ALU.add,
                                                 op1=ALU.mult).then_inc(gate_ready, 1)
                        dve.wait_ge(gate_ready, b * KH + m + 1)
                        dve.scalar_tensor_tensor(out=hidT[:, m, :], in0=act_gate[:, m % 2, :], scalar=0.5,
                                                 in1=psum[:, 3 + 2 * (m % 2), :], op0=ALU.mult,
                                                 op1=ALU.mult).then_inc(hid_ready, 1)
                    for o in range(2):
                        dve.wait_ge(down_done, b * 2 + o + 1)
                        dve.tensor_tensor(block_out[:, o, :].rearrange("p (i c) -> p i c", i=2),
                                          psum[:, 6 + o, :].rearrange("p (i c) -> p i c", i=2),
                                          h_res[:, bass.ds(b * TPS + 2 * o, 2), :], ALU.add).then_inc(down_read, 1)

            @block.tensor
            def _(pe):
                pe.wait_ge(weights_in, 64)
                with pe.Fori(0, NSEQ) as b:
                    pe.wait_ge(z_ready, b + 1)
                    for k in range(KD):
                        for i in range(TPS):
                            ins = pe.transpose(psum[:, k, i * P:(i + 1) * P], z[:, i, k * P:(k + 1) * P],
                                               cst["ident"][:])
                        ins.then_inc(z_turned, 1)
                    pe.wait_ge(zT_ready, b * KD + KD)
                    for m in range(KH):
                        if m >= 2:
                            pe.wait_ge(hid_ready, b * KH + m - 1)
                        for n, wt in enumerate((w1, w3)):
                            for k in range(KD):
                                ins = pe.matmul(psum[:, 2 + 2 * (m % 2) + n, :], wt[:, k, m * P:(m + 1) * P],
                                                zT[:, k, :], start=(k == 0), stop=(k == KD - 1))
                        ins.then_inc(up_done, 1)
                    pe.wait_ge(hid_ready, b * KH + KH)
                    for i in range(TPS):
                        for k in range(KH):
                            ins = pe.matmul(psum[:, 6 + i // 2, (i % 2) * D:(i % 2 + 1) * D],
                                            hidT[:, k, i * P:(i + 1) * P], w2[:, k, :],
                                            start=(k == 0), stop=(k == KH - 1))
                        if i % 2:
                            ins.then_inc(down_done, 1)


def experts(pr, name, x_res, z_all, stats, w, cst, psum, slots_in, slots_out):
    nc = pr.nc
    pr.prefix = name
    SEG = 512
    NSTEP = NE * CAP // SEG
    BIG = float(4 * NE * CAP)
    with ExitStack() as ctx:
        sb = lambda n, s, d=F32: pr.sb(n, s, d, ctx)
        scatter_at = sb("scatter_at", [P, TOPK, NT], U32)
        gather_at = sb("gather_at", [P, TOPK, NT], U32)
        weight = sb("weight", [P, TOPK, NT])
        route(pr, name + "r_", x_res, z_all, stats, w, cst, psum, scatter_at, gather_at, weight, BIG)
        pr.prefix = name
        fc1 = sb("fc1", [P, 2, KD, EH])
        fc2 = sb("fc2", [P, 2, KE, D])
        bias1 = sb("bias1", [P, NE, KE])
        bias2 = sb("bias2", [P, NE, D])
        rows_in = sb("rows_in", [P, 2, TPS, D])
        rowsT = sb("rowsT", [P, 2, KD, SEG])
        hidT = sb("hidT", [P, KE, SEG])
        rows_out = sb("rows_out", [P, 2, TPS, D])
        NG = 8
        picked = sb("picked", [P, NG, D])
        bias_in, fc_in = pr.sem("bias_in"), [pr.sem("fc_in0"), pr.sem("fc_in1")]
        scattered = pr.sem("scattered")
        rows_loaded = [pr.sem("rows_loaded0"), pr.sem("rows_loaded1")]
        rows_turned, rowsT_ready = pr.sem("rows_turned"), pr.sem("rowsT_ready")
        up_done, hid_ready, down_done, out_ready = (pr.sem("up_done"), pr.sem("hid_ready"), pr.sem("down_done"),
                                                    pr.sem("out_ready"))
        out_stored = pr.sem("out_stored")
        gathered = [pr.sem(f"gathered{j}") for j in range(NG)]
        added = pr.sem("added")
        passed = pr.sem("passed")
        with nc.Block() as block:

            @block.sync
            def _(sp):
                def load_expert(e, s):
                    sp.dma_start(fc1[:, s], w["fc1"][bass.ds(e, 1)].rearrange("o p k h -> p (o k) h")
                                 ).then_inc(fc_in[s], 16)
                    sp.dma_start(fc2[:, s], w["fc2"][bass.ds(e, 1)].rearrange("o p k h -> p (o k) h")
                                 ).then_inc(fc_in[s], 16)

                def load_rows(n, s):
                    sp.dma_start(rows_in[:, s], slots_in[bass.ds(n * SEG, SEG), :].rearrange("(i p) d -> p i d", p=P)
                                 ).then_inc(rows_loaded[s], 16)

                sp.dma_start(bias1[:], w["bias1"]).then_inc(bias_in, 16)
                sp.dma_start(bias2[:], w["bias2"]).then_inc(bias_in, 16)
                for s in range(2):
                    load_expert(s, s)
                sp.wait_ge(scattered, 16 * TOPK * NT)
                for s in range(2):
                    load_rows(s, s)

                def store(n, s):
                    sp.wait_ge(out_ready, n * 2 + 2)
                    sp.dma_start(slots_out[bass.ds(n * SEG, SEG), :].rearrange("(i p) d -> p i d", p=P),
                                 rows_out[:, s]).then_inc(out_stored, 16)

                with sp.Fori(0, NSTEP // 4 - 1) as it:
                    for c in range(4):
                        n = it * 4 + c
                        store(n, c % 2)
                        if c % 2:
                            load_expert(it * 2 + c // 2 + 2, c // 2)
                        sp.wait_ge(out_stored, n * 16 + 16)
                        load_rows(n + 2, c % 2)
                for n in range(NSTEP - 4, NSTEP):
                    store(n, n % 2)
                    sp.wait_ge(out_stored, n * 16 + 16)
                    if n + 2 < NSTEP:
                        load_rows(n + 2, n % 2)

            @block.gpsimd
            def _(pool):
                for k in range(TOPK):
                    for t in range(NT):
                        pool.indirect_dma_start(
                            out=slots_in[:, :], out_offset=bass.IndirectOffsetOnAxis(scatter_at[:, k, t:t + 1], 0),
                            in_=z_all[:, t, :], in_offset=None, bounds_check=NE * CAP - 1, oob_is_err=False,
                        ).then_inc(scattered, 16)
                pool.wait_ge(out_stored, 16 * NSTEP)
                for g in range(NT * TOPK):
                    t, k = g // TOPK, g % TOPK
                    if g >= NG:
                        pool.wait_ge(added, g - NG + 1)
                    pool.indirect_dma_start(
                        out=picked[:, g % NG, :], out_offset=None, in_=slots_out[:, :],
                        in_offset=bass.IndirectOffsetOnAxis(gather_at[:, k, t:t + 1], 0),
                        bounds_check=NE * CAP - 1, oob_is_err=False,
                    ).then_inc(gathered[g % NG], 16)

            @block.scalar
            def _(act):
                act.wait_ge(bias_in, 32)
                with act.Fori(0, NE // 2) as it:
                    for c in range(4):
                        n = it * 4 + c
                        for m in range(KE):
                            act.wait_ge(up_done, n * KE + m + 1)
                            act.sem_inc(passed, 1)
                            act.activation(hidT[:, m, :], psum[:, 2 + m % 4, :], ACT.Relu,
                                           bias=bias1[:, bass.ds(it * 2 + c // 2, 1), m:m + 1].rearrange("p a b -> p (a b)"),
                                           ).then_inc(hid_ready, 1)

            @block.vector
            def _(dve):
                dve.wait_ge(bias_in, 32)
                with dve.Fori(0, NE // 2) as it:
                    for c in range(4):
                        n = it * 4 + c
                        for k in range(KD):
                            dve.wait_ge(rows_turned, n * KD + k + 1)
                            dve.tensor_copy(rowsT[:, c % 2, k, :], psum[:, k, :]).then_inc(rowsT_ready, 1)
                        for o in range(2):
                            dve.wait_ge(down_done, n * 2 + o + 1)
                            for i in range(2):
                                ins = dve.tensor_tensor(rows_out[:, c % 2, 2 * o + i:2 * o + i + 1, :],
                                                        psum[:, 6 + o, i * D:(i + 1) * D].rearrange("p (o d) -> p o d", o=1),
                                                        bias2[:, bass.ds(it * 2 + c // 2, 1), :], ALU.add)
                            ins.then_inc(out_ready, 1)
                for g in range(NT * TOPK):
                    t, k = g // TOPK, g % TOPK
                    dve.wait_ge(gathered[g % NG], 16 * (g // NG + 1))
                    if k:
                        dve.wait_ge(added, g)
                    dve.scalar_tensor_tensor(out=x_res[:, t, :], in0=picked[:, g % NG, :],
                                             scalar=weight[:, k, t:t + 1], in1=x_res[:, t, :],
                                             op0=ALU.mult, op1=ALU.add).then_inc(added, 1)
                dve.wait_ge(added, NT * TOPK)

            @block.tensor
            def _(pe):
                with pe.Fori(0, NE // 2) as it:
                    for c in range(4):
                        n = it * 4 + c
                        e, s = c // 2, c % 2
                        pe.wait_ge(rows_loaded[s], (it * 2 + e) * 16 + 16)
                        for k in range(KD):
                            for i in range(TPS):
                                ins = pe.transpose(psum[:, k, i * P:(i + 1) * P],
                                                   rows_in[:, s, i, k * P:(k + 1) * P], cst["ident"][:])
                            ins.then_inc(rows_turned, 1)
                        pe.wait_ge(fc_in[e], it * 32 + 32)
                        pe.wait_ge(rowsT_ready, n * KD + KD)
                        for m in range(KE):
                            if m >= 4:
                                pe.wait_ge(hid_ready, n * KE + m - 3)
                            for k in range(KD):
                                ins = pe.matmul(psum[:, 2 + m % 4, :], fc1[:, e, k, m * P:(m + 1) * P],
                                                rowsT[:, s, k, :], start=(k == 0), stop=(k == KD - 1))
                            ins.then_inc(up_done, 1)
                        pe.wait_ge(hid_ready, n * KE + KE)
                        for i in range(TPS):
                            for k in range(KE):
                                ins = pe.matmul(psum[:, 6 + i // 2, (i % 2) * D:(i % 2 + 1) * D],
                                                hidT[:, k, i * P:(i + 1) * P], fc2[:, e, k, :],
                                                start=(k == 0), stop=(k == KE - 1))
                            if i % 2:
                                ins.then_inc(down_done, 1)


def route(pr, name, x_res, z_all, stats, w, cst, psum, scatter_at, gather_at, weight, big):
    nc = pr.nc
    pr.prefix = name
    with ExitStack() as ctx:
        sb = lambda n, s, d=F32: pr.sb(n, s, d, ctx)
        gate = sb("gate", [P, KD, NE])
        count_in = sb("count_in", [P, 2 * P + NE])
        z = sb("z", [P, TPS, D])
        zT = sb("zT", [P, KD, SEQ])
        logits = sb("logits", [P, TPS, NE])
        top8 = sb("top8", [P, TPS, 8])
        at8 = sb("at8", [P, TPS, 8], U32)
        top = sb("top", [P, NT, TOPK])
        choice = sb("choice", [P, NT, TOPK])
        onehot = sb("onehot", [P, TOPK, NT, NE])
        run = sb("run", [P, 2, NT, NE])
        before = sb("before", [P, TOPK, NT, NE])
        small = sb("small", [P, 4, NT])
        loc = sb("loc", [P, TOPK, NT])
        slot = sb("slot", [P, 3, NT])
        in_ = pr.sem("in")
        z_normed, z_kept, z_turned, zT_ready = (pr.sem("z_normed"), pr.sem("z_kept"), pr.sem("z_turned"),
                                                pr.sem("zT_ready"))
        passed = pr.sem("passed")
        logits_done, chain, bulk = pr.sem("logits_done"), pr.sem("chain"), pr.sem("bulk")
        gap_ready, exp_ready, before_ready, places_done = (pr.sem("gap_ready"), pr.sem("exp_ready"),
                                                           pr.sem("before_ready"), pr.sem("places_done"))
        with nc.Block() as block:

            @block.sync
            def _(sp):
                sp.dma_start(gate[:], w["gate"]).then_inc(in_, 16)
                sp.dma_start(count_in[:], w["count"]).then_inc(in_, 16)

            @block.gpsimd
            def _(pool):
                with pool.Fori(0, NSEQ) as b:
                    pool.wait_ge(z_normed, b + 1)
                    pool.tensor_copy(z_all[:, bass.ds(b * TPS, TPS), :], z[:]).then_inc(z_kept, 1)
                pool.wait_ge(z_kept, NSEQ)

            @block.scalar
            def _(act):
                with act.Fori(0, NSEQ) as b:
                    for k in range(KD):
                        act.wait_ge(z_turned, b * KD + k + 1)
                        act.activation(zT[:, k, :], psum[:, k, :], ACT.Copy).then_inc(zT_ready, 1)
                act.wait_ge(gap_ready, 1)
                act.activation(small[:, 1, :], small[:, 0, :], ACT.Exp).then_inc(exp_ready, 1)

            @block.vector
            def _(dve):
                with dve.Fori(0, NSEQ) as b:
                    link = Chain(dve, chain, 5, b)
                    for i in range(TPS):
                        t = b * TPS + i
                        ins = dve.tensor_scalar(z[:, i:i + 1, :], x_res[:, bass.ds(t, 1), :],
                                                stats["mean"][:, bass.ds(t, 1)], stats["rstd"][:, bass.ds(t, 1)],
                                                ALU.subtract, ALU.mult)
                    ins.then_inc(z_normed, 1)
                    dve.wait_ge(logits_done, b + 1)
                    link(dve.tensor_copy(logits[:], psum[:, 2, 0:TPS * NE].rearrange("p (i e) -> p i e", e=NE)))
                    dve.sem_inc(passed, 1)
                    for i in range(TPS):
                        ins = dve.max(top8[:, i, :], logits[:, i, :])
                    link(ins)
                    dve.sem_inc(passed, 1)
                    for i in range(TPS):
                        ins = dve.max_index(at8[:, i, :], top8[:, i, :], logits[:, i, :])
                    link(ins)
                    link(dve.tensor_copy(top[:, bass.ds(b * TPS, TPS), :], top8[:, :, 0:TOPK]))
                    link(dve.tensor_copy(choice[:, bass.ds(b * TPS, TPS), :], at8[:, :, 0:TOPK]))
                    dve.wait_ge(z_kept, b + 1)
                link = Chain(dve, bulk)
                dve.tensor_tensor(small[:, 0, :], top[:, :, 1], top[:, :, 0], ALU.subtract).then_inc(gap_ready, 1)
                dve.wait_ge(in_, 32)
                iota = count_in[:, 2 * P:2 * P + NE].rearrange("p (o e) -> p o e", o=1).broadcast_to((P, NT, NE))
                for k in range(TOPK):
                    link(dve.tensor_tensor(onehot[:, k], iota, choice[:, :, k:k + 1].broadcast_to((P, NT, NE)),
                                           ALU.is_equal))
                for k in range(TOPK):
                    held, other = onehot[:, k], 0
                    step = 1
                    while step < NT:
                        dst = run[:, other]
                        dve.tensor_copy(dst[:, 0:step], held[:, 0:step])
                        link(dve.tensor_tensor(dst[:, step:], held[:, step:], held[:, 0:NT - step], ALU.add))
                        held, other, step = dst, 1 - other, step * 2
                    link(dve.tensor_tensor(before[:, k], held, onehot[:, k], ALU.subtract))
                    if k == 0:
                        total = sb("total", [P, 1, NE])
                        link(dve.tensor_copy(total[:], held[:, NT - 1:NT]))
                    else:
                        dve.tensor_tensor(before[:, k], before[:, k], total[:].broadcast_to((P, NT, NE)),
                                          ALU.add).then_inc(before_ready, 1)
                dve.wait_ge(exp_ready, 1)
                link(dve.tensor_scalar(small[:, 2, :], small[:, 1, :], 1.0, None, ALU.add))
                link(dve.reciprocal(small[:, 3, :], small[:, 2, :]))
                dve.wait_ge(before_ready, 1)
                for k in range(TOPK):
                    dve.wait_ge(places_done, k + 1)
                    link(dve.tensor_tensor(run[:, 0], psum[:, 4 + k, 0:NT * NE].rearrange("p (t e) -> p t e", e=NE),
                                           onehot[:, k], ALU.mult))
                    link(dve.tensor_reduce(loc[:, k, :], run[:, 0], AX.X, ALU.add))
                    link(dve.scalar_tensor_tensor(out=slot[:, 0, :], in0=choice[:, :, k], scalar=float(CAP),
                                                  in1=loc[:, k, :], op0=ALU.mult, op1=ALU.add))
                    link(dve.tensor_scalar(slot[:, 1, :], loc[:, k, :], float(CAP), None, ALU.is_lt))
                    link(dve.tensor_tensor(slot[:, 0, :], slot[:, 0, :], slot[:, 1, :], ALU.mult))
                    link(dve.tensor_copy(gather_at[:, k, :], slot[:, 0, :]))
                    link(dve.tensor_scalar(slot[:, 2, :], slot[:, 1, :], -big, big, ALU.mult, ALU.add))
                    link(dve.tensor_tensor(slot[:, 2, :], slot[:, 2, :], slot[:, 0, :], ALU.add))
                    link(dve.tensor_copy(scatter_at[:, k, :], slot[:, 2, :]))
                    link(dve.tensor_tensor(weight[:, k, :], small[:, 3, :], slot[:, 1, :], ALU.mult))
                    if k:
                        link(dve.tensor_tensor(weight[:, k, :], weight[:, k, :], small[:, 1, :], ALU.mult))

            @block.tensor
            def _(pe):
                pe.wait_ge(in_, 32)
                with pe.Fori(0, NSEQ) as b:
                    pe.wait_ge(z_normed, b + 1)
                    for k in range(KD):
                        for i in range(TPS):
                            ins = pe.transpose(psum[:, k, i * P:(i + 1) * P], z[:, i, k * P:(k + 1) * P],
                                               cst["ident"][:])
                        ins.then_inc(z_turned, 1)
                    pe.wait_ge(zT_ready, b * KD + KD)
                    for i in range(TPS):
                        for k in range(KD):
                            ins = pe.matmul(psum[:, 2, i * NE:(i + 1) * NE], zT[:, k, i * P:(i + 1) * P],
                                            gate[:, k, :], start=(k == 0), stop=(k == KD - 1))
                    ins.then_inc(logits_done, 1)
                pe.wait_ge(before_ready, 1)
                for k in range(TOPK):
                    out = psum[:, 4 + k, 0:NT * NE]
                    pe.matmul(out, count_in[:, 0:P], onehot[:, k].rearrange("p t e -> p (t e)"), start=True, stop=False)
                    pe.matmul(out, count_in[:, P:2 * P], before[:, k].rearrange("p t e -> p (t e)"),
                              start=False, stop=True).then_inc(places_done, 1)


def build(nc, a, upto=99):
    with ExitStack() as ctx:
        pr = Program(nc, ctx)
        psum = ctx.enter_context(nc.psum_tensor("banks", [P, 8, SEQ], F32))
        x_res = pr.sb("x_res", [P, NT, D])
        y_res = pr.sb("y_res", [P, NT, D])
        consts = pr.sb("consts", [P, P])
        ident_bf = pr.sb("ident_bf", [P, P], BF16)
        cst = {"ident": consts, "ident_bf": ident_bf}
        stats = {"stat": pr.sb("stat", [P, NT, 6]), "mean": pr.sb("mean", [P, NT]), "rstd": pr.sb("rstd", [P, NT]),
                 "tmp": pr.sb("tmp", [P, 3, NT])}
        stats2 = {"stat": pr.sb("stat2", [P, NT, 6]), "mean": pr.sb("mean2", [P, NT]),
                  "rstd": pr.sb("rstd2", [P, NT]), "tmp": pr.sb("tmp2", [P, 3, NT])}
        qk_parts = nc.dram_tensor("qk_parts", (2, 3, D, SEQ), BF16, kind="Internal").ap()
        slots_in = nc.dram_tensor("slots_in", (NE * CAP, D), F32, kind="Internal").ap()
        slots_out = nc.dram_tensor("slots_out", (NE * CAP, D), F32, kind="Internal").ap()

        x_in, zero_ready, zeroed, ident_ready = pr.sem("x_in"), pr.sem("zero_ready"), pr.sem("zeroed"), pr.sem("ident_ready")
        with ExitStack() as first:
            zero = pr.sb("zero", [P, 8 * D], F32, first)
            with nc.Block() as block:

                @block.sync
                def _(sp):
                    sp.dma_start(x_res[:], a["x"].rearrange("(t p) d -> p t d", p=P)).then_inc(x_in, 16)
                    sp.dma_start(consts[:], a["ident"]).then_inc(x_in, 16)
                    sp.wait_ge(x_in, 32)
                    sp.wait_ge(zero_ready, 1)
                    for r in range(8):
                        sp.dma_start(slots_in.rearrange("(r p j) d -> r p (j d)", p=P, r=8)[r], zero[:]
                                     ).then_inc(zeroed, 16)
                    sp.wait_ge(zeroed, 128)

                @block.vector
                def _(dve):
                    dve.memset(zero[:], 0.0).then_inc(zero_ready, 1)
                    dve.wait_ge(x_in, 32)
                    dve.tensor_copy(ident_bf[:], consts[:]).then_inc(ident_ready, 1)
                    dve.wait_ge(ident_ready, 1)

        if upto >= 1:
            statistics(pr, "sa_", x_res, stats, y_res, stats2)
            attention(pr, "a_", True, y_res, stats2,
                      {"qk": a["a_qk"], "v": a["a_v"], "o": a["a_o"], "rope": a["rope"], "gain": a["ln1"],
                       "window": a["window"]}, cst, psum, qk_parts)
            pr.end_layer()
        if upto >= 2:
            statistics(pr, "sf_", y_res, stats)
            swiglu(pr, "f_", x_res, y_res, stats, {"w1": a["w1"], "w3": a["w3"], "w2": a["w2"], "gain": a["ln2"]},
                   cst, psum)
            pr.end_layer()
        moe = {k: a[k] for k in ("gate", "count", "fc1", "fc2", "bias1", "bias2")}
        if upto >= 3:
            statistics(pr, "sm_", x_res, stats)
            experts(pr, "m_", x_res, y_res, stats, moe, cst, psum, slots_in, slots_out)
            pr.end_layer()
        if upto >= 4:
            statistics(pr, "sb_", x_res, stats)
            attention(pr, "b_", False, x_res, stats, {"qk": a["b_qk"], "v": a["b_v"], "o": a["b_o"]}, cst, psum,
                      qk_parts)
            pr.end_layer()
        if upto >= 5:
            statistics(pr, "sn_", x_res, stats)
            experts(pr, "n_", x_res, y_res, stats, moe, cst, psum, slots_in, slots_out)
            pr.end_layer()
        stored = pr.sem("stored")
        with nc.Block() as block:

            @block.sync
            def _(sp):
                sp.dma_start(a["out"].rearrange("(t p) d -> p t d", p=P), (y_res if upto == 1 else x_res)[:]).then_inc(stored, 16)
                sp.wait_ge(stored, 16)


def by_rows(m, k):
    return np.ascontiguousarray(m.reshape(k, P, -1).transpose(1, 0, 2))


def padded_heads(wo):
    out = np.zeros((NH, 2 * HD, D), wo.dtype)
    out[:, :HD] = wo.reshape(NH, HD, D)
    return by_rows(out.reshape(2 * NH * HD, D), NH // 4)


def padded(m, shape):
    out = np.zeros(shape, m.dtype)
    out[:m.shape[0], :m.shape[1]] = m
    return out


def shape_constants():
    f = 1.0 / np.float32(10000.0) ** (np.arange(0, HD, 2, dtype=np.float32) / np.float32(HD))
    angle = np.outer(np.arange(SEQ, dtype=np.float32), f.astype(np.float32)).astype(np.float32)
    cos, sin = np.cos(angle).astype(np.float32), np.sin(angle).astype(np.float32)
    d = np.arange(P) % HD
    rope = np.stack([cos[:, d // 2].T, np.where(d % 2 == 0, -1, 1)[:, None] * sin[:, d // 2].T], 1)
    p, c = np.arange(P)[:, None], np.arange(2 * P)[None, :]
    by_query = (c <= p + P) & (c >= p)
    by_key = (c >= p) & (c - p <= WINDOW)
    window = np.stack([np.tile(np.where(m, 0.0, MASKED), 2) for m in (by_query, by_key)], 1)
    before = (np.arange(P)[:, None] < np.arange(P)[None, :]).astype(np.float32)
    count = np.concatenate([before, np.ones((P, P)), np.tile(np.arange(NE), (P, 1))], 1)
    return {"rope": rope.astype(np.float32), "window": window.astype(np.float32), "count": count.astype(np.float32),
            "ident": np.eye(P, dtype=np.float32)}


def layouts(i):
    i = {k.replace("L0_", ""): np.asarray(v) for k, v in i.items()}
    swap = np.arange(D) ^ 1
    both = lambda g, b: np.ascontiguousarray(np.broadcast_to(np.stack([g, b])[None], (P, 2, D)))
    fc1 = i["ffn_fc1_w"].transpose(0, 2, 1).reshape(NE, KD, P, EH).transpose(0, 2, 1, 3)
    fc2 = i["ffn_fc2_w"].reshape(NE, KE, P, D).transpose(0, 2, 1, 3)
    wq, wk = i["attn_a_wq"], i["attn_a_wk"]
    return {
        "x": i["attn_a_x"].reshape(NTOK, D),
        "a_qk": by_rows(np.concatenate([wq, wq[:, swap], wk, wk[:, swap]], 1), KD),
        "a_v": by_rows(i["attn_a_wv"], KD), "a_o": padded_heads(i["attn_a_wo"]),
        "ln1": both(i["attn_a_ln1_g"], i["attn_a_ln1_b"]), "ln2": both(i["attn_a_ln2_g"], i["attn_a_ln2_b"]),
        "w1": by_rows(padded(i["attn_a_w1"], (D, HIDP)), KD), "w3": by_rows(padded(i["attn_a_w3"], (D, HIDP)), KD),
        "w2": by_rows(padded(i["attn_a_w2"], (HIDP, D)), KH),
        "b_qk": by_rows(np.concatenate([i["attn_b_w_q"].T, i["attn_b_w_k"].T], 1), KD),
        "b_v": by_rows(i["attn_b_w_v"].T, KD), "b_o": padded_heads(i["attn_b_w_o"].T),
        "gate": by_rows(i["ffn_gate_w"].T, KD),
        "fc1": np.ascontiguousarray(fc1), "fc2": np.ascontiguousarray(fc2),
        "bias1": np.ascontiguousarray(i["ffn_fc1_b"].reshape(NE, KE, P).transpose(2, 0, 1)),
        "bias2": np.ascontiguousarray(np.broadcast_to(i["ffn_fc2_b"].reshape(1, NE, D), (P, NE, D))),
        **shape_constants(),
    }


def kernel(**inputs):
    import concourse.bacc as bacc
    from concourse.bass_utils import run_bass_kernel_spmd

    nc = bacc.Bacc("TRN2", target_bir_lowering=False, num_devices=1)
    arrays = {f"in_{k}": v for k, v in layouts(inputs).items()}
    aps = {k[3:]: nc.dram_tensor(k, v.shape, F32, kind="ExternalInput").ap() for k, v in arrays.items()}
    aps["out"] = nc.dram_tensor("out", (NTOK, D), F32, kind="ExternalOutput").ap()
    build(nc, aps)
    r = run_bass_kernel_spmd(nc, [arrays], core_ids=[0])
    return r.results[0]["out"].reshape(NSEQ, SEQ, D)
```

```python
from contextlib import ExitStack

import numpy as np

import concourse.bass as bass
from concourse import mybir

ALU = mybir.AluOpType
ACT = mybir.ActivationFunctionType
AX = mybir.AxisListType
F32 = mybir.dt.float32
BF16 = mybir.dt.bfloat16
U32 = mybir.dt.uint32

P = 128
NSEQ, SEQ, D = 8, 512, 256
NTOK = NSEQ * SEQ
NT = NTOK // P
TPS = SEQ // P
KD = D // P
NH, HD = 16, 16
SCALE = HD ** -0.5
WINDOW = 128
EPS = 1e-5
HID, HIDP = 704, 768
KH = HIDP // P
NE, TOPK, EH = 8, 2, 1024
CAP = TOPK * ((NTOK + NE - 1) // NE)
KE = EH // P
MASKED = -(2.0 ** 127)
Q_PARTS = (0, 0, 1, 1, 0, 2)
K_PARTS = (0, 1, 0, 1, 2, 0)
NPROD = len(Q_PARTS)
SROWS = NPROD * HD


class Program:

    def __init__(self, nc, ctx):
        self.nc, self.ctx, self.prefix, self.sems = nc, ctx, "", []

    def sem(self, name):
        self.sems.append(self.nc.alloc_semaphore(name=self.prefix + name))
        return self.sems[-1]

    def end_layer(self):
        self.nc.clear_and_free_semaphores(self.sems)
        self.nc.all_engine_barrier()
        self.sems = []

    def sb(self, name, shape, dt=F32, ctx=None):
        return (ctx or self.ctx).enter_context(self.nc.sbuf_tensor(self.prefix + name, shape, dt))


class Chain:

    def __init__(self, eng, sem, per=0, it=None, start=0):
        self.eng, self.sem, self.base, self.k, self.per = eng, sem, start, 0, per
        self.it = it

    def value(self):
        n = self.base + self.k
        return n if self.it is None else self.it * self.per + n

    def __call__(self, ins):
        ins.then_inc(self.sem, 1)
        self.k += 1
        self.eng.wait_ge(self.sem, self.value())


class LoopChain(Chain):

    def __init__(self, eng, sem):
        super().__init__(eng, sem)

    def start(self, it, per, base):
        self.it, self.per, self.base, self.k = it, per, 0, base


def rstd_steps(link, dve, act_sqrt, stat, mean, rstd, tmp, sq_done):
    me, mo = stat[:, :, 1], stat[:, :, 4]
    link(dve.tensor_tensor(mean[:, :], me, mo, ALU.add))
    link(dve.tensor_scalar(mean[:, :], mean[:, :], 0.5, None, ALU.mult))
    link(dve.tensor_tensor(tmp[:, 0, :], me, mo, ALU.subtract))
    link(dve.tensor_tensor(tmp[:, 0, :], tmp[:, 0, :], tmp[:, 0, :], ALU.mult))
    link(dve.tensor_tensor(tmp[:, 1, :], stat[:, :, 2], stat[:, :, 5], ALU.add))
    link(dve.tensor_scalar(tmp[:, 1, :], tmp[:, 1, :], 1.0 / D, EPS, ALU.mult, ALU.add))
    act_sqrt(dve.scalar_tensor_tensor(out=tmp[:, 1, :], in0=tmp[:, 0, :], scalar=0.25, in1=tmp[:, 1, :],
                                      op0=ALU.mult, op1=ALU.add))
    sq_done()
    link(dve.reciprocal(rstd[:, :], tmp[:, 2, :]))
    link(dve.tensor_tensor(tmp[:, 0, :], rstd[:, :], rstd[:, :], ALU.mult))
    link(dve.tensor_tensor(tmp[:, 0, :], tmp[:, 0, :], tmp[:, 1, :], ALU.mult))
    link(dve.tensor_scalar(tmp[:, 0, :], tmp[:, 0, :], -0.5, 1.5, ALU.mult, ALU.add))
    link(dve.tensor_tensor(rstd[:, :], rstd[:, :], tmp[:, 0, :], ALU.mult))


def statistics(pr, name, src, stats, normalised=None, stat_of_normalised=None):
    nc = pr.nc
    pr.prefix = name
    chain, var_ready, sqrt_ready = pr.sem("chain"), pr.sem("var_ready"), pr.sem("sqrt_ready")
    rows_ready = pr.sem("rows_ready")
    rounds = [(src, stats)] + ([(normalised, stat_of_normalised)] if normalised is not None else [])
    with nc.Block() as block:

        @block.scalar
        def _(act):
            for n, (_, st) in enumerate(rounds):
                act.wait_ge(var_ready, n + 1)
                act.activation(st["tmp"][:, 2, :], st["tmp"][:, 1, :], ACT.Sqrt).then_inc(sqrt_ready, 1)

        @block.vector
        def _(dve):
            link = Chain(dve, chain)
            for n, (rows, st) in enumerate(rounds):
                with dve.Fori(0, NSEQ) as b:
                    for i in range(TPS):
                        last = dve.bn_stats(st["stat"][:, bass.ds(b * TPS + i, 1), :].rearrange("p o c -> p (o c)"),
                                            rows[:, bass.ds(b * TPS + i, 1), :].rearrange("p o c -> p (o c)"))
                    last.then_inc(rows_ready, 1)
                dve.wait_ge(rows_ready, NSEQ * (2 * n + 1))

                def to_sqrt(ins, n=n):
                    ins.then_inc(var_ready, 1)

                def sqrt_back(n=n):
                    dve.wait_ge(sqrt_ready, n + 1)

                rstd_steps(link, dve, to_sqrt, st["stat"], st["mean"], st["rstd"], st["tmp"], sqrt_back)
                if n + 1 < len(rounds):
                    with dve.Fori(0, NSEQ) as b:
                        for i in range(TPS):
                            t = b * TPS + i
                            last = dve.tensor_scalar(normalised[:, bass.ds(t, 1), :], rows[:, bass.ds(t, 1), :],
                                                     st["mean"][:, bass.ds(t, 1)], st["rstd"][:, bass.ds(t, 1)],
                                                     ALU.subtract, ALU.mult)
                        last.then_inc(rows_ready, 1)
                    dve.wait_ge(rows_ready, NSEQ * (2 * n + 2))


def attention_plan(windowed):
    NJ = 8 if windowed else 4
    rounds = 4 if windowed else 8
    per_group = rounds // 4
    units = 8 if windowed else 16
    second = []
    for r in range(rounds):
        second += [("S", 4 * r + s, 0) for s in range(4)]
        if r > per_group and r % per_group == 0:
            second.insert(-1, ("H", r // per_group - 2, 0))
        if r:
            second.append(("O", r - 1, 0))
    maxima = []
    for i in range(TPS):
        for m in range(units):
            maxima.append(("M", i * units + m, 1))
            if i and m == units // 2:
                maxima.append(("N", i - 1, 1))
    ahead = [("T", 0, 2), ("T", 1, 2)]
    project = [("J", j, 2) for j in range(NJ)]
    tail = [("H", 2, 0), ("O", rounds - 1, 0), ("H", 3, 0), ("G", 0, 0), ("G", 1, 0), ("W", 0, 0), ("W", 1, 0)]
    project = ahead + project
    plan = [("Z", 0, 2), ("V", 0, 1), ("V", 1, 1)]
    late = 6
    early, rest = maxima[:len(maxima) - 2 * late], maxima[len(maxima) - 2 * late:]
    first = len(second) // 6
    taken = 0
    for n, unit in enumerate(second):
        plan.append(unit)
        if n >= 3 and project and (windowed or n % 2):
            plan.append(project.pop(0))
        want = len(early) * max(0, n + 1 - first) // (len(second) - first)
        plan += early[taken:want]
        taken = want
    for unit in tail:
        plan += rest[:2]
        rest = rest[2:]
        plan.append(unit)
    plan += rest + [("N", TPS - 1, 1)]
    return plan


def attention(pr, name, windowed, src, stats, w, cst, psum, qk_parts):
    nc = pr.nc
    pr.prefix = name
    NPJ = 2 * KD
    UPT = 8 if windowed else 16
    MU = TPS * UPT + TPS
    RND = 4 if windowed else 8
    RPG = RND // 4
    SU = 4 * RND
    NJ = 8 if windowed else 4
    step_plan = attention_plan(windowed)
    only = lambda *ds: [u for u in step_plan if u[2] in ds]
    shift = lambda plan, d: [(k, n, x + d) for k, n, x in plan]
    ahead_of_all = shift(only(2), -2) + shift([u for u in only(1) if u[0] == "V"], -1) + shift(only(2), -1) \
        + shift([u for u in only(1) if u[0] != "V"], -1)
    BANK7 = "TJVHGW"
    x_units = lambda plan: sum(k in BANK7 for k, _, _ in plan)
    LINKS = {"J": 2, "H": 1}
    links = lambda plan: sum(LINKS.get(k, 0) + 4 * (k == "M" and n % UPT == UPT - 1) for k, n, _ in plan)

    def first(it, c):
        return type(it) is int and it == 0 and c == 0

    def order(eng, unit, link=None):
        per = x_units(step_plan)

        def steps(plan, it, c, x, looped=False):
            for kind, n, d in plan:
                unit(kind, n, it, c + d, it * (2 * per) + x if looped else x)
                x += kind in BANK7
            return x

        x0 = x = x_units(ahead_of_all)
        if link:
            link.start(None, 0, 0)
        steps(ahead_of_all, 0, 0, 0)
        with eng.Fori(0, NSEQ // 2 - 1) as it:
            if link:
                link.start(it, 2 * links(step_plan), links(ahead_of_all))
            for c in range(2):
                x = steps(step_plan, it, c, x, looped=True)
            if link:
                assert link.k == links(ahead_of_all) + link.per, (link.k, link.per)
        it = NSEQ // 2 - 1
        x = x0 + per * (NSEQ - 2)
        if link:
            link.start(None, 0, links(ahead_of_all) + links(step_plan) * (NSEQ - 2))
        x = steps(only(0, 1), it, 0, x)
        steps(only(0), it, 1, x)

    with ExitStack() as ctx:
        sb = lambda n, s, d=F32: pr.sb(n, s, d, ctx)
        wqk = sb("wqk", [P, KD, w["qk"].shape[-1]])
        wv = sb("wv", [P, KD, D])
        wo = sb("wo", [P, KD, D])
        z = sb("z", [P, TPS, D])
        zT = sb("zT", [P, 2, KD, SEQ])
        rows = sb("rows", [P, 3, SEQ])
        parts = sb("parts", [P, 2, 3, SEQ], BF16)
        q_stack = sb("q_stack", [P, 2, NH, SEQ], BF16)
        k_stack = sb("k_stack", [P, 2, NH, SEQ], BF16)
        v_ones = sb("v_ones", [P, 2, TPS, NH, 2 * HD])
        probs = sb("probs", [P, 2, 4, 2 * SEQ])
        row_max = sb("row_max", [P, TPS, NH])
        neg_max = sb("neg_max", [P, 2, NH])
        neg_parts = sb("neg_parts", [P, TPS, 3, NH], BF16)
        maxT = sb("maxT", [3 * NH, SEQ], BF16)
        headsT = sb("headsT", [P, 2, SEQ])
        recip = sb("recip", [P, TPS, 4])
        heads = sb("heads", [P, TPS, D])
        catT = sb("catT", [P, KD, SEQ])
        if windowed:
            rope = sb("rope", [P, 2, SEQ])
            gain = sb("gain", [P, 2, D])
            window_bf = sb("window_bf", [P, 2, SEQ], BF16)

        weights_in = pr.sem("weights_in")
        setup_done, window_ready = pr.sem("setup_done"), pr.sem("window_ready")
        passed = pr.sem("passed")
        z_normed, z_scaled, z_ready, z_turned = (pr.sem("z_normed"), pr.sem("z_scaled"), pr.sem("z_ready"),
                                                 pr.sem("z_turned"))
        x_done, x_free = pr.sem("bank7_done"), pr.sem("bank7_read")
        zT_ready, v_ready = pr.sem("zT_ready"), pr.sem("v_ready")
        turned_rows_ready = pr.sem("rotated_ready")
        parts_ready = pr.sem("parts_ready")
        parts_out = [pr.sem(f"parts_out{g}") for g in range(2)]
        stack_in = [[pr.sem(f"q_stack_in{s}"), pr.sem(f"k_stack_in{s}")] for s in range(2)]
        scores_done, max_done = pr.sem("scores_done"), pr.sem("max_done")
        neg_ready = pr.sem("neg_ready")
        max_in = [pr.sem("max_in0"), pr.sem("max_in1")]
        scoresT_done, probs_ready, values_done = pr.sem("scoresT_done"), pr.sem("probs_ready"), pr.sem("values_done")
        headsT_ready, heads_ready, catT_ready, out_added = (pr.sem("headsT_ready"), pr.sem("heads_ready"),
                                                            pr.sem("catT_ready"), pr.sem("out_added"))
        chain = pr.sem("chain")
        NW = 6 if windowed else 3

        with nc.Block() as block:

            @block.sync
            def _(sp):
                sp.dma_start(wqk[:], w["qk"]).then_inc(weights_in, 16)
                sp.dma_start(wv[:], w["v"]).then_inc(weights_in, 16)
                sp.dma_start(wo[:], w["o"]).then_inc(weights_in, 16)
                if windowed:
                    sp.dma_start(rope[:], w["rope"]).then_inc(weights_in, 16)
                    sp.dma_start(gain[:], w["gain"]).then_inc(weights_in, 16)
                    sp.dma_start(rows[:, 0:2, :], w["window"]).then_inc(weights_in, 16)

                def store_parts(g, it, c):
                    sp.wait_ge(parts_ready, (it * 2 + c) * NPJ + g + 1)
                    sp.dma_start(qk_parts[c % 2, g // KD, :, g % KD * P:(g % KD + 1) * P, :
                                          ].rearrange("c p t -> p c t"), parts[:, g % 2]).then_inc(parts_out[g % 2], 16)

                def load_stacks(it, c):
                    s = c % 2
                    for g in range(2):
                        sp.wait_ge(parts_out[g], (it * 2 + c) * 32 + 32)
                    for qk in range(2):
                        stack = (q_stack, k_stack)[qk]
                        for n in range(NPROD):
                            part = (Q_PARTS, K_PARTS)[qk][n]
                            sp.dma_start(stack[n * HD:(n + 1) * HD, s],
                                         qk_parts[s, qk, part].rearrange("(h d) t -> d h t", d=HD)
                                         ).then_inc(stack_in[s][qk], 16)

                def load_max(it, c):
                    sp.wait_ge(max_done, (it * 2 + c) * MU + MU)
                    for k in range(3):
                        sp.dma_start(q_stack[SROWS + k:SROWS + k + 1, c % 2],
                                     maxT[k * NH:(k + 1) * NH, :]).then_inc(max_in[c % 2], 16)

                def step(it, c, project=True, maxima=True):
                    if maxima:
                        sp.wait_ge(scoresT_done, (it * 2 + c) * SU + 1)
                        load_stacks(it, c + 1)
                    if project:
                        for qk in range(2):
                            sp.wait_ge(stack_in[c % 2][qk], (it + c // 2) * 96 + 96)
                        for g in range(NPJ):
                            store_parts(g, it, c + 2)
                    if maxima:
                        load_max(it, c + 1)

                for g in range(NPJ):
                    store_parts(g, 0, 0)
                load_stacks(0, 0)
                for g in range(NPJ):
                    store_parts(g, 0, 1)
                load_max(0, 0)
                with sp.Fori(0, NSEQ // 2 - 1) as it:
                    step(it, 0)
                    step(it, 1)
                step(NSEQ // 2 - 1, 0, project=False)

            @block.gpsimd
            def _(pool):
                pool.memset(v_ones[:, :, :, :, HD:], 1.0).then_inc(setup_done, 1)
                pool.wait_ge(setup_done, 1)
                pool.memset(k_stack[SROWS:SROWS + 32, :, :, :], 1.0).then_inc(setup_done, 1)
                pool.wait_ge(setup_done, 2)
                if windowed:
                    pool.wait_ge(weights_in, 16 * NW)
                    with pool.Fori(0, NSEQ) as b:
                        pool.wait_ge(z_normed, b + 1)
                        for i in range(TPS):
                            ins = pool.tensor_tensor(z[:, i, :], z[:, i, :], gain[:, 0, :], ALU.mult)
                        ins.then_inc(z_scaled, 1)
                        pool.wait_ge(z_scaled, b + 1)
                        for i in range(TPS):
                            ins = pool.tensor_tensor(z[:, i, :], z[:, i, :], gain[:, 1, :], ALU.add)
                        ins.then_inc(z_ready, 1)

            @block.scalar
            def _(act):
                def unit(kind, n, it, c, x):
                    b = it * 2 + c
                    if kind == "T":
                        act.wait_ge(x_done, x + 1)
                        act.activation(zT[:, c % 2, n, :], psum[:, 7, :], ACT.Copy).then_inc(x_free, 1)
                    elif kind == "V":
                        act.wait_ge(x_done, x + 1)
                        act.activation(v_ones[:, c % 2, 2 * n:2 * n + 2, :, 0:HD],
                                       psum[:, 7, :].rearrange("p (i h d) -> p i h d", i=2, h=NH),
                                       ACT.Copy).then_inc(x_free, 1)
                    elif kind == "S":
                        r, s = n // 4, n % 4
                        act.wait_ge(scoresT_done, b * SU + n + 2)
                        if r >= 2:
                            act.wait_ge(values_done, b * RND + r - 1)
                        act.activation(probs[:, r % 2, s, :],
                                       psum[:, 2 + 2 * (n % 2):4 + 2 * (n % 2), :].rearrange("p a c -> p (a c)"),
                                       ACT.Exp, scale=SCALE).then_inc(probs_ready, 1)
                    elif kind == "O" and n % RPG == RPG - 1:
                        act.wait_ge(values_done, b * RND + n + 1)
                        act.activation(headsT[:, n // RPG % 2, :], psum[:, 6, :], ACT.Copy).then_inc(headsT_ready, 1)
                    elif kind == "G":
                        act.wait_ge(x_done, x + 1)
                        act.activation(catT[:, n, :], psum[:, 7, :], ACT.Copy).then_inc(x_free, 1)

                order(act, unit)

            @block.vector
            def _(dve):
                if windowed:
                    dve.wait_ge(weights_in, 16 * NW)
                    dve.tensor_copy(window_bf[:], rows[:, 0:2, :]).then_inc(window_ready, 1)
                    dve.wait_ge(window_ready, 1)
                link = LoopChain(dve, chain)

                def split(whole, g, b, read):
                    slot = parts[:, g % 2]
                    link(dve.tensor_copy(slot[:, 0, :], whole))
                    read(dve.tensor_tensor(rows[:, 0, :], whole, slot[:, 0, :], ALU.subtract))
                    link(dve.tensor_copy(slot[:, 1, :], rows[:, 0, :]))
                    dve.tensor_tensor(slot[:, 2, :], rows[:, 0, :], slot[:, 1, :], ALU.subtract
                                      ).then_inc(parts_ready, 1)
                    dve.wait_ge(parts_ready, b * NPJ + g + 1)

                def unit(kind, n, it, c, x):
                    b = it * 2 + c
                    if kind == "Z":
                        for i in range(TPS):
                            t = b * TPS + i
                            ins = dve.tensor_scalar(z[:, i:i + 1, :], src[:, bass.ds(t, 1), :],
                                                    stats["mean"][:, bass.ds(t, 1)], stats["rstd"][:, bass.ds(t, 1)],
                                                    ALU.subtract, ALU.mult)
                        ins.then_inc(z_normed, 1)
                    elif kind == "J":
                        g = n // 2 if windowed else n
                        dve.wait_ge(x_done, x + 1)
                        if windowed and n % 2 == 0:
                            dve.tensor_tensor(rows[:, 1, :], psum[:, 7, :], rope[:, 0, :], ALU.mult
                                              ).then_inc(x_free, 1)
                            return
                        if windowed:
                            link_free = dve.tensor_tensor(rows[:, 2, :], psum[:, 7, :], rope[:, 1, :], ALU.mult)
                            link_free.then_inc(x_free, 1)
                            dve.wait_ge(x_free, x + 1)
                            link(dve.tensor_tensor(rows[:, 1, :], rows[:, 1, :], rows[:, 2, :], ALU.add))
                            whole, read = rows[:, 1, :], link
                        else:
                            def read(ins):
                                ins.then_inc(x_free, 1)
                                dve.wait_ge(x_free, x + 1)
                            whole = psum[:, 7, :]
                        if g >= 2 or not first(it, c):
                            dve.wait_ge(parts_out[g % 2], b * 32 + g // 2 * 16)
                        split(whole, g, b, read)
                    elif kind == "M":
                        i = n // UPT
                        k = n + max(i - 1, 0) + (1 if i and n % UPT > UPT // 2 else 0)
                        dve.wait_ge(scores_done, b * MU + k + 1)
                        if windowed:
                            h = 2 * (n % UPT)
                            lo = WINDOW if i == 0 else 0
                            scores = psum[:, k % 2, :].rearrange("p (h c) -> p h c", h=2)[:, :, lo:]
                            ins = dve.tensor_reduce(row_max[:, i, h:h + 2], scores, AX.X, ALU.max)
                        else:
                            h = n % UPT
                            ins = dve.tensor_reduce(row_max[:, i, h:h + 1], psum[:, k % 2, :], AX.X, ALU.max)
                        ins.then_inc(max_done, 1)
                        if n % UPT == UPT - 1:
                            dve.wait_ge(max_done, b * MU + k + 1)
                            link(dve.tensor_scalar(neg_max[:, 0, :], row_max[:, i, :], -1.0, None, ALU.mult))
                            link(dve.tensor_copy(neg_parts[:, i, 0, :], neg_max[:, 0, :]))
                            link(dve.tensor_tensor(neg_max[:, 1, :], neg_max[:, 0, :], neg_parts[:, i, 0, :],
                                                   ALU.subtract))
                            link(dve.tensor_copy(neg_parts[:, i, 1, :], neg_max[:, 1, :]))
                            dve.tensor_tensor(neg_parts[:, i, 2, :], neg_max[:, 1, :], neg_parts[:, i, 1, :],
                                              ALU.subtract).then_inc(neg_ready, 1)
                            dve.wait_ge(neg_ready, b * TPS + i + 1)
                    elif kind == "N":
                        k = (n + 1) * UPT + n + (UPT // 2 + 1 if n < TPS - 1 else 0)
                        dve.wait_ge(scores_done, b * MU + k + 1)
                        dve.tensor_copy(maxT[:, n * P:(n + 1) * P],
                                        psum[:, k % 2, :].bitcast(BF16)[0:3 * NH, 0:P]).then_inc(max_done, 1)
                    elif kind == "H":
                        dve.wait_ge(x_done, x + 1)
                        by_token = psum[:, 7, :].rearrange("p (i h d) -> p i h d", i=TPS, h=4)
                        link(dve.reciprocal(recip[:], by_token[:, :, :, HD]))
                        out = heads[:, :, n * 4 * HD:(n + 1) * 4 * HD].rearrange("p i (h d) -> p i h d", h=4)
                        dve.tensor_tensor(out, by_token[:, :, :, 0:HD],
                                          recip[:].rearrange("p i (h o) -> p i h o", o=1).broadcast_to((P, TPS, 4, HD)),
                                          ALU.mult).then_inc(x_free, 1)
                        dve.wait_ge(x_free, x + 1)
                    elif kind == "W":
                        dve.wait_ge(x_done, x + 1)
                        res = src[:, bass.ds(b * TPS + 2 * n, 2), :]
                        dve.tensor_tensor(res, psum[:, 7, :].rearrange("p (i c) -> p i c", i=2), res,
                                          ALU.add).then_inc(x_free, 1)

                order(dve, unit, link)
                dve.tensor_copy(recip[:, 0, 0:1], row_max[:, 0, 0:1]).then_inc(out_added, 1)
                dve.wait_ge(out_added, 1)

            @block.tensor
            def _(pe):
                pe.wait_ge(weights_in, 16 * NW)
                pe.wait_ge(setup_done, 2)
                if windowed:
                    pe.wait_ge(window_ready, 1)
                pe.sem_inc(scoresT_done, 1)
                bank7 = psum[:, 7, :]

                def bank7_free(x):
                    if not (type(x) is int and x == 0):
                        pe.wait_ge(x_free, x)

                def unit(kind, n, it, c, x):
                    b = it * 2 + c
                    s = c % 2
                    if kind == "T":
                        if n == 0:
                            pe.wait_ge(z_ready if windowed else z_normed, b + 1)
                        bank7_free(x)
                        for i in range(TPS):
                            ins = pe.transpose(bank7[:, i * P:(i + 1) * P], z[:, i, n * P:(n + 1) * P],
                                               cst["ident"][:])
                        ins.then_inc(x_done, 1)
                    elif kind == "J":
                        g, swapped = (n // 2, n % 2) if windowed else (n, 0)
                        col = (g // KD * (2 if windowed else 1) + swapped) * D + (g % KD) * P
                        bank7_free(x)
                        for k in range(KD):
                            ins = pe.matmul(bank7, wqk[:, k, col:col + P], zT[:, s, k, :],
                                            start=(k == 0), stop=(k == KD - 1))
                        ins.then_inc(x_done, 1)
                    elif kind == "V":
                        bank7_free(x)
                        for i in range(2):
                            for k in range(KD):
                                ins = pe.matmul(bank7[:, i * D:(i + 1) * D],
                                                zT[:, s, k, (2 * n + i) * P:(2 * n + i + 1) * P], wv[:, k, :],
                                                start=(k == 0), stop=(k == KD - 1))
                        ins.then_inc(x_done, 1)
                    elif kind == "M":
                        i = n // UPT
                        k = n + max(i - 1, 0) + (1 if i and n % UPT > UPT // 2 else 0)
                        if n == 0:
                            for qk in range(2):
                                pe.wait_ge(stack_in[s][qk], (it + c // 2) * 96 + 96)
                        if k >= 2 or not first(it, c):
                            pe.wait_ge(max_done, b * MU + k - 1)
                        bank = psum[:, k % 2, :]
                        if windowed:
                            pe.matmul(bank, cst["ident_bf"][:], window_bf[:, 0, :], start=True, stop=False)
                            for m in range(2):
                                h = 2 * (n % UPT) + m
                                lo = 0 if i else WINDOW
                                ins = pe.matmul(bank[:, 2 * m * P + lo:2 * (m + 1) * P],
                                                q_stack[0:SROWS, s, h, i * P:(i + 1) * P],
                                                k_stack[0:SROWS, s, h, (i - 1) * P + lo:(i + 1) * P],
                                                start=False, stop=(m == 1))
                        else:
                            ins = pe.matmul(bank, q_stack[0:SROWS, s, n % UPT, i * P:(i + 1) * P],
                                            k_stack[0:SROWS, s, n % UPT, :], start=True, stop=True)
                        ins.then_inc(scores_done, 1)
                    elif kind == "N":
                        k = (n + 1) * UPT + n + (UPT // 2 + 1 if n < TPS - 1 else 0)
                        pe.wait_ge(max_done, b * MU + k - 1)
                        pe.wait_ge(neg_ready, b * TPS + n + 1)
                        pe.sem_inc(passed, 1)
                        pe.transpose(psum[:, k % 2, :].bitcast(BF16)[0:3 * NH, 0:P],
                                     neg_parts[:, n].rearrange("p c h -> p (c h)"),
                                     cst["ident_bf"][:]).then_inc(scores_done, 1)
                    elif kind == "S":
                        h = n // 4 // RPG * 4 + n % 4
                        if n == 0:
                            pe.wait_ge(max_in[s], (it + c // 2) * 48 + 48)
                        if n >= 2:
                            pe.wait_ge(probs_ready, b * SU + n - 1)
                        for a in range(2):
                            bank = psum[:, 2 + 2 * (n % 2) + a, :]
                            if windowed:
                                pe.matmul(bank, cst["ident_bf"][:], window_bf[:, 1, :], start=True, stop=False)
                                for m in range(2):
                                    j = 2 * a + m
                                    w_ = min(2 * P, SEQ - j * P)
                                    ins = pe.matmul(bank[:, 2 * m * P:2 * m * P + w_],
                                                    k_stack[0:SROWS + 3, s, h, j * P:(j + 1) * P],
                                                    q_stack[0:SROWS + 3, s, h, j * P:j * P + w_],
                                                    start=False, stop=(m == 1))
                            else:
                                j = 2 * (n // 4 % 2) + a
                                ins = pe.matmul(bank, k_stack[0:SROWS + 3, s, h, j * P:(j + 1) * P],
                                                q_stack[0:SROWS + 3, s, h, :], start=True, stop=True)
                        ins.then_inc(scoresT_done, 1)
                    elif kind == "O":
                        g = n // RPG
                        pe.wait_ge(probs_ready, b * SU + 4 * n + 4)
                        if g >= 1 and n % RPG == 0:
                            pe.wait_ge(headsT_ready, b * 4 + g)
                        if windowed:
                            for i in range(TPS):
                                for j in range(max(i - 1, 0), i + 1):
                                    for q in range(4):
                                        at = 2 * P * j + P * (i - j)
                                        ins = pe.matmul(psum[32 * q:32 * q + 32, 6, i * P:(i + 1) * P],
                                                        v_ones[:, s, j, 4 * g + q, :], probs[:, n % 2, q, at:at + P],
                                                        start=(j == max(i - 1, 0)), stop=(j == i))
                        else:
                            for a in range(2):
                                j = 2 * (n % 2) + a
                                for q in range(4):
                                    ins = pe.matmul(psum[32 * q:32 * q + 32, 6, :], v_ones[:, s, j, 4 * g + q, :],
                                                    probs[:, n % 2, q, a * SEQ:(a + 1) * SEQ],
                                                    start=(j == 0), stop=(j == TPS - 1))
                        ins.then_inc(values_done, 1)
                    elif kind == "H":
                        pe.wait_ge(headsT_ready, b * 4 + n + 1)
                        bank7_free(x)
                        for i in range(TPS):
                            ins = pe.transpose(bank7[:, i * P:(i + 1) * P], headsT[:, n % 2, i * P:(i + 1) * P],
                                               cst["ident"][:])
                        ins.then_inc(x_done, 1)
                    elif kind == "G":
                        bank7_free(x)
                        for i in range(TPS):
                            ins = pe.transpose(bank7[:, i * P:(i + 1) * P], heads[:, i, n * P:(n + 1) * P],
                                               cst["ident"][:])
                        ins.then_inc(x_done, 1)
                    elif kind == "W":
                        bank7_free(x)
                        for i in range(2):
                            for k in range(KD):
                                ins = pe.matmul(bank7[:, i * D:(i + 1) * D],
                                                catT[:, k, (2 * n + i) * P:(2 * n + i + 1) * P], wo[:, k, :],
                                                start=(k == 0), stop=(k == KD - 1))
                        ins.then_inc(x_done, 1)

                order(pe, unit)


def swiglu(pr, name, x_dram, h_res, stats, w, cst, psum):
    nc = pr.nc
    pr.prefix = name
    with ExitStack() as ctx:
        sb = lambda n, s, d=F32: pr.sb(n, s, d, ctx)
        w1, w3, w2 = sb("w1", [P, KD, HIDP]), sb("w3", [P, KD, HIDP]), sb("w2", [P, KH, D])
        gain = sb("gain", [P, 2, D])
        z = sb("z", [P, TPS, D])
        zT = sb("zT", [P, KD, SEQ])
        th = sb("th", [P, 2, SEQ])
        act_gate = sb("act_gate", [P, 2, SEQ])
        hidT = sb("hidT", [P, KH, SEQ])
        block_out = sb("block_out", [P, 2, 2 * D])
        x_rows = sb("x_rows", [P, 2, TPS, D])
        weights_in = pr.sem("weights_in")
        z_normed, z_scaled, z_ready = pr.sem("z_normed"), pr.sem("z_scaled"), pr.sem("z_ready")
        z_turned, zT_ready = pr.sem("z_turned"), pr.sem("zT_ready")
        up_done, tanh_ready, gate_ready, hid_ready = (pr.sem("up_done"), pr.sem("tanh_ready"), pr.sem("gate_ready"),
                                                      pr.sem("hid_ready"))
        down_done, down_read, added = pr.sem("down_done"), pr.sem("down_read"), pr.sem("added")
        x_in = [pr.sem("x_in0"), pr.sem("x_in1")]
        with nc.Block() as block:

            @block.sync
            def _(sp):
                for dst, s in ((w1, w["w1"]), (w3, w["w3"]), (w2, w["w2"]), (gain, w["gain"])):
                    sp.dma_start(dst[:], s).then_inc(weights_in, 16)

                def load_x(b, s):
                    sp.dma_start(x_rows[:, s], x_dram[bass.ds(b * SEQ, SEQ), :].rearrange("(i p) d -> p i d", p=P)
                                 ).then_inc(x_in[s], 16)

                for s in range(2):
                    load_x(s, s)
                with sp.Fori(0, NSEQ // 2 - 1) as it:
                    for c in range(2):
                        sp.wait_ge(added, (it * 2 + c) * 2 + 2)
                        load_x(it * 2 + c + 2, c)

            @block.gpsimd
            def _(pool):
                pool.wait_ge(weights_in, 64)
                with pool.Fori(0, NSEQ // 2) as it:
                  for c in range(2):
                    b = it * 2 + c
                    pool.wait_ge(z_normed, b + 1)
                    for i in range(TPS):
                        ins = pool.tensor_tensor(z[:, i, :], z[:, i, :], gain[:, 0, :], ALU.mult)
                    ins.then_inc(z_scaled, 1)
                    pool.wait_ge(z_scaled, b + 1)
                    for i in range(TPS):
                        ins = pool.tensor_tensor(z[:, i, :], z[:, i, :], gain[:, 1, :], ALU.add)
                    ins.then_inc(z_ready, 1)
                    pool.wait_ge(x_in[c], it * 16 + 16)
                    for o in range(2):
                        pool.wait_ge(down_read, b * 2 + o + 1)
                        pool.tensor_tensor(h_res[:, bass.ds(b * TPS + 2 * o, 2), :],
                                           block_out[:, o, :].rearrange("p (i c) -> p i c", i=2),
                                           x_rows[:, c, 2 * o:2 * o + 2, :], ALU.add).then_inc(added, 1)
                pool.wait_ge(added, 2 * NSEQ)

            @block.scalar
            def _(act):
                with act.Fori(0, NSEQ) as b:
                    for k in range(KD):
                        act.wait_ge(z_turned, b * KD + k + 1)
                        act.activation(zT[:, k, :], psum[:, k, :], ACT.Copy).then_inc(zT_ready, 1)
                    for m in range(KH):
                        act.wait_ge(up_done, b * KH + m + 1)
                        if m >= 2:
                            act.wait_ge(gate_ready, b * KH + m - 1)
                        act.activation(th[:, m % 2, :], psum[:, 2 + 2 * (m % 2), :], ACT.Tanh,
                                       scale=0.5).then_inc(tanh_ready, 1)

            @block.vector
            def _(dve):
                with dve.Fori(0, NSEQ) as b:
                    for i in range(TPS):
                        t = b * TPS + i
                        ins = dve.tensor_scalar(z[:, i:i + 1, :], h_res[:, bass.ds(t, 1), :],
                                                stats["mean"][:, bass.ds(t, 1)], stats["rstd"][:, bass.ds(t, 1)],
                                                ALU.subtract, ALU.mult)
                    ins.then_inc(z_normed, 1)
                    for m in range(KH):
                        dve.wait_ge(tanh_ready, b * KH + m + 1)
                        if m >= 2:
                            dve.wait_ge(hid_ready, b * KH + m - 1)
                        dve.scalar_tensor_tensor(out=act_gate[:, m % 2, :], in0=th[:, m % 2, :], scalar=1.0,
                                                 in1=psum[:, 2 + 2 * (m % 2), :], op0=ALU.add,
                                                 op1=ALU.mult).then_inc(gate_ready, 1)
                        dve.wait_ge(gate_ready, b * KH + m + 1)
                        dve.scalar_tensor_tensor(out=hidT[:, m, :], in0=act_gate[:, m % 2, :], scalar=0.5,
                                                 in1=psum[:, 3 + 2 * (m % 2), :], op0=ALU.mult,
                                                 op1=ALU.mult).then_inc(hid_ready, 1)
                    for o in range(2):
                        dve.wait_ge(down_done, b * 2 + o + 1)
                        dve.tensor_tensor(block_out[:, o, :].rearrange("p (i c) -> p i c", i=2),
                                          psum[:, 6 + o, :].rearrange("p (i c) -> p i c", i=2),
                                          h_res[:, bass.ds(b * TPS + 2 * o, 2), :], ALU.add).then_inc(down_read, 1)

            @block.tensor
            def _(pe):
                pe.wait_ge(weights_in, 64)
                with pe.Fori(0, NSEQ) as b:
                    pe.wait_ge(z_ready, b + 1)
                    for k in range(KD):
                        for i in range(TPS):
                            ins = pe.transpose(psum[:, k, i * P:(i + 1) * P], z[:, i, k * P:(k + 1) * P],
                                               cst["ident"][:])
                        ins.then_inc(z_turned, 1)
                    pe.wait_ge(zT_ready, b * KD + KD)
                    for m in range(KH):
                        if m >= 2:
                            pe.wait_ge(hid_ready, b * KH + m - 1)
                        for n, wt in enumerate((w1, w3)):
                            for k in range(KD):
                                ins = pe.matmul(psum[:, 2 + 2 * (m % 2) + n, :], wt[:, k, m * P:(m + 1) * P],
                                                zT[:, k, :], start=(k == 0), stop=(k == KD - 1))
                        ins.then_inc(up_done, 1)
                    pe.wait_ge(hid_ready, b * KH + KH)
                    for i in range(TPS):
                        for k in range(KH):
                            ins = pe.matmul(psum[:, 6 + i // 2, (i % 2) * D:(i % 2 + 1) * D],
                                            hidT[:, k, i * P:(i + 1) * P], w2[:, k, :],
                                            start=(k == 0), stop=(k == KH - 1))
                        if i % 2:
                            ins.then_inc(down_done, 1)


def experts(pr, name, x_res, stats, w, cst, psum, slots_in, slots_out):
    nc = pr.nc
    pr.prefix = name
    SEG = 512
    NSTEP = NE * CAP // SEG
    BIG = float(4 * NE * CAP)
    with ExitStack() as ctx:
        sb = lambda n, s, d=F32: pr.sb(n, s, d, ctx)
        z_all = sb("z_all", [P, NT, D])
        scatter_at = sb("scatter_at", [P, TOPK, NT], U32)
        gather_at = sb("gather_at", [P, TOPK, NT], U32)
        weight = sb("weight", [P, TOPK, NT])
        route(pr, name + "r_", x_res, z_all, stats, w, cst, psum, scatter_at, gather_at, weight, BIG)
        pr.prefix = name
        fc1 = sb("fc1", [P, 2, KD, EH])
        fc2 = sb("fc2", [P, 2, KE, D])
        bias1 = sb("bias1", [P, NE, KE])
        bias2 = sb("bias2", [P, NE, D])
        rows_in = sb("rows_in", [P, 2, TPS, D])
        rowsT = sb("rowsT", [P, 2, KD, SEG])
        hidT = sb("hidT", [P, KE, SEG])
        rows_out = sb("rows_out", [P, 2, TPS, D])
        NG = 8
        picked = sb("picked", [P, NG, D])
        bias_in, fc_in = pr.sem("bias_in"), [pr.sem("fc_in0"), pr.sem("fc_in1")]
        scattered = pr.sem("scattered")
        rows_loaded = [pr.sem("rows_loaded0"), pr.sem("rows_loaded1")]
        rows_turned, rowsT_ready = pr.sem("rows_turned"), pr.sem("rowsT_ready")
        up_done, hid_ready, down_done, out_ready = (pr.sem("up_done"), pr.sem("hid_ready"), pr.sem("down_done"),
                                                    pr.sem("out_ready"))
        out_stored = pr.sem("out_stored")
        gathered = [pr.sem(f"gathered{j}") for j in range(NG)]
        added = pr.sem("added")
        passed = pr.sem("passed")
        with nc.Block() as block:

            @block.sync
            def _(sp):
                def load_expert(e, s):
                    sp.dma_start(fc1[:, s], w["fc1"][bass.ds(e, 1)].rearrange("o p k h -> p (o k) h")
                                 ).then_inc(fc_in[s], 16)
                    sp.dma_start(fc2[:, s], w["fc2"][bass.ds(e, 1)].rearrange("o p k h -> p (o k) h")
                                 ).then_inc(fc_in[s], 16)

                def load_rows(n, s):
                    sp.dma_start(rows_in[:, s], slots_in[bass.ds(n * SEG, SEG), :].rearrange("(i p) d -> p i d", p=P)
                                 ).then_inc(rows_loaded[s], 16)

                sp.dma_start(bias1[:], w["bias1"]).then_inc(bias_in, 16)
                sp.dma_start(bias2[:], w["bias2"]).then_inc(bias_in, 16)
                for s in range(2):
                    load_expert(s, s)
                sp.wait_ge(scattered, 16 * TOPK * NT)
                for s in range(2):
                    load_rows(s, s)

                def store(n, s):
                    sp.wait_ge(out_ready, n * 2 + 2)
                    sp.dma_start(slots_out[bass.ds(n * SEG, SEG), :].rearrange("(i p) d -> p i d", p=P),
                                 rows_out[:, s]).then_inc(out_stored, 16)

                with sp.Fori(0, NSTEP // 4 - 1) as it:
                    for c in range(4):
                        n = it * 4 + c
                        store(n, c % 2)
                        if c % 2:
                            load_expert(it * 2 + c // 2 + 2, c // 2)
                        sp.wait_ge(out_stored, n * 16 + 16)
                        load_rows(n + 2, c % 2)
                for n in range(NSTEP - 4, NSTEP):
                    store(n, n % 2)
                    sp.wait_ge(out_stored, n * 16 + 16)
                    if n + 2 < NSTEP:
                        load_rows(n + 2, n % 2)

            @block.gpsimd
            def _(pool):
                for k in range(TOPK):
                    for t in range(NT):
                        pool.indirect_dma_start(
                            out=slots_in[:, :], out_offset=bass.IndirectOffsetOnAxis(scatter_at[:, k, t:t + 1], 0),
                            in_=z_all[:, t, :], in_offset=None, bounds_check=NE * CAP - 1, oob_is_err=False,
                        ).then_inc(scattered, 16)
                pool.wait_ge(out_stored, 16 * NSTEP)
                for g in range(NT * TOPK):
                    t, k = g // TOPK, g % TOPK
                    if g >= NG:
                        pool.wait_ge(added, g - NG + 1)
                    pool.indirect_dma_start(
                        out=picked[:, g % NG, :], out_offset=None, in_=slots_out[:, :],
                        in_offset=bass.IndirectOffsetOnAxis(gather_at[:, k, t:t + 1], 0),
                        bounds_check=NE * CAP - 1, oob_is_err=False,
                    ).then_inc(gathered[g % NG], 16)

            @block.scalar
            def _(act):
                act.wait_ge(bias_in, 32)
                with act.Fori(0, NE // 2) as it:
                    for c in range(4):
                        n = it * 4 + c
                        for m in range(KE):
                            act.wait_ge(up_done, n * KE + m + 1)
                            act.sem_inc(passed, 1)
                            act.activation(hidT[:, m, :], psum[:, 2 + m % 4, :], ACT.Relu,
                                           bias=bias1[:, bass.ds(it * 2 + c // 2, 1), m:m + 1].rearrange("p a b -> p (a b)"),
                                           ).then_inc(hid_ready, 1)

            @block.vector
            def _(dve):
                dve.wait_ge(bias_in, 32)
                with dve.Fori(0, NE // 2) as it:
                    for c in range(4):
                        n = it * 4 + c
                        for k in range(KD):
                            dve.wait_ge(rows_turned, n * KD + k + 1)
                            dve.tensor_copy(rowsT[:, c % 2, k, :], psum[:, k, :]).then_inc(rowsT_ready, 1)
                        for o in range(2):
                            dve.wait_ge(down_done, n * 2 + o + 1)
                            for i in range(2):
                                ins = dve.tensor_tensor(rows_out[:, c % 2, 2 * o + i:2 * o + i + 1, :],
                                                        psum[:, 6 + o, i * D:(i + 1) * D].rearrange("p (o d) -> p o d", o=1),
                                                        bias2[:, bass.ds(it * 2 + c // 2, 1), :], ALU.add)
                            ins.then_inc(out_ready, 1)
                for g in range(NT * TOPK):
                    t, k = g // TOPK, g % TOPK
                    dve.wait_ge(gathered[g % NG], 16 * (g // NG + 1))
                    if k:
                        dve.wait_ge(added, g)
                    dve.scalar_tensor_tensor(out=x_res[:, t, :], in0=picked[:, g % NG, :],
                                             scalar=weight[:, k, t:t + 1], in1=x_res[:, t, :],
                                             op0=ALU.mult, op1=ALU.add).then_inc(added, 1)
                dve.wait_ge(added, NT * TOPK)

            @block.tensor
            def _(pe):
                with pe.Fori(0, NE // 2) as it:
                    for c in range(4):
                        n = it * 4 + c
                        e, s = c // 2, c % 2
                        pe.wait_ge(rows_loaded[s], (it * 2 + e) * 16 + 16)
                        for k in range(KD):
                            for i in range(TPS):
                                ins = pe.transpose(psum[:, k, i * P:(i + 1) * P],
                                                   rows_in[:, s, i, k * P:(k + 1) * P], cst["ident"][:])
                            ins.then_inc(rows_turned, 1)
                        pe.wait_ge(fc_in[e], it * 32 + 32)
                        pe.wait_ge(rowsT_ready, n * KD + KD)
                        for m in range(KE):
                            if m >= 4:
                                pe.wait_ge(hid_ready, n * KE + m - 3)
                            for k in range(KD):
                                ins = pe.matmul(psum[:, 2 + m % 4, :], fc1[:, e, k, m * P:(m + 1) * P],
                                                rowsT[:, s, k, :], start=(k == 0), stop=(k == KD - 1))
                            ins.then_inc(up_done, 1)
                        pe.wait_ge(hid_ready, n * KE + KE)
                        for i in range(TPS):
                            for k in range(KE):
                                ins = pe.matmul(psum[:, 6 + i // 2, (i % 2) * D:(i % 2 + 1) * D],
                                                hidT[:, k, i * P:(i + 1) * P], fc2[:, e, k, :],
                                                start=(k == 0), stop=(k == KE - 1))
                            if i % 2:
                                ins.then_inc(down_done, 1)


def route(pr, name, x_res, z_all, stats, w, cst, psum, scatter_at, gather_at, weight, big):
    nc = pr.nc
    pr.prefix = name
    with ExitStack() as ctx:
        sb = lambda n, s, d=F32: pr.sb(n, s, d, ctx)
        gate = sb("gate", [P, KD, NE])
        count_in = sb("count_in", [P, 2 * P + NE])
        z = sb("z", [P, TPS, D])
        zT = sb("zT", [P, KD, SEQ])
        logits = sb("logits", [P, TPS, NE])
        top8 = sb("top8", [P, TPS, 8])
        at8 = sb("at8", [P, TPS, 8], U32)
        top = sb("top", [P, NT, TOPK])
        choice = sb("choice", [P, NT, TOPK])
        onehot = sb("onehot", [P, TOPK, NT, NE])
        run = sb("run", [P, 2, NT, NE])
        before = sb("before", [P, TOPK, NT, NE])
        small = sb("small", [P, 4, NT])
        loc = sb("loc", [P, TOPK, NT])
        slot = sb("slot", [P, 3, NT])
        in_ = pr.sem("in")
        z_normed, z_kept, z_turned, zT_ready = (pr.sem("z_normed"), pr.sem("z_kept"), pr.sem("z_turned"),
                                                pr.sem("zT_ready"))
        passed = pr.sem("passed")
        logits_done, chain, bulk = pr.sem("logits_done"), pr.sem("chain"), pr.sem("bulk")
        gap_ready, exp_ready, before_ready, places_done = (pr.sem("gap_ready"), pr.sem("exp_ready"),
                                                           pr.sem("before_ready"), pr.sem("places_done"))
        with nc.Block() as block:

            @block.sync
            def _(sp):
                sp.dma_start(gate[:], w["gate"]).then_inc(in_, 16)
                sp.dma_start(count_in[:], w["count"]).then_inc(in_, 16)

            @block.gpsimd
            def _(pool):
                with pool.Fori(0, NSEQ) as b:
                    pool.wait_ge(z_normed, b + 1)
                    pool.tensor_copy(z_all[:, bass.ds(b * TPS, TPS), :], z[:]).then_inc(z_kept, 1)
                pool.wait_ge(z_kept, NSEQ)

            @block.scalar
            def _(act):
                with act.Fori(0, NSEQ) as b:
                    for k in range(KD):
                        act.wait_ge(z_turned, b * KD + k + 1)
                        act.activation(zT[:, k, :], psum[:, k, :], ACT.Copy).then_inc(zT_ready, 1)
                act.wait_ge(gap_ready, 1)
                act.activation(small[:, 1, :], small[:, 0, :], ACT.Exp).then_inc(exp_ready, 1)

            @block.vector
            def _(dve):
                with dve.Fori(0, NSEQ) as b:
                    link = Chain(dve, chain, 5, b)
                    for i in range(TPS):
                        t = b * TPS + i
                        ins = dve.tensor_scalar(z[:, i:i + 1, :], x_res[:, bass.ds(t, 1), :],
                                                stats["mean"][:, bass.ds(t, 1)], stats["rstd"][:, bass.ds(t, 1)],
                                                ALU.subtract, ALU.mult)
                    ins.then_inc(z_normed, 1)
                    dve.wait_ge(logits_done, b + 1)
                    link(dve.tensor_copy(logits[:], psum[:, 2, 0:TPS * NE].rearrange("p (i e) -> p i e", e=NE)))
                    dve.sem_inc(passed, 1)
                    for i in range(TPS):
                        ins = dve.max(top8[:, i, :], logits[:, i, :])
                    link(ins)
                    dve.sem_inc(passed, 1)
                    for i in range(TPS):
                        ins = dve.max_index(at8[:, i, :], top8[:, i, :], logits[:, i, :])
                    link(ins)
                    link(dve.tensor_copy(top[:, bass.ds(b * TPS, TPS), :], top8[:, :, 0:TOPK]))
                    link(dve.tensor_copy(choice[:, bass.ds(b * TPS, TPS), :], at8[:, :, 0:TOPK]))
                    dve.wait_ge(z_kept, b + 1)
                link = Chain(dve, bulk)
                dve.tensor_tensor(small[:, 0, :], top[:, :, 1], top[:, :, 0], ALU.subtract).then_inc(gap_ready, 1)
                dve.wait_ge(in_, 32)
                iota = count_in[:, 2 * P:2 * P + NE].rearrange("p (o e) -> p o e", o=1).broadcast_to((P, NT, NE))
                for k in range(TOPK):
                    link(dve.tensor_tensor(onehot[:, k], iota, choice[:, :, k:k + 1].broadcast_to((P, NT, NE)),
                                           ALU.is_equal))
                for k in range(TOPK):
                    held, other = onehot[:, k], 0
                    step = 1
                    while step < NT:
                        dst = run[:, other]
                        dve.tensor_copy(dst[:, 0:step], held[:, 0:step])
                        link(dve.tensor_tensor(dst[:, step:], held[:, step:], held[:, 0:NT - step], ALU.add))
                        held, other, step = dst, 1 - other, step * 2
                    link(dve.tensor_tensor(before[:, k], held, onehot[:, k], ALU.subtract))
                    if k == 0:
                        total = sb("total", [P, 1, NE])
                        link(dve.tensor_copy(total[:], held[:, NT - 1:NT]))
                    else:
                        dve.tensor_tensor(before[:, k], before[:, k], total[:].broadcast_to((P, NT, NE)),
                                          ALU.add).then_inc(before_ready, 1)
                dve.wait_ge(exp_ready, 1)
                link(dve.tensor_scalar(small[:, 2, :], small[:, 1, :], 1.0, None, ALU.add))
                link(dve.reciprocal(small[:, 3, :], small[:, 2, :]))
                dve.wait_ge(before_ready, 1)
                for k in range(TOPK):
                    dve.wait_ge(places_done, k + 1)
                    link(dve.tensor_tensor(run[:, 0], psum[:, 4 + k, 0:NT * NE].rearrange("p (t e) -> p t e", e=NE),
                                           onehot[:, k], ALU.mult))
                    link(dve.tensor_reduce(loc[:, k, :], run[:, 0], AX.X, ALU.add))
                    link(dve.scalar_tensor_tensor(out=slot[:, 0, :], in0=choice[:, :, k], scalar=float(CAP),
                                                  in1=loc[:, k, :], op0=ALU.mult, op1=ALU.add))
                    link(dve.tensor_scalar(slot[:, 1, :], loc[:, k, :], float(CAP), None, ALU.is_lt))
                    link(dve.tensor_tensor(slot[:, 0, :], slot[:, 0, :], slot[:, 1, :], ALU.mult))
                    link(dve.tensor_copy(gather_at[:, k, :], slot[:, 0, :]))
                    link(dve.tensor_scalar(slot[:, 2, :], slot[:, 1, :], -big, big, ALU.mult, ALU.add))
                    link(dve.tensor_tensor(slot[:, 2, :], slot[:, 2, :], slot[:, 0, :], ALU.add))
                    link(dve.tensor_copy(scatter_at[:, k, :], slot[:, 2, :]))
                    link(dve.tensor_tensor(weight[:, k, :], small[:, 3, :], slot[:, 1, :], ALU.mult))
                    if k:
                        link(dve.tensor_tensor(weight[:, k, :], weight[:, k, :], small[:, 1, :], ALU.mult))

            @block.tensor
            def _(pe):
                pe.wait_ge(in_, 32)
                with pe.Fori(0, NSEQ) as b:
                    pe.wait_ge(z_normed, b + 1)
                    for k in range(KD):
                        for i in range(TPS):
                            ins = pe.transpose(psum[:, k, i * P:(i + 1) * P], z[:, i, k * P:(k + 1) * P],
                                               cst["ident"][:])
                        ins.then_inc(z_turned, 1)
                    pe.wait_ge(zT_ready, b * KD + KD)
                    for i in range(TPS):
                        for k in range(KD):
                            ins = pe.matmul(psum[:, 2, i * NE:(i + 1) * NE], zT[:, k, i * P:(i + 1) * P],
                                            gate[:, k, :], start=(k == 0), stop=(k == KD - 1))
                    ins.then_inc(logits_done, 1)
                pe.wait_ge(before_ready, 1)
                for k in range(TOPK):
                    out = psum[:, 4 + k, 0:NT * NE]
                    pe.matmul(out, count_in[:, 0:P], onehot[:, k].rearrange("p t e -> p (t e)"), start=True, stop=False)
                    pe.matmul(out, count_in[:, P:2 * P], before[:, k].rearrange("p t e -> p (t e)"),
                              start=False, stop=True).then_inc(places_done, 1)


def build(nc, a, upto=99):
    with ExitStack() as ctx:
        pr = Program(nc, ctx)
        psum = ctx.enter_context(nc.psum_tensor("banks", [P, 8, SEQ], F32))
        y_res = pr.sb("y_res", [P, NT, D])
        consts = pr.sb("consts", [P, P])
        ident_bf = pr.sb("ident_bf", [P, P], BF16)
        cst = {"ident": consts, "ident_bf": ident_bf}
        stats = {"stat": pr.sb("stat", [P, NT, 6]), "mean": pr.sb("mean", [P, NT]), "rstd": pr.sb("rstd", [P, NT]),
                 "tmp": pr.sb("tmp", [P, 3, NT])}
        stats2 = {"stat": pr.sb("stat2", [P, NT, 6]), "mean": pr.sb("mean2", [P, NT]),
                  "rstd": pr.sb("rstd2", [P, NT]), "tmp": pr.sb("tmp2", [P, 3, NT])}
        qk_parts = nc.dram_tensor("qk_parts", (2, 2, 3, D, SEQ), BF16, kind="Internal").ap()
        slots_in = nc.dram_tensor("slots_in", (NE * CAP, D), F32, kind="Internal").ap()
        slots_out = nc.dram_tensor("slots_out", (NE * CAP, D), F32, kind="Internal").ap()

        x_in, zero_ready, zeroed, ident_ready = pr.sem("x_in"), pr.sem("zero_ready"), pr.sem("zeroed"), pr.sem("ident_ready")
        with ExitStack() as first:
            x_res = pr.sb("x_res", [P, NT, D], F32, first)
            zero = pr.sb("zero", [P, 8 * D], F32, first)
            with nc.Block() as block:

                @block.sync
                def _(sp):
                    sp.dma_start(x_res[:], a["x"].rearrange("(t p) d -> p t d", p=P)).then_inc(x_in, 16)
                    sp.dma_start(consts[:], a["ident"]).then_inc(x_in, 16)
                    sp.wait_ge(x_in, 32)
                    sp.wait_ge(zero_ready, 1)
                    for r in range(8):
                        sp.dma_start(slots_in.rearrange("(r p j) d -> r p (j d)", p=P, r=8)[r], zero[:]
                                     ).then_inc(zeroed, 16)
                    sp.wait_ge(zeroed, 128)

                @block.vector
                def _(dve):
                    dve.memset(zero[:], 0.0).then_inc(zero_ready, 1)
                    dve.wait_ge(x_in, 32)
                    dve.tensor_copy(ident_bf[:], consts[:]).then_inc(ident_ready, 1)
                    dve.wait_ge(ident_ready, 1)

            statistics(pr, "sa_", x_res, stats, y_res, stats2)
        if upto >= 1:
            attention(pr, "a_", True, y_res, stats2,
                      {"qk": a["a_qk"], "v": a["a_v"], "o": a["a_o"], "rope": a["rope"], "gain": a["ln1"],
                       "window": a["window"]}, cst, psum, qk_parts)
            pr.end_layer()
        if upto >= 2:
            statistics(pr, "sf_", y_res, stats)
            swiglu(pr, "f_", a["x"], y_res, stats, {"w1": a["w1"], "w3": a["w3"], "w2": a["w2"], "gain": a["ln2"]},
                   cst, psum)
            pr.end_layer()
        moe = {k: a[k] for k in ("gate", "count", "fc1", "fc2", "bias1", "bias2")}
        if upto >= 3:
            statistics(pr, "sm_", y_res, stats)
            experts(pr, "m_", y_res, stats, moe, cst, psum, slots_in, slots_out)
            pr.end_layer()
        if upto >= 4 or upto == -2:
            statistics(pr, "sb_", y_res, stats)
            attention(pr, "b_", False, y_res, stats, {"qk": a["b_qk"], "v": a["b_v"], "o": a["b_o"]}, cst, psum,
                      qk_parts)
            pr.end_layer()
        if upto >= 5:
            statistics(pr, "sn_", y_res, stats)
            experts(pr, "n_", y_res, stats, moe, cst, psum, slots_in, slots_out)
            pr.end_layer()
        stored = pr.sem("stored")
        with nc.Block() as block:

            @block.sync
            def _(sp):
                sp.dma_start(a["out"].rearrange("(t p) d -> p t d", p=P), y_res[:]).then_inc(stored, 16)
                sp.wait_ge(stored, 16)


def by_rows(m, k):
    return np.ascontiguousarray(m.reshape(k, P, -1).transpose(1, 0, 2))


def padded(m, shape):
    out = np.zeros(shape, m.dtype)
    out[:m.shape[0], :m.shape[1]] = m
    return out


def shape_constants():
    f = 1.0 / np.float32(10000.0) ** (np.arange(0, HD, 2, dtype=np.float32) / np.float32(HD))
    angle = np.outer(np.arange(SEQ, dtype=np.float32), f.astype(np.float32)).astype(np.float32)
    cos, sin = np.cos(angle).astype(np.float32), np.sin(angle).astype(np.float32)
    d = np.arange(P) % HD
    rope = np.stack([cos[:, d // 2].T, np.where(d % 2 == 0, -1, 1)[:, None] * sin[:, d // 2].T], 1)
    p, c = np.arange(P)[:, None], np.arange(2 * P)[None, :]
    by_query = (c <= p + P) & (c >= p)
    by_key = (c >= p) & (c - p <= WINDOW)
    window = np.stack([np.tile(np.where(m, 0.0, MASKED), 2) for m in (by_query, by_key)], 1)
    before = (np.arange(P)[:, None] < np.arange(P)[None, :]).astype(np.float32)
    count = np.concatenate([before, np.ones((P, P)), np.tile(np.arange(NE), (P, 1))], 1)
    return {"rope": rope.astype(np.float32), "window": window.astype(np.float32), "count": count.astype(np.float32),
            "ident": np.eye(P, dtype=np.float32)}


def layouts(i):
    i = {k.replace("L0_", ""): np.asarray(v) for k, v in i.items()}
    swap = np.arange(D) ^ 1
    both = lambda g, b: np.ascontiguousarray(np.broadcast_to(np.stack([g, b])[None], (P, 2, D)))
    fc1 = i["ffn_fc1_w"].transpose(0, 2, 1).reshape(NE, KD, P, EH).transpose(0, 2, 1, 3)
    fc2 = i["ffn_fc2_w"].reshape(NE, KE, P, D).transpose(0, 2, 1, 3)
    wq, wk = i["attn_a_wq"], i["attn_a_wk"]
    return {
        "x": i["attn_a_x"].reshape(NTOK, D),
        "a_qk": by_rows(np.concatenate([wq, wq[:, swap], wk, wk[:, swap]], 1), KD),
        "a_v": by_rows(i["attn_a_wv"], KD), "a_o": by_rows(i["attn_a_wo"], KD),
        "ln1": both(i["attn_a_ln1_g"], i["attn_a_ln1_b"]), "ln2": both(i["attn_a_ln2_g"], i["attn_a_ln2_b"]),
        "w1": by_rows(padded(i["attn_a_w1"], (D, HIDP)), KD), "w3": by_rows(padded(i["attn_a_w3"], (D, HIDP)), KD),
        "w2": by_rows(padded(i["attn_a_w2"], (HIDP, D)), KH),
        "b_qk": by_rows(np.concatenate([i["attn_b_w_q"].T, i["attn_b_w_k"].T], 1), KD),
        "b_v": by_rows(i["attn_b_w_v"].T, KD), "b_o": by_rows(i["attn_b_w_o"].T, KD),
        "gate": by_rows(i["ffn_gate_w"].T, KD),
        "fc1": np.ascontiguousarray(fc1), "fc2": np.ascontiguousarray(fc2),
        "bias1": np.ascontiguousarray(i["ffn_fc1_b"].reshape(NE, KE, P).transpose(2, 0, 1)),
        "bias2": np.ascontiguousarray(np.broadcast_to(i["ffn_fc2_b"].reshape(1, NE, D), (P, NE, D))),
        **shape_constants(),
    }


def kernel(**inputs):
    import concourse.bacc as bacc
    from concourse.bass_utils import run_bass_kernel_spmd

    nc = bacc.Bacc("TRN2", target_bir_lowering=False, num_devices=1)
    arrays = {f"in_{k}": v for k, v in layouts(inputs).items()}
    aps = {k[3:]: nc.dram_tensor(k, v.shape, F32, kind="ExternalInput").ap() for k, v in arrays.items()}
    aps["out"] = nc.dram_tensor("out", (NTOK, D), F32, kind="ExternalOutput").ap()
    build(nc, aps)
    r = run_bass_kernel_spmd(nc, [arrays], core_ids=[0])
    return r.results[0]["out"].reshape(NSEQ, SEQ, D)
```

```python
from contextlib import ExitStack

import numpy as np

import concourse.bass as bass
from concourse import mybir

ALU = mybir.AluOpType
ACT = mybir.ActivationFunctionType
AX = mybir.AxisListType
F32 = mybir.dt.float32
BF16 = mybir.dt.bfloat16
U32 = mybir.dt.uint32
F32R = mybir.dt.float32r

P = 128
NSEQ, SEQ, D = 8, 512, 256
NTOK = NSEQ * SEQ
NT = NTOK // P
TPS = SEQ // P
KD = D // P
NH, HD = 16, 16
SCALE = HD ** -0.5
WINDOW = 128
EPS = 1e-5
HID, HIDP = 704, 768
KH = HIDP // P
NE, TOPK, EH = 8, 2, 1024
CAP = TOPK * ((NTOK + NE - 1) // NE)
KE = EH // P
SPLIT_PRODUCTS = ((0, 0), (0, 1), (1, 0))
MASKED = -(2.0 ** 127)
BEGIN = {True: 0, False: 8}
SPREAD = 2
Q_PARTS = (0, 0, 1, 1, 0, 2)
K_PARTS = (0, 1, 0, 1, 2, 0)
NPROD = len(Q_PARTS)
SROWS = NPROD * HD


class Program:

    def __init__(self, nc, ctx):
        self.nc, self.ctx, self.prefix, self.sems = nc, ctx, "", []

    def sem(self, name):
        self.sems.append(self.nc.alloc_semaphore(name=self.prefix + name))
        return self.sems[-1]

    def end_layer(self):
        self.nc.clear_and_free_semaphores(self.sems)
        self.nc.all_engine_barrier()
        self.sems = []

    def sb(self, name, shape, dt=F32, ctx=None):
        return (ctx or self.ctx).enter_context(self.nc.sbuf_tensor(self.prefix + name, shape, dt))


class Chain:

    def __init__(self, eng, sem, per=0, it=None, start=0):
        self.eng, self.sem, self.base, self.k, self.per = eng, sem, start, 0, per
        self.it = it

    def value(self):
        n = self.base + self.k
        return n if self.it is None else self.it * self.per + n

    def __call__(self, ins):
        ins.then_inc(self.sem, 1)
        self.k += 1
        self.eng.wait_ge(self.sem, self.value())


class LoopChain(Chain):

    def __init__(self, eng, sem):
        super().__init__(eng, sem)

    def start(self, it, per, base):
        self.it, self.per, self.base, self.k = it, per, 0, base


def rstd_steps(link, dve, act_sqrt, stat, mean, rstd, tmp, sq_done):
    me, mo = stat[:, :, 1], stat[:, :, 4]
    link(dve.tensor_tensor(mean[:, :], me, mo, ALU.add))
    link(dve.tensor_scalar(mean[:, :], mean[:, :], 0.5, None, ALU.mult))
    link(dve.tensor_tensor(tmp[:, 0, :], me, mo, ALU.subtract))
    link(dve.tensor_tensor(tmp[:, 0, :], tmp[:, 0, :], tmp[:, 0, :], ALU.mult))
    link(dve.tensor_tensor(tmp[:, 1, :], stat[:, :, 2], stat[:, :, 5], ALU.add))
    link(dve.tensor_scalar(tmp[:, 1, :], tmp[:, 1, :], 1.0 / D, EPS, ALU.mult, ALU.add))
    act_sqrt(dve.scalar_tensor_tensor(out=tmp[:, 1, :], in0=tmp[:, 0, :], scalar=0.25, in1=tmp[:, 1, :],
                                      op0=ALU.mult, op1=ALU.add))
    sq_done()
    link(dve.reciprocal(rstd[:, :], tmp[:, 2, :]))
    link(dve.tensor_tensor(tmp[:, 0, :], rstd[:, :], rstd[:, :], ALU.mult))
    link(dve.tensor_tensor(tmp[:, 0, :], tmp[:, 0, :], tmp[:, 1, :], ALU.mult))
    link(dve.tensor_scalar(tmp[:, 0, :], tmp[:, 0, :], -0.5, 1.5, ALU.mult, ALU.add))
    link(dve.tensor_tensor(rstd[:, :], rstd[:, :], tmp[:, 0, :], ALU.mult))


def row_statistics(dve, stat, rows, t):
    return dve.bn_stats(stat[:, bass.ds(t, 1), :].rearrange("p o c -> p (o c)"),
                        rows[:, bass.ds(t, 1), :].rearrange("p o c -> p (o c)"))


def statistics(pr, name, src, stats, normalised=None, stat_of_normalised=None, loads=(), arrivals=(None,)):
    nc = pr.nc
    layer_prefix = pr.prefix
    pr.prefix = name
    chain, var_ready, sqrt_ready = pr.sem("chain"), pr.sem("var_ready"), pr.sem("sqrt_ready")
    rows_ready = pr.sem("rows_ready")
    rounds = [(src, stats)] + ([(normalised, stat_of_normalised)] if normalised is not None else [])
    with nc.Block() as block:

        @block.sync
        def _(sp):
            for dst, source, sem in loads:
                sp.dma_start(dst, source).then_inc(sem, 16)
        @block.scalar
        def _(act):
            for n, (_, st) in enumerate(rounds):
                act.wait_ge(var_ready, n + 1)
                act.activation(st["tmp"][:, 2, :], st["tmp"][:, 1, :], ACT.Sqrt).then_inc(sqrt_ready, 1)

        @block.vector
        def _(dve):
            link = Chain(dve, chain)
            for n, (rows, st) in enumerate(rounds):
                if normalised is not None:
                    shares = arrivals if n == 0 else (None,)
                    for share, arrived in enumerate(shares):
                        if arrived is not None:
                            dve.wait_ge(arrived, 16)
                        with dve.Fori(share * NSEQ // len(shares), (share + 1) * NSEQ // len(shares)) as b:
                            for i in range(TPS):
                                last = row_statistics(dve, st["stat"], rows, b * TPS + i)
                            last.then_inc(rows_ready, 1)
                    dve.wait_ge(rows_ready, NSEQ * (2 * n + 1))

                def to_sqrt(ins, n=n):
                    ins.then_inc(var_ready, 1)

                def sqrt_back(n=n):
                    dve.wait_ge(sqrt_ready, n + 1)

                rstd_steps(link, dve, to_sqrt, st["stat"], st["mean"], st["rstd"], st["tmp"], sqrt_back)
                if n + 1 < len(rounds):
                    with dve.Fori(0, NSEQ) as b:
                        for i in range(TPS):
                            t = b * TPS + i
                            last = dve.tensor_scalar(normalised[:, bass.ds(t, 1), :], rows[:, bass.ds(t, 1), :],
                                                     st["mean"][:, bass.ds(t, 1)], st["rstd"][:, bass.ds(t, 1)],
                                                     ALU.subtract, ALU.mult)
                        last.then_inc(rows_ready, 1)
                    dve.wait_ge(rows_ready, NSEQ * (2 * n + 2))
    pr.prefix = layer_prefix


def attention_plan(windowed):
    NJ = 8 if windowed else 4
    rounds = 4 if windowed else 8
    per_group = rounds // 4
    units = 8 if windowed else 16
    weight = {"Z": 0, "S": 4 if windowed else 2, "O": 5, "O1": 5, "H": 2, "T": 2, "J1": 4, "J": 4, "V1": 4, "V": 4}
    project = [(k, n, 1) for n in range(2) for k in ("V1", "V")] + [("T", 0, 2), ("T", 1, 2)] \
        + [(k, j, 2) for j in range(NJ) for k in ("J1", "J")]
    others = [("Z", 0, 2)]
    for r in range(rounds):
        for s in range(4):
            if s == 2 and r:
                others.append(("O1", r - 1, 0))
            if s == 3 and r % per_group == 1 % per_group and r > per_group:
                others.append(("H", (r - 1) // per_group - 1, 0))
            others.append(("S", 4 * r + s, 0))
            for _ in range(3 if windowed else 1):
                if project and 4 * r + s >= (4 if windowed and project[0][2] == 2 else 1):
                    others.append(project.pop(0))
        if r:
            others.append(("O", r - 1, 0))
    others += [("O1", rounds - 1, 0)] + ([("H", 2, 0)] if windowed else []) + [("O", rounds - 1, 0), ("H", 3, 0)]
    assert not project
    maxima = []
    for i in range(TPS):
        for m in range(units):
            maxima.append(("M", i * units + m, 1))
            if i and m == units // 2:
                maxima.append(("N", i - 1, 1))
    begin = BEGIN[windowed]
    total = sum(weight[k] for k, _, _ in others) - begin
    plan, done, taken = [], -begin, 0
    for unit in others:
        plan.append(unit)
        done += weight[unit[0]]
        want = len(maxima) * max(0, done) // total
        plan += maxima[taken:want]
        taken = want
    return plan + [("G", 0, 0), ("N", TPS - 1, 1), ("G", 1, 0), ("W", 0, 0), ("W", 1, 0)]


def attention(pr, name, windowed, src, stats, next_stat, w, cst, psum, qk_parts, row_statistics_and):
    nc = pr.nc
    pr.prefix = name
    NPJ = 2 * KD
    UPT = 8 if windowed else 16
    MU = TPS * UPT + TPS
    RND = 4 if windowed else 8
    RPG = RND // 4
    SU = 4 * RND
    NJ = 8 if windowed else 4
    step_plan = attention_plan(windowed)
    only = lambda *ds: [u for u in step_plan if u[2] in ds]
    shift = lambda plan, d: [(k, n, x + d) for k, n, x in plan]
    rows_to_parts = shift(only(2), -2)
    turned = 3
    then = shift(rows_to_parts[1:], 1)
    maxima = shift([u for u in only(1) if u[0][0] != "V"], -1)
    ahead_of_all = rows_to_parts[:turned] + shift(rows_to_parts[:1], 1) + rows_to_parts[turned:] \
        + shift([u for u in only(1) if u[0][0] == "V"], -1) + then[:len(then) // 2]
    then = then[len(then) // 2:]
    while then:
        ahead_of_all += [then.pop(0)] + maxima[:SPREAD]
        maxima = maxima[SPREAD:]
    ahead_of_all += maxima
    BANK7 = "TJVH"
    x_units = lambda plan: sum(k in BANK7 for k, _, _ in plan)
    LINKS = {"J": 2, "H": 1}
    links = lambda plan: sum(LINKS.get(k, 0) + 4 * (k == "M" and n % UPT == UPT - 1) for k, n, _ in plan)

    def first(it, c):
        return type(it) is int and it == 0 and c == 0

    def order(eng, unit, link=None):
        per = x_units(step_plan)

        def steps(plan, it, c, x, looped=False):
            for kind, n, d in plan:
                unit(kind, n, it, c + d, it * (2 * per) + x if looped else x)
                x += kind in BANK7
            return x

        x0 = x = x_units(ahead_of_all)
        if link:
            link.start(None, 0, 0)
        steps(ahead_of_all, 0, 0, 0)
        with eng.Fori(0, NSEQ // 2 - 1) as it:
            if link:
                link.start(it, 2 * links(step_plan), links(ahead_of_all))
            for c in range(2):
                x = steps(step_plan, it, c, x, looped=True)
            if link:
                assert link.k == links(ahead_of_all) + link.per, (link.k, link.per)
        it = NSEQ // 2 - 1
        x = x0 + per * (NSEQ - 2)
        if link:
            link.start(None, 0, links(ahead_of_all) + links(step_plan) * (NSEQ - 2))
        x = steps(only(0, 1), it, 0, x)
        steps(only(0), it, 1, x)

    with ExitStack() as ctx:
        sb = lambda n, s, d=F32: pr.sb(n, s, d, ctx)
        wqk = sb("wqk", [P, KD, w["qk"].shape[-1]])
        wv = sb("wv", [P, KD, D])
        wo = sb("wo", [P, KD, D])
        rows = sb("rows", [P, 3, SEQ])
        weights_in = pr.sem("weights_in")
        loads = [(wqk[:], w["qk"], weights_in), (wv[:], w["v"], weights_in), (wo[:], w["o"], weights_in)]
        if windowed:
            rope = sb("rope", [P, 2, SEQ])
            gain = sb("gain", [P, 2, D])
            loads += [(rope[:], w["rope"], weights_in), (gain[:], w["gain"], weights_in),
                      (rows[:, 0:2, :], w["window"], weights_in)]
        pending = row_statistics_and(loads)
        z = sb("z", [P, TPS, D])
        zT = sb("zT", [P, KD, SEQ])
        parts = sb("parts", [P, NPJ, 3, SEQ], BF16)
        q_stack = sb("q_stack", [P, 2, NH, SEQ], BF16)
        k_stack = sb("k_stack", [P, 2, NH, SEQ], BF16)
        v_ones = sb("v_ones", [P, 2, TPS, NH, 2 * HD])
        probs = sb("probs", [P, 2, 4, 2 * SEQ])
        row_max = sb("row_max", [P, TPS, NH])
        neg_max = sb("neg_max", [P, 2, NH])
        neg_parts = sb("neg_parts", [P, TPS, 3, NH], BF16)
        maxT = sb("maxT", [3 * NH, SEQ], BF16)
        headsT = sb("headsT", [P, 2, SEQ])
        recip = sb("recip", [P, TPS, 4])
        heads = sb("heads", [P, TPS, D])
        catT = sb("catT", [P, KD, SEQ])
        if windowed:
            window_bf = sb("window_bf", [P, 2, SEQ], BF16)

        setup_done, window_ready = pr.sem("setup_done"), pr.sem("window_ready")
        passed = pr.sem("passed")
        z_normed, z_scaled, z_ready = pr.sem("z_normed"), pr.sem("z_scaled"), pr.sem("z_ready")
        x_done, x_free = pr.sem("bank7_done"), pr.sem("bank7_read")
        parts_ready = pr.sem("parts_ready")
        parts_out = [pr.sem(f"parts_out{g}") for g in range(NPJ)]
        stack_in = [[pr.sem(f"stack_in{s}_half{half}") for half in range(KD)] for s in range(2)]
        scores_done, max_done = pr.sem("scores_done"), pr.sem("max_done")
        neg_ready = pr.sem("neg_ready")
        max_in = [pr.sem("max_in0"), pr.sem("max_in1")]
        scoresT_done, probs_ready, values_done = pr.sem("scoresT_done"), pr.sem("probs_ready"), pr.sem("values_done")
        headsT_ready, cat_turned, catT_ready = pr.sem("headsT_ready"), pr.sem("cat_turned"), pr.sem("catT_ready")
        out_done, out_added = pr.sem("out_done"), pr.sem("out_added")
        chain = pr.sem("chain")
        NW = 6 if windowed else 3
        LOADS = 16 * 2 * NPROD

        with nc.Block() as block:

            @block.sync
            def _(sp):
                def store_parts(g, it, c):
                    sp.wait_ge(parts_ready, (it * 2 + c) * NPJ + g + 1)
                    sp.dma_start(qk_parts[c % 2, g // KD, :, g % KD * P:(g % KD + 1) * P, :
                                          ].rearrange("c p t -> p c t"), parts[:, g]).then_inc(parts_out[g], 16)

                def load_half(half, it, c):
                    s = c % 2
                    heads_ = slice(half * NH // 2, (half + 1) * NH // 2)
                    for qk in range(2):
                        sp.wait_ge(parts_out[qk * KD + half], (it * 2 + c) * 16 + 16)
                    for qk in range(2):
                        stack = (q_stack, k_stack)[qk]
                        for n in range(NPROD):
                            part = (Q_PARTS, K_PARTS)[qk][n]
                            sp.dma_start(stack[n * HD:(n + 1) * HD, s, heads_],
                                         qk_parts[s, qk, part, half * P:(half + 1) * P].rearrange("(h d) t -> d h t", d=HD)
                                         ).then_inc(stack_in[s][half], 16)

                def step(it, c, project=True):
                    sp.wait_ge(scoresT_done, (it * 2 + c) * SU + 1)
                    load_half(1, it, c + 1)
                    if project:
                        for half in range(KD):
                            sp.wait_ge(stack_in[c % 2][half], (it + c // 2) * LOADS + LOADS)
                        for g in range(NPJ):
                            store_parts(g, it, c + 2)
                        sp.wait_ge(scoresT_done, (it * 2 + c) * SU + SU // 2 + 1)
                        load_half(0, it, c + 2)

                for g in range(NPJ):
                    store_parts(g, 0, 0)
                for half in range(KD):
                    load_half(half, 0, 0)
                for g in range(NPJ):
                    store_parts(g, 0, 1)
                load_half(0, 0, 1)
                with sp.Fori(0, NSEQ // 2 - 1) as it:
                    step(it, 0)
                    step(it, 1)
                step(NSEQ // 2 - 1, 0, project=False)
                if pending:
                    sp.wait_ge(*pending)

            @block.gpsimd
            def _(pool):
                def set_ones():
                    pool.memset(v_ones[:, :, :, :, HD:], 1.0).then_inc(setup_done, 1)
                    pool.wait_ge(setup_done, 1)
                    pool.memset(k_stack[SROWS:SROWS + 32, :, :, :], 1.0).then_inc(setup_done, 1)
                    pool.wait_ge(setup_done, 2)

                if windowed:
                    pool.wait_ge(weights_in, 16 * NW)

                def scale_rows(b):
                    if not windowed:
                        return
                    pool.wait_ge(z_normed, b + 1)
                    for i in range(TPS):
                        ins = pool.tensor_tensor(z[:, i, :], z[:, i, :], gain[:, 0, :], ALU.mult)
                    ins.then_inc(z_scaled, 1)
                    pool.wait_ge(z_scaled, b + 1)
                    for i in range(TPS):
                        ins = pool.tensor_tensor(z[:, i, :], z[:, i, :], gain[:, 1, :], ALU.add)
                    ins.then_inc(z_ready, 1)

                def load_max(it, c):
                    pool.wait_ge(max_done, (it * 2 + c) * MU + MU)
                    pool.sem_inc(passed, 1)
                    for k in range(3):
                        pool.dma_start(q_stack[SROWS + k:SROWS + k + 1, c % 2],
                                       maxT[k * NH:(k + 1) * NH, :]).then_inc(max_in[c % 2], 16)

                scale_rows(0)
                scale_rows(1)
                set_ones()
                load_max(0, 0)
                with pool.Fori(0, NSEQ // 2 - 1) as it:
                    for c in range(2):
                        scale_rows(it * 2 + c + 2)
                        load_max(it, c + 1)
                load_max(NSEQ // 2 - 1, 1)

            @block.scalar
            def _(act):
                def unit(kind, n, it, c, x):
                    b = it * 2 + c
                    if kind == "T":
                        act.wait_ge(x_done, x + 1)
                        act.activation(zT[:, n, :], psum[:, 7, :], ACT.Copy).then_inc(x_free, 1)
                    elif kind == "V":
                        act.wait_ge(x_done, x + 1)
                        act.activation(v_ones[:, c % 2, 2 * n:2 * n + 2, :, 0:HD],
                                       psum[:, 7, :].rearrange("p (i h d) -> p i h d", i=2, h=NH),
                                       ACT.Copy).then_inc(x_free, 1)
                    elif kind == "S":
                        r, s = n // 4, n % 4
                        act.wait_ge(scoresT_done, b * SU + n + 2)
                        if r >= 2:
                            act.wait_ge(values_done, b * RND + r - 1)
                        act.activation(probs[:, r % 2, s, :],
                                       psum[:, 2 + 2 * (n % 2):4 + 2 * (n % 2), :].rearrange("p a c -> p (a c)"),
                                       ACT.Exp, scale=SCALE).then_inc(probs_ready, 1)
                    elif kind == "O" and n % RPG == RPG - 1:
                        act.wait_ge(values_done, b * RND + n + 1)
                        act.activation(headsT[:, n // RPG % 2, :], psum[:, 6, :], ACT.Copy).then_inc(headsT_ready, 1)
                    elif kind == "G":
                        act.wait_ge(cat_turned, b * KD + n + 1)
                        act.activation(catT[:, n, :], psum[:, 2 + n, :], ACT.Copy).then_inc(catT_ready, 1)

                order(act, unit)

            @block.vector
            def _(dve):
                if windowed:
                    dve.wait_ge(weights_in, 16 * NW)
                    dve.tensor_copy(window_bf[:], rows[:, 0:2, :]).then_inc(window_ready, 1)
                    dve.wait_ge(window_ready, 1)
                link = LoopChain(dve, chain)

                def split(whole, g, b, read):
                    slot = parts[:, g]
                    link(dve.tensor_copy(slot[:, 0, :], whole))
                    read(dve.tensor_tensor(rows[:, 0, :], whole, slot[:, 0, :], ALU.subtract))
                    link(dve.tensor_copy(slot[:, 1, :], rows[:, 0, :]))
                    dve.tensor_tensor(slot[:, 2, :], rows[:, 0, :], slot[:, 1, :], ALU.subtract
                                      ).then_inc(parts_ready, 1)
                    dve.wait_ge(parts_ready, b * NPJ + g + 1)

                def unit(kind, n, it, c, x):
                    b = it * 2 + c
                    if kind == "Z":
                        if not first(it, c):
                            dve.wait_ge(x_done, x)
                        for i in range(TPS):
                            t = b * TPS + i
                            ins = dve.tensor_scalar(z[:, i:i + 1, :], src[:, bass.ds(t, 1), :],
                                                    stats["mean"][:, bass.ds(t, 1)], stats["rstd"][:, bass.ds(t, 1)],
                                                    ALU.subtract, ALU.mult)
                        ins.then_inc(z_normed, 1)
                    elif kind == "J":
                        g = n // 2 if windowed else n
                        dve.wait_ge(x_done, x + 1)
                        if windowed and n % 2 == 0:
                            dve.tensor_tensor(rows[:, 1, :], psum[:, 7, :], rope[:, 0, :], ALU.mult
                                              ).then_inc(x_free, 1)
                            return
                        if windowed:
                            link_free = dve.tensor_tensor(rows[:, 2, :], psum[:, 7, :], rope[:, 1, :], ALU.mult)
                            link_free.then_inc(x_free, 1)
                            dve.wait_ge(x_free, x + 1)
                            link(dve.tensor_tensor(rows[:, 1, :], rows[:, 1, :], rows[:, 2, :], ALU.add))
                            whole, read = rows[:, 1, :], link
                        else:
                            def read(ins):
                                ins.then_inc(x_free, 1)
                                dve.wait_ge(x_free, x + 1)
                            whole = psum[:, 7, :]
                        if not first(it, c):
                            dve.wait_ge(parts_out[g], b * 16)
                        split(whole, g, b, read)
                    elif kind == "M":
                        i = n // UPT
                        k = n + max(i - 1, 0) + (1 if i and n % UPT > UPT // 2 else 0)
                        dve.wait_ge(scores_done, b * MU + k + 1)
                        if windowed:
                            h = 2 * (n % UPT)
                            lo = WINDOW if i == 0 else 0
                            scores = psum[:, k % 2, :].rearrange("p (h c) -> p h c", h=2)[:, :, lo:]
                            ins = dve.tensor_reduce(row_max[:, i, h:h + 2], scores, AX.X, ALU.max)
                        else:
                            h = n % UPT
                            ins = dve.tensor_reduce(row_max[:, i, h:h + 1], psum[:, k % 2, :], AX.X, ALU.max)
                        ins.then_inc(max_done, 1)
                        if n % UPT == UPT - 1:
                            dve.wait_ge(max_done, b * MU + k + 1)
                            link(dve.tensor_scalar(neg_max[:, 0, :], row_max[:, i, :], -1.0, None, ALU.mult))
                            link(dve.tensor_copy(neg_parts[:, i, 0, :], neg_max[:, 0, :]))
                            link(dve.tensor_tensor(neg_max[:, 1, :], neg_max[:, 0, :], neg_parts[:, i, 0, :],
                                                   ALU.subtract))
                            link(dve.tensor_copy(neg_parts[:, i, 1, :], neg_max[:, 1, :]))
                            dve.tensor_tensor(neg_parts[:, i, 2, :], neg_max[:, 1, :], neg_parts[:, i, 1, :],
                                              ALU.subtract).then_inc(neg_ready, 1)
                            dve.wait_ge(neg_ready, b * TPS + i + 1)
                    elif kind == "N":
                        k = (n + 1) * UPT + n + (UPT // 2 + 1 if n < TPS - 1 else 0)
                        dve.wait_ge(scores_done, b * MU + k + 1)
                        dve.tensor_copy(maxT[:, n * P:(n + 1) * P],
                                        psum[:, k % 2, :].bitcast(BF16)[0:3 * NH, 0:P]).then_inc(max_done, 1)
                    elif kind == "H":
                        dve.wait_ge(x_done, x + 1)
                        by_token = psum[:, 7, :].rearrange("p (i h d) -> p i h d", i=TPS, h=4)
                        link(dve.reciprocal(recip[:], by_token[:, :, :, HD]))
                        out = heads[:, :, n * 4 * HD:(n + 1) * 4 * HD].rearrange("p i (h d) -> p i h d", h=4)
                        dve.tensor_tensor(out, by_token[:, :, :, 0:HD],
                                          recip[:].rearrange("p i (h o) -> p i h o", o=1).broadcast_to((P, TPS, 4, HD)),
                                          ALU.mult).then_inc(x_free, 1)
                        dve.wait_ge(x_free, x + 1)
                    elif kind == "W":
                        dve.wait_ge(out_done, b * 2 + n + 1)
                        res = src[:, bass.ds(b * TPS + 2 * n, 2), :]
                        dve.tensor_tensor(res, psum[:, 4 + n, :].rearrange("p (i c) -> p i c", i=2), res,
                                          ALU.add).then_inc(out_added, 1)
                        dve.wait_ge(out_added, b * 2 + n + 3)
                        for i in range(2):
                            row_statistics(dve, next_stat, src, b * TPS + 2 * n + i)

                order(dve, unit, link)
                dve.tensor_copy(recip[:, 0, 0:1], row_max[:, 0, 0:1]).then_inc(out_added, 1)
                dve.wait_ge(out_added, 2 * NSEQ + 3)

            @block.tensor
            def _(pe):
                pe.wait_ge(weights_in, 16 * NW)
                if windowed:
                    pe.wait_ge(window_ready, 1)
                pe.sem_inc(scoresT_done, 1)
                pe.sem_inc(out_added, 2)
                bank7 = psum[:, 7, :]

                def bank7_free(x):
                    if not (type(x) is int and x == 0):
                        pe.wait_ge(x_free, x)

                def unit(kind, n, it, c, x):
                    b = it * 2 + c
                    s = c % 2
                    if kind == "T":
                        if n == 0:
                            pe.wait_ge(z_ready if windowed else z_normed, b + 1)
                        bank7_free(x)
                        for i in range(TPS):
                            ins = pe.transpose(bank7[:, i * P:(i + 1) * P], z[:, i, n * P:(n + 1) * P],
                                               cst["ident"][:])
                        ins.then_inc(x_done, 1)
                    elif kind in ("J1", "J"):
                        g, swapped = (n // 2, n % 2) if windowed else (n, 0)
                        col = (g // KD * (2 if windowed else 1) + swapped) * D + (g % KD) * P
                        k = KD - 1
                        if kind == "J1":
                            bank7_free(x)
                            k = 0
                        ins = pe.matmul(bank7, wqk[:, k, col:col + P], zT[:, k, :], start=(k == 0), stop=(k == KD - 1))
                        if kind == "J":
                            ins.then_inc(x_done, 1)
                    elif kind in ("V1", "V"):
                        i = 1
                        if kind == "V1":
                            bank7_free(x)
                            i = 0
                        for k in range(KD):
                            ins = pe.matmul(bank7[:, i * D:(i + 1) * D],
                                            zT[:, k, (2 * n + i) * P:(2 * n + i + 1) * P], wv[:, k, :],
                                            start=(k == 0), stop=(k == KD - 1))
                        if kind == "V":
                            ins.then_inc(x_done, 1)
                    elif kind == "M":
                        i = n // UPT
                        k = n + max(i - 1, 0) + (1 if i and n % UPT > UPT // 2 else 0)
                        if n == 0 and first(it, c):
                            pe.wait_ge(setup_done, 2)
                        if n in (0, UPT // 2):
                            pe.wait_ge(stack_in[s][2 * n // UPT], (it + c // 2) * LOADS + LOADS)
                        if k >= 2 or not first(it, c):
                            pe.wait_ge(max_done, b * MU + k - 1)
                        bank = psum[:, k % 2, :]
                        if windowed:
                            pe.matmul(bank, cst["ident_bf"][:], window_bf[:, 0, :], start=True, stop=False)
                            for m in range(2):
                                h = 2 * (n % UPT) + m
                                lo = 0 if i else WINDOW
                                ins = pe.matmul(bank[:, 2 * m * P + lo:2 * (m + 1) * P],
                                                q_stack[0:SROWS, s, h, i * P:(i + 1) * P],
                                                k_stack[0:SROWS, s, h, (i - 1) * P + lo:(i + 1) * P],
                                                start=False, stop=(m == 1))
                        else:
                            ins = pe.matmul(bank, q_stack[0:SROWS, s, n % UPT, i * P:(i + 1) * P],
                                            k_stack[0:SROWS, s, n % UPT, :], start=True, stop=True)
                        ins.then_inc(scores_done, 1)
                    elif kind == "N":
                        k = (n + 1) * UPT + n + (UPT // 2 + 1 if n < TPS - 1 else 0)
                        pe.wait_ge(max_done, b * MU + k - 1)
                        pe.wait_ge(neg_ready, b * TPS + n + 1)
                        pe.sem_inc(passed, 1)
                        pe.transpose(psum[:, k % 2, :].bitcast(BF16)[0:3 * NH, 0:P],
                                     neg_parts[:, n].rearrange("p c h -> p (c h)"),
                                     cst["ident_bf"][:]).then_inc(scores_done, 1)
                    elif kind == "S":
                        h = n // 4 // RPG * 4 + n % 4
                        if n == 0:
                            pe.wait_ge(max_in[s], (it + c // 2) * 48 + 48)
                        if n == 1 and not first(it, c):
                            pe.wait_ge(out_added, b * 2 + 2)
                        if n >= 2:
                            pe.wait_ge(probs_ready, b * SU + n - 1)
                        for a in range(2):
                            bank = psum[:, 2 + 2 * (n % 2) + a, :]
                            if windowed:
                                pe.matmul(bank, cst["ident_bf"][:], window_bf[:, 1, :], start=True, stop=False)
                                for m in range(2):
                                    j = 2 * a + m
                                    w_ = min(2 * P, SEQ - j * P)
                                    ins = pe.matmul(bank[:, 2 * m * P:2 * m * P + w_],
                                                    k_stack[0:SROWS + 3, s, h, j * P:(j + 1) * P],
                                                    q_stack[0:SROWS + 3, s, h, j * P:j * P + w_],
                                                    start=False, stop=(m == 1))
                            else:
                                j = 2 * (n // 4 % 2) + a
                                ins = pe.matmul(bank, k_stack[0:SROWS + 3, s, h, j * P:(j + 1) * P],
                                                q_stack[0:SROWS + 3, s, h, :], start=True, stop=True)
                        ins.then_inc(scoresT_done, 1)
                    elif kind in ("O1", "O"):
                        g, half = n // RPG, 0 if kind == "O1" else 1
                        if half == 0:
                            pe.wait_ge(probs_ready, b * SU + 4 * n + 4)
                            if g >= 1 and n % RPG == 0:
                                pe.wait_ge(headsT_ready, b * 4 + g)
                        if windowed:
                            for i in range(half * 2, half * 2 + 2):
                                for j in range(max(i - 1, 0), i + 1):
                                    for q in range(4):
                                        at = 2 * P * j + P * (i - j)
                                        ins = pe.matmul(psum[32 * q:32 * q + 32, 6, i * P:(i + 1) * P],
                                                        v_ones[:, s, j, 4 * g + q, :], probs[:, n % 2, q, at:at + P],
                                                        start=(j == max(i - 1, 0)), stop=(j == i))
                        else:
                            j = 2 * (n % 2) + half
                            for q in range(4):
                                ins = pe.matmul(psum[32 * q:32 * q + 32, 6, :], v_ones[:, s, j, 4 * g + q, :],
                                                probs[:, n % 2, q, half * SEQ:(half + 1) * SEQ],
                                                start=(j == 0), stop=(j == TPS - 1))
                        if half:
                            ins.then_inc(values_done, 1)
                    elif kind == "H":
                        pe.wait_ge(headsT_ready, b * 4 + n + 1)
                        bank7_free(x)
                        for i in range(TPS):
                            ins = pe.transpose(bank7[:, i * P:(i + 1) * P], headsT[:, n % 2, i * P:(i + 1) * P],
                                               cst["ident"][:])
                        ins.then_inc(x_done, 1)
                    elif kind == "G":
                        bank7_free(x)
                        for i in range(TPS):
                            ins = pe.transpose(psum[:, 2 + n, i * P:(i + 1) * P], heads[:, i, n * P:(n + 1) * P],
                                               cst["ident"][:])
                        ins.then_inc(cat_turned, 1)
                    elif kind == "W":
                        pe.wait_ge(catT_ready, b * KD + KD)
                        for i in range(2):
                            for k in range(KD):
                                ins = pe.matmul(psum[:, 4 + n, i * D:(i + 1) * D],
                                                catT[:, k, (2 * n + i) * P:(2 * n + i + 1) * P], wo[:, k, :],
                                                start=(k == 0), stop=(k == KD - 1))
                        ins.then_inc(out_done, 1)

                order(pe, unit)


def swiglu(pr, name, x_dram, h_res, stats, w, cst, psum):
    nc = pr.nc
    pr.prefix = name
    with ExitStack() as ctx:
        sb = lambda n, s, d=F32: pr.sb(n, s, d, ctx)
        w1, w3, w2 = sb("w1", [P, KD, HIDP]), sb("w3", [P, KD, HIDP]), sb("w2", [P, KH, D])
        gain = sb("gain", [P, 2, D])
        z = sb("z", [P, TPS, D])
        w1_parts, w3_parts = sb("w1_parts", [P, 2, KD, HIDP], F32R), sb("w3_parts", [P, 2, KD, HIDP], F32R)
        zT = sb("zT", [P, 2, KD, SEQ], F32R)
        th = sb("th", [P, 2, SEQ])
        act_gate = sb("act_gate", [P, 2, SEQ])
        hidT = sb("hidT", [P, KH, SEQ])
        x_rows = sb("x_rows", [P, 2, TPS, D])
        gain_in, up_in, down_in = pr.sem("gain_in"), pr.sem("up_weights_in"), pr.sem("down_weights_in")
        z_normed, z_scaled, z_ready = pr.sem("z_normed"), pr.sem("z_scaled"), pr.sem("z_ready")
        z_turned, zT_high, zT_ready = pr.sem("z_turned"), pr.sem("zT_high"), pr.sem("zT_ready")
        weights_high, weights_ready = pr.sem("weights_high"), pr.sem("weights_ready")
        up_done, tanh_ready, gate_ready, hid_ready = (pr.sem("up_done"), pr.sem("tanh_ready"), pr.sem("gate_ready"),
                                                      pr.sem("hid_ready"))
        down_done, down_read, added = pr.sem("down_done"), pr.sem("down_read"), pr.sem("added")
        counted = pr.sem("counted")
        x_in = [pr.sem("x_in0"), pr.sem("x_in1")]

        statistics(pr, name + "s_", h_res, stats,
                   loads=[(gain[:], w["gain"], gain_in), (w1[:], w["w1"], up_in), (w3[:], w["w3"], up_in),
                          (w2[:], w["w2"], down_in)])

        def all_sequences(eng, pair):
            with eng.Fori(0, NSEQ // 2 - 1) as it:
                pair(it, True)
            pair(NSEQ // 2 - 1, False)

        with nc.Block() as block:

            @block.sync
            def _(sp):
                def load_x(b, s):
                    sp.dma_start(x_rows[:, s], x_dram[bass.ds(b * SEQ, SEQ), :].rearrange("(i p) d -> p i d", p=P)
                                 ).then_inc(x_in[s], 16)

                for s in range(2):
                    load_x(s, s)
                with sp.Fori(0, NSEQ // 2 - 1) as it:
                    for c in range(2):
                        sp.wait_ge(added, (it * 2 + c) * 2 + 2)
                        load_x(it * 2 + c + 2, c)

            @block.gpsimd
            def _(pool):
                pool.wait_ge(gain_in, 16)
                with pool.Fori(0, NSEQ) as b:
                    pool.wait_ge(z_normed, b + 1)
                    for i in range(TPS):
                        ins = pool.tensor_tensor(z[:, i, :], z[:, i, :], gain[:, 0, :], ALU.mult)
                    ins.then_inc(z_scaled, 1)
                    pool.wait_ge(z_scaled, b + 1)
                    for i in range(TPS):
                        ins = pool.tensor_tensor(z[:, i, :], z[:, i, :], gain[:, 1, :], ALU.add)
                    ins.then_inc(z_ready, 1)

            @block.scalar
            def _(act):
                def turned(b):
                    for k in range(KD):
                        act.wait_ge(z_turned, b * KD + k + 1)
                        act.activation(zT[:, 0, k, :], psum[:, k, :], ACT.Copy).then_inc(zT_high, 1)

                def pair(it, more):
                    for c in range(2):
                        b = it * 2 + c
                        for m in range(KH):
                            act.wait_ge(up_done, b * KH + m + 1)
                            if m >= 2:
                                act.wait_ge(gate_ready, b * KH + m - 1)
                            act.activation(th[:, m % 2, :], psum[:, 2 + 2 * (m % 2), :], ACT.Tanh,
                                           scale=0.5).then_inc(tanh_ready, 1)
                        if more or c == 0:
                            turned(b + 1)

                act.wait_ge(up_in, 32)
                for n, (wt, parts) in enumerate(((w1, w1_parts), (w3, w3_parts))):
                    for k in range(KD):
                        ins = act.activation(parts[:, 0, k, :], wt[:, k, :], ACT.Copy)
                    ins.then_inc(weights_high, 1)
                turned(0)
                all_sequences(act, pair)

            @block.vector
            def _(dve):
                def normalise(b):
                    for i in range(TPS):
                        t = b * TPS + i
                        ins = dve.tensor_scalar(z[:, i:i + 1, :], h_res[:, bass.ds(t, 1), :],
                                                stats["mean"][:, bass.ds(t, 1)], stats["rstd"][:, bass.ds(t, 1)],
                                                ALU.subtract, ALU.mult)
                    ins.then_inc(z_normed, 1)

                def turned(b):
                    for k in range(KD):
                        dve.wait_ge(zT_high, b * KD + k + 1)
                        dve.tensor_tensor(zT[:, 1, k, :], psum[:, k, :], zT[:, 0, k, :].bitcast(F32),
                                          ALU.subtract).then_inc(zT_ready, 1)

                def pair(it, more):
                    for c in range(2):
                        b = it * 2 + c
                        if more or c == 0:
                            dve.wait_ge(z_turned, b * KD + KD)
                            normalise(b + 1)
                        for m in range(KH):
                            dve.wait_ge(tanh_ready, b * KH + m + 1)
                            if m >= 2:
                                dve.wait_ge(hid_ready, b * KH + m - 1)
                            dve.scalar_tensor_tensor(out=act_gate[:, m % 2, :], in0=th[:, m % 2, :], scalar=1.0,
                                                     in1=psum[:, 2 + 2 * (m % 2), :], op0=ALU.add,
                                                     op1=ALU.mult).then_inc(gate_ready, 1)
                            dve.wait_ge(gate_ready, b * KH + m + 1)
                            dve.scalar_tensor_tensor(out=hidT[:, m, :], in0=act_gate[:, m % 2, :], scalar=0.5,
                                                     in1=psum[:, 3 + 2 * (m % 2), :], op0=ALU.mult,
                                                     op1=ALU.mult).then_inc(hid_ready, 1)
                        if more or c == 0:
                            turned(b + 1)
                        dve.wait_ge(x_in[c], it * 16 + 16)
                        for o in range(2):
                            rows = h_res[:, bass.ds(b * TPS + 2 * o, 2), :]
                            dve.tensor_tensor(rows, rows, x_rows[:, c, 2 * o:2 * o + 2, :], ALU.add).then_inc(added, 1)
                        for o in range(2):
                            rows = h_res[:, bass.ds(b * TPS + 2 * o, 2), :]
                            dve.wait_ge(added, b * 2 + 2)
                            dve.wait_ge(down_done, b * 2 + o + 1)
                            dve.tensor_tensor(rows, psum[:, 6 + o, :].rearrange("p (i c) -> p i c", i=2), rows,
                                              ALU.add).then_inc(down_read, 1)
                            dve.wait_ge(down_read, b * 2 + o + 1)
                            for i in range(2):
                                ins = row_statistics(dve, stats["stat"], h_res, b * TPS + 2 * o + i)
                        ins.then_inc(counted, 1)

                normalise(0)
                for n, (wt, parts) in enumerate(((w1, w1_parts), (w3, w3_parts))):
                    dve.wait_ge(weights_high, n + 1)
                    for k in range(KD):
                        ins = dve.tensor_tensor(parts[:, 1, k, :], wt[:, k, :], parts[:, 0, k, :].bitcast(F32),
                                                ALU.subtract)
                    ins.then_inc(weights_ready, 1)
                turned(0)
                all_sequences(dve, pair)
                dve.wait_ge(counted, NSEQ)

            @block.tensor
            def _(pe):
                def turn(b):
                    pe.wait_ge(z_ready, b + 1)
                    for k in range(KD):
                        for i in range(TPS):
                            ins = pe.transpose(psum[:, k, i * P:(i + 1) * P], z[:, i, k * P:(k + 1) * P],
                                               cst["ident"][:])
                        ins.then_inc(z_turned, 1)

                def pair(it, more):
                    for c in range(2):
                        b = it * 2 + c
                        pe.wait_ge(zT_ready, b * KD + KD)
                        for m in range(KH):
                            if m >= 2:
                                pe.wait_ge(hid_ready, b * KH + m - 1)
                            for n, parts in enumerate((w1_parts, w3_parts)):
                                for k in range(KD):
                                    for w_part, z_part in SPLIT_PRODUCTS:
                                        ins = pe.matmul(psum[:, 2 + 2 * (m % 2) + n, :],
                                                        parts[:, w_part, k, m * P:(m + 1) * P], zT[:, z_part, k, :],
                                                        start=(k == 0 and w_part == z_part),
                                                        stop=(k == KD - 1 and w_part == 1))
                            ins.then_inc(up_done, 1)
                        if more or c == 0:
                            turn(b + 1)
                        pe.wait_ge(hid_ready, b * KH + KH)
                        for i in range(TPS):
                            for k in range(KH):
                                ins = pe.matmul(psum[:, 6 + i // 2, (i % 2) * D:(i % 2 + 1) * D],
                                                hidT[:, k, i * P:(i + 1) * P], w2[:, k, :],
                                                start=(k == 0), stop=(k == KH - 1))
                            if i % 2:
                                ins.then_inc(down_done, 1)

                turn(0)
                pe.wait_ge(weights_ready, 2)
                pe.wait_ge(down_in, 16)
                all_sequences(pe, pair)


def experts(pr, name, x_res, stats, w, cst, psum, slots_in, slots_out, out=None):
    nc = pr.nc
    pr.prefix = name
    SEG = 512
    NSTEP = NE * CAP // SEG
    BIG = float(4 * NE * CAP)
    with ExitStack() as ctx:
        sb = lambda n, s, d=F32: pr.sb(n, s, d, ctx)
        fc1 = sb("fc1", [P, 2, KD, EH])
        fc2 = sb("fc2", [P, 2, KE, D])
        bias1 = sb("bias1", [P, NE, KE])
        bias2 = sb("bias2", [P, NE, D])
        bias_in, fc_in = pr.sem("bias_in"), [pr.sem("fc_in0"), pr.sem("fc_in1")]
        scattered = pr.sem("scattered")
        gate = sb("gate", [P, KD, NE])
        count_in = sb("count_in", [P, 2 * P + NE])
        tables_in = pr.sem("tables_in")
        z_all = sb("z_all", [P, NT, D])
        scatter_at = sb("scatter_at", [P, TOPK, NT], U32)
        gather_at = sb("gather_at", [P, TOPK, NT], U32)
        weight = sb("weight", [P, TOPK, NT])
        statistics(pr, name + "s_", x_res, stats,
                   loads=[(gate[:], w["gate"], tables_in), (count_in[:], w["count"], tables_in),
                          (bias1[:], w["bias1"], bias_in), (bias2[:], w["bias2"], bias_in)]
                   + [(dst[:, e], w[n][e], fc_in[e]) for e in range(2) for dst, n in ((fc1, "fc1"), (fc2, "fc2"))])
        route(pr, name + "r_", x_res, z_all, stats, gate, count_in, tables_in, cst, psum, scatter_at, gather_at, weight,
              BIG, slots_in, scattered)
        pr.prefix = name
        rows_in = sb("rows_in", [P, 2, TPS, D])
        fc1_parts = sb("fc1_parts", [P, 2, 2, KD, EH], F32R)
        rowsT = sb("rowsT", [P, 2, KD, SEG], F32R)
        hidT = sb("hidT", [P, KE, SEG])
        rows_out = sb("rows_out", [P, 2, TPS, D])
        NG = 8
        picked = sb("picked", [P, NG, D])
        rows_loaded = [pr.sem("rows_loaded0"), pr.sem("rows_loaded1")]
        rows_turned, rowsT_high, rowsT_ready = pr.sem("rows_turned"), pr.sem("rowsT_high"), pr.sem("rowsT_ready")
        fc1_high, fc1_ready = pr.sem("fc1_high"), pr.sem("fc1_ready")
        up_done, hid_ready, down_done, out_ready = (pr.sem("up_done"), pr.sem("hid_ready"), pr.sem("down_done"),
                                                    pr.sem("out_ready"))
        out_stored = [pr.sem("out_stored0"), pr.sem("out_stored1")]
        gathered = [pr.sem(f"gathered{j}") for j in range(NG)]
        added, stored = pr.sem("added"), pr.sem("stored")
        passed = pr.sem("passed")
        with nc.Block() as block:

            @block.sync
            def _(sp):
                def load_expert(e, s):
                    sp.dma_start(fc1[:, s], w["fc1"][bass.ds(e, 1)].rearrange("o p k h -> p (o k) h")
                                 ).then_inc(fc_in[s], 16)
                    sp.dma_start(fc2[:, s], w["fc2"][bass.ds(e, 1)].rearrange("o p k h -> p (o k) h")
                                 ).then_inc(fc_in[s], 16)

                def load_rows(n, s):
                    sp.dma_start(rows_in[:, s], slots_in[bass.ds(n * SEG, SEG), :].rearrange("(i p) d -> p i d", p=P)
                                 ).then_inc(rows_loaded[s], 16)

                sp.wait_ge(scattered, 16 * TOPK * NT)
                for s in range(2):
                    load_rows(s, s)

                def step(it, c, more):
                    n = it * 4 + c
                    if more or c < 2:
                        sp.wait_ge(rows_turned, n * KD + KD)
                        load_rows(n + 2, c % 2)
                    sp.wait_ge(out_ready, n * 2 + 4)
                    sp.dma_start(slots_out[bass.ds(n * SEG, SEG), :].rearrange("(i p) d -> p i d", p=P),
                                 rows_out[:, c % 2]).then_inc(out_stored[c % 2], 16)
                    if c % 2 and more:
                        load_expert(it * 2 + c // 2 + 2, c // 2)

                with sp.Fori(0, NSTEP // 4 - 1) as it:
                    for c in range(4):
                        step(it, c, True)
                for c in range(4):
                    step(NSTEP // 4 - 1, c, False)
                if out is not None:
                    stores = 4
                    for g in range(stores):
                        tiles = slice(g * NT // stores, (g + 1) * NT // stores)
                        sp.wait_ge(added, TOPK * tiles.stop)
                        sp.dma_start(out.rearrange("(t p) d -> p t d", p=P)[:, tiles], x_res[:, tiles]
                                     ).then_inc(stored, 16)
                    sp.wait_ge(stored, 16 * stores)

            @block.gpsimd
            def _(pool):
                for s in range(2):
                    pool.wait_ge(out_stored[s], 16 * NSTEP // 2 + 16)
                for g in range(NT * TOPK):
                    t, k = g // TOPK, g % TOPK
                    if g >= NG:
                        pool.wait_ge(added, g - NG + 1)
                    pool.indirect_dma_start(
                        out=picked[:, g % NG, :], out_offset=None, in_=slots_out[:, :],
                        in_offset=bass.IndirectOffsetOnAxis(gather_at[:, k, t:t + 1], 0),
                        bounds_check=NE * CAP - 1, oob_is_err=False,
                    ).then_inc(gathered[g % NG], 16)

            @block.scalar
            def _(act):
                act.wait_ge(bias_in, 32)
                with act.Fori(0, NE // 2) as it:
                    for c in range(4):
                        n = it * 4 + c
                        for m in range(KE):
                            act.wait_ge(up_done, n * KE + m + 1)
                            act.sem_inc(passed, 1)
                            act.activation(hidT[:, m, :], psum[:, 2 + m % 4, :], ACT.Relu,
                                           bias=bias1[:, bass.ds(it * 2 + c // 2, 1), m:m + 1].rearrange("p a b -> p (a b)"),
                                           ).then_inc(hid_ready, 1)

            @block.vector
            def _(dve):
                def turned(n):
                    for k in range(KD):
                        dve.wait_ge(rows_turned, n * KD + k + 1)
                        dve.tensor_copy(rowsT[:, 0, k, :], psum[:, k, :]).then_inc(rowsT_high, 1)
                        dve.wait_ge(rowsT_high, n * KD + k + 1)
                        dve.tensor_tensor(rowsT[:, 1, k, :], psum[:, k, :], rowsT[:, 0, k, :].bitcast(F32),
                                          ALU.subtract).then_inc(rowsT_ready, 1)

                def split_fc1(e, s, loads):
                    dve.wait_ge(fc_in[s], loads * 32)
                    for k in range(KD):
                        ins = dve.tensor_copy(fc1_parts[:, s, 0, k, :], fc1[:, s, k, :])
                    ins.then_inc(fc1_high, 1)
                    dve.wait_ge(fc1_high, e + 1)
                    for k in range(KD):
                        ins = dve.tensor_tensor(fc1_parts[:, s, 1, k, :], fc1[:, s, k, :],
                                                fc1_parts[:, s, 0, k, :].bitcast(F32), ALU.subtract)
                    ins.then_inc(fc1_ready, 1)

                def group(it, more):
                    for c in range(4):
                        n = it * 4 + c
                        if c == 0:
                            split_fc1(it * 2 + 1, 1, it + 1)
                        elif c == 2 and more:
                            split_fc1(it * 2 + 2, 0, it + 2)
                        if more or c < 3:
                            turned(n + 1)
                        dve.wait_ge(out_stored[c % 2], (it * 2 + c // 2) * 16 + 16)
                        for o in range(2):
                            dve.wait_ge(down_done, n * 2 + o + 1)
                            for i in range(2):
                                ins = dve.tensor_tensor(rows_out[:, c % 2, 2 * o + i:2 * o + i + 1, :],
                                                        psum[:, 6 + o, i * D:(i + 1) * D].rearrange("p (o d) -> p o d", o=1),
                                                        bias2[:, bass.ds(it * 2 + c // 2, 1), :], ALU.add)
                            ins.then_inc(out_ready, 1)

                for s in range(2):
                    dve.sem_inc(out_stored[s], 16)
                dve.wait_ge(bias_in, 32)
                split_fc1(0, 0, 1)
                turned(0)
                with dve.Fori(0, NE // 2 - 1) as it:
                    group(it, True)
                group(NE // 2 - 1, False)
                for g in range(NT * TOPK):
                    t, k = g // TOPK, g % TOPK
                    dve.wait_ge(gathered[g % NG], 16 * (g // NG + 1))
                    if k:
                        dve.wait_ge(added, g)
                    dve.scalar_tensor_tensor(out=x_res[:, t, :], in0=picked[:, g % NG, :],
                                             scalar=weight[:, k, t:t + 1], in1=x_res[:, t, :],
                                             op0=ALU.mult, op1=ALU.add).then_inc(added, 1)
                    if k and t and out is None:
                        row_statistics(dve, stats["stat"], x_res, t - 1)
                dve.wait_ge(added, NT * TOPK)
                if out is None:
                    row_statistics(dve, stats["stat"], x_res, NT - 1).then_inc(added, 1)
                    dve.wait_ge(added, NT * TOPK + 1)

            @block.tensor
            def _(pe):
                def turn(n, s, loads):
                    pe.wait_ge(rows_loaded[s], loads * 16)
                    for k in range(KD):
                        for i in range(TPS):
                            ins = pe.transpose(psum[:, k, i * P:(i + 1) * P],
                                               rows_in[:, s, i, k * P:(k + 1) * P], cst["ident"][:])
                        ins.then_inc(rows_turned, 1)

                def group(it, more):
                    for c in range(4):
                        n = it * 4 + c
                        e, s = c // 2, c % 2
                        if s == 0:
                            pe.wait_ge(fc_in[e], it * 32 + 32)
                            pe.wait_ge(fc1_ready, it * 2 + e + 1)
                        pe.wait_ge(rowsT_ready, n * KD + KD)
                        for m in range(KE):
                            if m >= 4:
                                pe.wait_ge(hid_ready, n * KE + m - 3)
                            for k in range(KD):
                                for w_part, row_part in SPLIT_PRODUCTS:
                                    ins = pe.matmul(psum[:, 2 + m % 4, :],
                                                    fc1_parts[:, e, w_part, k, m * P:(m + 1) * P],
                                                    rowsT[:, row_part, k, :], start=(k == 0 and w_part == row_part),
                                                    stop=(k == KD - 1 and w_part == 1))
                            ins.then_inc(up_done, 1)
                        if more or c < 3:
                            turn(n + 1, 1 - s, it * 2 + (c + 1) // 2 + 1)
                        pe.wait_ge(hid_ready, n * KE + KE)
                        pe.wait_ge(out_ready, n * 2 + 2)
                        for i in range(TPS):
                            for k in range(KE):
                                ins = pe.matmul(psum[:, 6 + i // 2, (i % 2) * D:(i % 2 + 1) * D],
                                                hidT[:, k, i * P:(i + 1) * P], fc2[:, e, k, :],
                                                start=(k == 0), stop=(k == KE - 1))
                            if i % 2:
                                ins.then_inc(down_done, 1)

                pe.sem_inc(out_ready, 2)
                turn(0, 0, 1)
                with pe.Fori(0, NE // 2 - 1) as it:
                    group(it, True)
                group(NE // 2 - 1, False)


def route(pr, name, x_res, z_all, stats, gate, count_in, tables_in, cst, psum, scatter_at, gather_at, weight, big,
          slots_in, scattered):
    nc = pr.nc
    pr.prefix = name
    with ExitStack() as ctx:
        sb = lambda n, s, d=F32: pr.sb(n, s, d, ctx)
        z = sb("z", [P, 2, TPS, D])
        zT = sb("zT", [P, 2, KD, SEQ])
        logits = sb("logits", [P, TPS, NE])
        top8 = sb("top8", [P, TPS, 8])
        at8 = sb("at8", [P, TPS, 8], U32)
        top = sb("top", [P, NT, TOPK])
        choice = sb("choice", [P, NT, TOPK])
        onehot = sb("onehot", [P, TOPK, NT, NE])
        run = sb("run", [P, 2, NT, NE])
        before = sb("before", [P, TOPK, NT, NE])
        small = sb("small", [P, 4, NT])
        loc = sb("loc", [P, TOPK, NT])
        slot = sb("slot", [P, 2, NT])
        valid = sb("valid", [P, TOPK, NT])
        z_normed, z_kept, z_turned, zT_ready = (pr.sem("z_normed"), pr.sem("z_kept"), pr.sem("z_turned"),
                                                pr.sem("zT_ready"))
        passed = pr.sem("passed")
        slots_ready = pr.sem("slots_ready")
        logits_done, chain, bulk = pr.sem("logits_done"), pr.sem("chain"), pr.sem("bulk")
        gap_ready, exp_ready, before_ready, places_done = (pr.sem("gap_ready"), pr.sem("exp_ready"),
                                                           pr.sem("before_ready"), pr.sem("places_done"))
        with nc.Block() as block:

            @block.gpsimd
            def _(pool):
                with pool.Fori(0, NSEQ // 2) as it:
                    for c in range(2):
                        b = it * 2 + c
                        pool.wait_ge(z_normed, b + 1)
                        pool.tensor_copy(z_all[:, bass.ds(b * TPS, TPS), :], z[:, c]).then_inc(z_kept, 1)
                pool.wait_ge(z_kept, NSEQ + 1)
                for k in range(TOPK):
                    pool.wait_ge(slots_ready, k + 1)
                    for t in range(NT):
                        pool.indirect_dma_start(
                            out=slots_in[:, :], out_offset=bass.IndirectOffsetOnAxis(scatter_at[:, k, t:t + 1], 0),
                            in_=z_all[:, t, :], in_offset=None, bounds_check=NE * CAP - 1, oob_is_err=False,
                        ).then_inc(scattered, 16)

            @block.scalar
            def _(act):
                with act.Fori(0, NSEQ // 2) as it:
                    for c in range(2):
                        b = it * 2 + c
                        for k in range(KD):
                            act.wait_ge(z_turned, b * KD + k + 1)
                            act.activation(zT[:, c, k, :], psum[:, 2 * c + k, :], ACT.Copy).then_inc(zT_ready, 1)
                act.wait_ge(gap_ready, 1)
                act.activation(small[:, 1, :], small[:, 0, :], ACT.Exp).then_inc(exp_ready, 1)

            @block.vector
            def _(dve):
                def normalise(b, c):
                    for i in range(TPS):
                        t = b * TPS + i
                        ins = dve.tensor_scalar(z[:, c, i:i + 1, :], x_res[:, bass.ds(t, 1), :],
                                                stats["mean"][:, bass.ds(t, 1)], stats["rstd"][:, bass.ds(t, 1)],
                                                ALU.subtract, ALU.mult)
                    ins.then_inc(z_normed, 1)

                def pair(it, more):
                    for c in range(2):
                        b = it * 2 + c
                        link = Chain(dve, chain, 5, b)
                        if more or c == 0:
                            dve.wait_ge(z_kept, b + 1)
                            normalise(b + 1, 1 - c)
                        dve.wait_ge(logits_done, b + 1)
                        link(dve.tensor_copy(logits[:], psum[:, 4, 0:TPS * NE].rearrange("p (i e) -> p i e", e=NE)))
                        dve.sem_inc(passed, 1)
                        for i in range(TPS):
                            ins = dve.max(top8[:, i, :], logits[:, i, :])
                        link(ins)
                        dve.sem_inc(passed, 1)
                        for i in range(TPS):
                            ins = dve.max_index(at8[:, i, :], top8[:, i, :], logits[:, i, :])
                        link(ins)
                        link(dve.tensor_copy(top[:, bass.ds(b * TPS, TPS), :], top8[:, :, 0:TOPK]))
                        link(dve.tensor_copy(choice[:, bass.ds(b * TPS, TPS), :], at8[:, :, 0:TOPK]))

                dve.sem_inc(z_kept, 1)
                normalise(0, 0)
                with dve.Fori(0, NSEQ // 2 - 1) as it:
                    pair(it, True)
                pair(NSEQ // 2 - 1, False)
                link = Chain(dve, bulk)
                dve.tensor_tensor(small[:, 0, :], top[:, :, 1], top[:, :, 0], ALU.subtract).then_inc(gap_ready, 1)
                dve.wait_ge(tables_in, 32)
                iota = count_in[:, 2 * P:2 * P + NE].rearrange("p (o e) -> p o e", o=1).broadcast_to((P, NT, NE))
                for k in range(TOPK):
                    link(dve.tensor_tensor(onehot[:, k], iota, choice[:, :, k:k + 1].broadcast_to((P, NT, NE)),
                                           ALU.is_equal))
                total = sb("total", [P, 1, NE])

                def count_before(k):
                    held, other = onehot[:, k], 0
                    step = 1
                    while step < NT:
                        dst = run[:, other]
                        dve.tensor_copy(dst[:, 0:step], held[:, 0:step])
                        link(dve.tensor_tensor(dst[:, step:], held[:, step:], held[:, 0:NT - step], ALU.add))
                        held, other, step = dst, 1 - other, step * 2
                    if k == 0:
                        link(dve.tensor_copy(total[:], held[:, NT - 1:NT]))
                        dve.tensor_tensor(before[:, k], held, onehot[:, k], ALU.subtract).then_inc(before_ready, 1)
                    else:
                        link(dve.tensor_tensor(before[:, k], held, onehot[:, k], ALU.subtract))
                        dve.tensor_tensor(before[:, k], before[:, k], total[:].broadcast_to((P, NT, NE)),
                                          ALU.add).then_inc(before_ready, 1)
                    dve.wait_ge(before_ready, k + 1)

                def find_slots(k):
                    dve.wait_ge(places_done, k + 1)
                    link(dve.tensor_tensor(run[:, 0], psum[:, 5 + k, 0:NT * NE].rearrange("p (t e) -> p t e", e=NE),
                                           onehot[:, k], ALU.mult))
                    link(dve.tensor_reduce(loc[:, k, :], run[:, 0], AX.X, ALU.add))
                    link(dve.scalar_tensor_tensor(out=slot[:, 0, :], in0=choice[:, :, k], scalar=float(CAP),
                                                  in1=loc[:, k, :], op0=ALU.mult, op1=ALU.add))
                    link(dve.tensor_scalar(valid[:, k, :], loc[:, k, :], float(CAP), None, ALU.is_lt))
                    link(dve.tensor_tensor(slot[:, 0, :], slot[:, 0, :], valid[:, k, :], ALU.mult))
                    link(dve.tensor_scalar(slot[:, 1, :], valid[:, k, :], -big, big, ALU.mult, ALU.add))
                    link(dve.tensor_tensor(slot[:, 1, :], slot[:, 1, :], slot[:, 0, :], ALU.add))
                    dve.tensor_copy(scatter_at[:, k, :], slot[:, 1, :]).then_inc(slots_ready, 1)
                    link(dve.tensor_copy(gather_at[:, k, :], slot[:, 0, :]))

                count_before(0)
                find_slots(0)
                dve.wait_ge(slots_ready, 1)
                count_before(1)
                find_slots(1)
                dve.wait_ge(exp_ready, 1)
                link(dve.tensor_scalar(small[:, 2, :], small[:, 1, :], 1.0, None, ALU.add))
                link(dve.reciprocal(small[:, 3, :], small[:, 2, :]))
                for k in range(TOPK):
                    link(dve.tensor_tensor(weight[:, k, :], small[:, 3, :], valid[:, k, :], ALU.mult))
                link(dve.tensor_tensor(weight[:, 1, :], weight[:, 1, :], small[:, 1, :], ALU.mult))

            @block.tensor
            def _(pe):
                pe.wait_ge(tables_in, 32)
                def turn(b, c):
                    pe.wait_ge(z_normed, b + 1)
                    for k in range(KD):
                        for i in range(TPS):
                            ins = pe.transpose(psum[:, 2 * c + k, i * P:(i + 1) * P],
                                               z[:, c, i, k * P:(k + 1) * P], cst["ident"][:])
                        ins.then_inc(z_turned, 1)

                def pair(it, more):
                    for c in range(2):
                        b = it * 2 + c
                        if more or c == 0:
                            turn(b + 1, 1 - c)
                        else:
                            pe.wait_ge(chain, (b - 1) * 5 + 1)
                        pe.wait_ge(zT_ready, b * KD + KD)
                        for i in range(TPS):
                            for k in range(KD):
                                ins = pe.matmul(psum[:, 4, i * NE:(i + 1) * NE], zT[:, c, k, i * P:(i + 1) * P],
                                                gate[:, k, :], start=(k == 0), stop=(k == KD - 1))
                        ins.then_inc(logits_done, 1)

                turn(0, 0)
                with pe.Fori(0, NSEQ // 2 - 1) as it:
                    pair(it, True)
                pair(NSEQ // 2 - 1, False)
                for k in range(TOPK):
                    pe.wait_ge(before_ready, k + 1)
                    out = psum[:, 5 + k, 0:NT * NE]
                    pe.matmul(out, count_in[:, 0:P], onehot[:, k].rearrange("p t e -> p (t e)"), start=True, stop=False)
                    pe.matmul(out, count_in[:, P:2 * P], before[:, k].rearrange("p t e -> p (t e)"),
                              start=False, stop=True).then_inc(places_done, 1)


def build(nc, a):
    with ExitStack() as ctx:
        pr = Program(nc, ctx)
        psum = ctx.enter_context(nc.psum_tensor("banks", [P, 8, SEQ], F32))
        y_res = pr.sb("y_res", [P, NT, D])
        zero = pr.sb("zero", [P, D // 2])
        consts = pr.sb("consts", [P, P])
        ident_bf = pr.sb("ident_bf", [P, P], BF16)
        cst = {"ident": consts, "ident_bf": ident_bf}
        stats = {"stat": pr.sb("stat", [P, NT, 6]), "mean": pr.sb("mean", [P, NT]), "rstd": pr.sb("rstd", [P, NT]),
                 "tmp": pr.sb("tmp", [P, 3, NT])}
        stats2 = {"stat": pr.sb("stat2", [P, NT, 6]), "mean": pr.sb("mean2", [P, NT]),
                  "rstd": pr.sb("rstd2", [P, NT]), "tmp": pr.sb("tmp2", [P, 3, NT])}
        qk_parts = nc.dram_tensor("qk_parts", (2, 2, 3, D, SEQ), BF16, kind="Internal").ap()
        slots_in = nc.dram_tensor("slots_in", (NE * CAP, D), F32, kind="Internal").ap()
        slots_out = nc.dram_tensor("slots_out", (NE * CAP, D), F32, kind="Internal").ap()

        def input_statistics(loads):
            shares = 4
            x_in = [pr.sem(f"x_in{h}") for h in range(shares)]
            ident_in, zero_ready, zeroed, ident_ready = (pr.sem("ident_in"), pr.sem("zero_ready"), pr.sem("zeroed"),
                                                         pr.sem("ident_ready"))
            with ExitStack() as first:
                x_res = pr.sb("x_res", [P, NT, D], F32, first)
                x_rows = a["x"].rearrange("(t p) d -> p t d", p=P)
                with nc.Block() as block:

                    @block.sync
                    def _(sp):
                        sp.dma_start(consts[:], a["ident"]).then_inc(ident_in, 16)
                        for h in range(shares):
                            tiles = slice(h * NT // shares, (h + 1) * NT // shares)
                            sp.dma_start(x_res[:, tiles], x_rows[:, tiles]).then_inc(x_in[h], 16)

                    @block.gpsimd
                    def _(pool):
                        pool.memset(zero[:], 0.0).then_inc(zero_ready, 1)
                        pool.wait_ge(zero_ready, 1)

                    @block.vector
                    def _(dve):
                        dve.wait_ge(ident_in, 16)
                        dve.tensor_copy(ident_bf[:], consts[:]).then_inc(ident_ready, 1)
                        dve.wait_ge(ident_ready, 1)

                fill = [(slots_in.rearrange("(r p j) (c d) -> r p (j c) d", p=P, r=8, c=2)[r],
                         zero[:].rearrange("p (o d) -> p o d", o=1).broadcast_to((P, 2 * NE * CAP // (8 * P), D // 2)), zeroed)
                        for r in range(8)]
                statistics(pr, "sa_", x_res, stats, y_res, stats2, loads=loads + fill, arrivals=x_in)
            return zeroed, 128

        attention(pr, "a_", True, y_res, stats2, stats["stat"],
                  {"qk": a["a_qk"], "v": a["a_v"], "o": a["a_o"], "rope": a["rope"], "gain": a["ln1"],
                   "window": a["window"]}, cst, psum, qk_parts, input_statistics)
        pr.end_layer()
        swiglu(pr, "f_", a["x"], y_res, stats, {"w1": a["w1"], "w3": a["w3"], "w2": a["w2"], "gain": a["ln2"]},
               cst, psum)
        pr.end_layer()
        moe = {k: a[k] for k in ("gate", "count", "fc1", "fc2", "bias1", "bias2")}
        experts(pr, "m_", y_res, stats, moe, cst, psum, slots_in, slots_out)
        pr.end_layer()
        attention(pr, "b_", False, y_res, stats, stats["stat"], {"qk": a["b_qk"], "v": a["b_v"], "o": a["b_o"]},
                  cst, psum, qk_parts, lambda loads: statistics(pr, "sb_", y_res, stats, loads=loads))
        pr.end_layer()
        experts(pr, "n_", y_res, stats, moe, cst, psum, slots_in, slots_out, out=a["out"])


def by_rows(m, k):
    return np.ascontiguousarray(m.reshape(k, P, -1).transpose(1, 0, 2))


def padded(m, shape):
    out = np.zeros(shape, m.dtype)
    out[:m.shape[0], :m.shape[1]] = m
    return out


def shape_constants():
    f = 1.0 / np.float32(10000.0) ** (np.arange(0, HD, 2, dtype=np.float32) / np.float32(HD))
    angle = np.outer(np.arange(SEQ, dtype=np.float32), f.astype(np.float32)).astype(np.float32)
    cos, sin = np.cos(angle).astype(np.float32), np.sin(angle).astype(np.float32)
    d = np.arange(P) % HD
    rope = np.stack([cos[:, d // 2].T, np.where(d % 2 == 0, -1, 1)[:, None] * sin[:, d // 2].T], 1)
    p, c = np.arange(P)[:, None], np.arange(2 * P)[None, :]
    by_query = (c <= p + P) & (c >= p)
    by_key = (c >= p) & (c - p <= WINDOW)
    window = np.stack([np.tile(np.where(m, 0.0, MASKED), 2) for m in (by_query, by_key)], 1)
    before = (np.arange(P)[:, None] < np.arange(P)[None, :]).astype(np.float32)
    count = np.concatenate([before, np.ones((P, P)), np.tile(np.arange(NE), (P, 1))], 1)
    return {"rope": rope.astype(np.float32), "window": window.astype(np.float32), "count": count.astype(np.float32),
            "ident": np.eye(P, dtype=np.float32)}


def layouts(i):
    i = {k.replace("L0_", ""): np.asarray(v) for k, v in i.items()}
    swap = np.arange(D) ^ 1
    both = lambda g, b: np.ascontiguousarray(np.broadcast_to(np.stack([g, b])[None], (P, 2, D)))
    fc1 = i["ffn_fc1_w"].transpose(0, 2, 1).reshape(NE, KD, P, EH).transpose(0, 2, 1, 3)
    fc2 = i["ffn_fc2_w"].reshape(NE, KE, P, D).transpose(0, 2, 1, 3)
    wq, wk = i["attn_a_wq"], i["attn_a_wk"]
    return {
        "x": i["attn_a_x"].reshape(NTOK, D),
        "a_qk": by_rows(np.concatenate([wq, wq[:, swap], wk, wk[:, swap]], 1), KD),
        "a_v": by_rows(i["attn_a_wv"], KD), "a_o": by_rows(i["attn_a_wo"], KD),
        "ln1": both(i["attn_a_ln1_g"], i["attn_a_ln1_b"]), "ln2": both(i["attn_a_ln2_g"], i["attn_a_ln2_b"]),
        "w1": by_rows(padded(i["attn_a_w1"], (D, HIDP)), KD), "w3": by_rows(padded(i["attn_a_w3"], (D, HIDP)), KD),
        "w2": by_rows(padded(i["attn_a_w2"], (HIDP, D)), KH),
        "b_qk": by_rows(np.concatenate([i["attn_b_w_q"].T, i["attn_b_w_k"].T], 1), KD),
        "b_v": by_rows(i["attn_b_w_v"].T, KD), "b_o": by_rows(i["attn_b_w_o"].T, KD),
        "gate": by_rows(i["ffn_gate_w"].T, KD),
        "fc1": np.ascontiguousarray(fc1), "fc2": np.ascontiguousarray(fc2),
        "bias1": np.ascontiguousarray(i["ffn_fc1_b"].reshape(NE, KE, P).transpose(2, 0, 1)),
        "bias2": np.ascontiguousarray(np.broadcast_to(i["ffn_fc2_b"].reshape(1, NE, D), (P, NE, D))),
        **shape_constants(),
    }


def kernel(**inputs):
    import concourse.bacc as bacc
    from concourse.bass_utils import run_bass_kernel_spmd

    nc = bacc.Bacc("TRN2", target_bir_lowering=False, num_devices=1)
    arrays = {f"in_{k}": v for k, v in layouts(inputs).items()}
    aps = {k[3:]: nc.dram_tensor(k, v.shape, F32, kind="ExternalInput").ap() for k, v in arrays.items()}
    aps["out"] = nc.dram_tensor("out", (NTOK, D), F32, kind="ExternalOutput").ap()
    build(nc, aps)
    r = run_bass_kernel_spmd(nc, [arrays], core_ids=[0])
    return r.results[0]["out"].reshape(NSEQ, SEQ, D)
```
